# Optimizing a Trainium2 kernel written in Bass

```python
import numpy as np
import jax
import jax.numpy as jnp

def _softmax(x, axis=-1):
    return jax.nn.softmax(x, axis=axis)

def _gelu(x):
    return jax.nn.gelu(x, approximate=True)

def _silu(x):
    return jax.nn.silu(x)

def _sigmoid(x):
    return jax.nn.sigmoid(x)

def _layernorm(x, axis=-1, eps=1e-05):
    m = jnp.mean(x, axis=axis, keepdims=True)
    v = jnp.var(x, axis=axis, keepdims=True)
    return (x - m) / jnp.sqrt(v + eps)

def _scatter_add(tgt, idx, src, axis=0):
    return tgt.at[idx].add(src)

def _segment_sum(src, seg, n):
    return jax.ops.segment_sum(src, seg, n)
kernel_name = 'mk_xattn_ffn_d1_seqx_r4_10a197'

def setup_inputs(seed: int=0):
    np.random.seed(seed)
    _w = jnp.asarray

    def _rec_inputs():
        import jax
        import jax.numpy as jnp
        _rk = jax.random.key(seed)
        x = 7.22e-05 + 1 * jax.random.normal(jax.random.fold_in(_rk, 1), (16, 112, 256), jnp.float32)
        _lenS = 112 - jax.random.randint(jax.random.fold_in(_rk, 7), (16,), 0, max(1, 112 // 4) + 1, jnp.int32)
        _lenS2 = 375 - jax.random.randint(jax.random.fold_in(_rk, 8), (16,), 0, max(1, 375 // 4) + 1, jnp.int32)
        _ctx_1024P = jax.random.normal(jax.random.fold_in(_rk, 11), (16, 16, 256), jnp.float32)
        _ctx_1024c = jax.random.dirichlet(jax.random.fold_in(_rk, 511), 0.3 * jnp.ones((16,), jnp.float32), (16, 375))
        _ctx_1024t = jnp.einsum('bsk,bkd->bsd', _ctx_1024c, _ctx_1024P)
        _ctx_1024t = _ctx_1024t * jax.lax.rsqrt(jnp.mean(jnp.square(_ctx_1024t)) + 1e-12) * 0.953939
        ctx_1024 = -0.000514642 + 1.00011 * (_ctx_1024t + 0.3 * jax.random.normal(jax.random.fold_in(_rk, 611), (16, 375, 256), jnp.float32))
        return (x, ctx_1024)
    x, ctx_1024 = _rec_inputs()

    def _L0_xattn_setup():
        import jax, jax.numpy as jnp
        import numpy as np
        B, L_ENC, L_DEC, D = (16, 128, 128, 256)
        key = jax.random.key(seed)
        k1, k2, k3, k4, k5, k6 = jax.random.split(key, 6)
        encoder_hc = jax.random.normal(k1, (B, L_ENC, D), dtype=jnp.float32)
        decoder_hq = jax.random.normal(k2, (B, L_DEC, D), dtype=jnp.float32)
        w_sim = jax.random.normal(k3, (3 * D,), dtype=jnp.float32) * 0.02
        b_sim = jax.random.normal(k4, (1,), dtype=jnp.float32) * 0.02
        W_qv = jax.random.normal(k5, (4 * D, D), dtype=jnp.float32) * 0.02
        b_qv = jax.random.normal(k6, (D,), dtype=jnp.float32) * 0.02
        return {'encoder_hc': encoder_hc, 'decoder_hq': decoder_hq, 'w_sim': w_sim, 'b_sim': b_sim, 'W_qv': W_qv, 'b_qv': b_qv}
    _L0_xattn_all = _L0_xattn_setup()
    _L0_xattn_in = {k: v for k, v in _L0_xattn_all.items() if k in ('w_sim', 'b_sim', 'W_qv', 'b_qv')}
    del _L0_xattn_all

    def _L0_ffn_setup():
        import jax, jax.numpy as jnp
        import numpy as np
        L, H, NH, NKV, HD, FF, E, K = (4, 256, 16, 4, 64, 512, 8, 2)
        B, S = (2, 512)
        THETA, EPS = (10000.0, 1e-05)

        def _rms(x, w):
            return x * jax.lax.rsqrt(jnp.mean(x * x, axis=-1, keepdims=True) + EPS) * w

        def _rope_cos_sin(seq_len, head_dim, theta):
            inv = 1.0 / theta ** (jnp.arange(0, head_dim, 2, dtype=jnp.float32) / head_dim)
            f = jnp.arange(seq_len, dtype=jnp.float32)[:, None] * inv
            emb = jnp.concatenate([f, f], axis=-1)
            return (jnp.cos(emb), jnp.sin(emb))

        def _rot_half(x):
            h = x.shape[-1] // 2
            return jnp.concatenate([-x[..., h:], x[..., :h]], axis=-1)

        def _attention(x, wq, wk, wv, wo, cos, sin, causal_bias):
            b, s, _ = x.shape
            q = (x @ wq).reshape(b, s, NH, HD).transpose(0, 2, 1, 3)
            k = (x @ wk).reshape(b, s, NKV, HD).transpose(0, 2, 1, 3)
            v = (x @ wv).reshape(b, s, NKV, HD).transpose(0, 2, 1, 3)
            c = cos[None, None]
            sn = sin[None, None]
            q = q * c + _rot_half(q) * sn
            k = k * c + _rot_half(k) * sn
            rep = NH // NKV
            k = jnp.repeat(k, rep, axis=1)
            v = jnp.repeat(v, rep, axis=1)
            scores = jnp.einsum('bhqd,bhkd->bhqk', q, k) / jnp.sqrt(jnp.asarray(HD, x.dtype))
            scores = scores + causal_bias
            attn = jax.nn.softmax(scores, axis=-1)
            out = jnp.einsum('bhqk,bhkd->bhqd', attn, v)
            out = out.transpose(0, 2, 1, 3).reshape(b, s, NH * HD)
            return out @ wo

        def _moe(x, wr, wg, wu, wd):
            logits = x @ wr
            probs = jax.nn.softmax(logits, axis=-1)
            topv, topi = jax.lax.top_k(probs, K)
            topv = topv / jnp.sum(topv, axis=-1, keepdims=True)
            comb = jnp.sum(jax.nn.one_hot(topi, E, dtype=x.dtype) * topv[..., None], axis=-2)
            out = jnp.zeros_like(x)
            for e in range(E):
                h = jax.nn.silu(x @ wg[e]) * (x @ wu[e])
                out = out + comb[..., e:e + 1] * (h @ wd[e])
            return out
        key = jax.random.key(seed)
        ks = jax.random.split(key, 12)
        sc = 0.02
        inp = {'hidden_states': jax.random.normal(ks[0], (B, S, H), jnp.float32), 'ln1_w': jnp.ones((L, H), jnp.float32), 'ln2_w': jnp.ones((L, H), jnp.float32), 'wq': jax.random.normal(ks[1], (L, H, NH * HD), jnp.float32) * sc, 'wk': jax.random.normal(ks[2], (L, H, NKV * HD), jnp.float32) * sc, 'wv': jax.random.normal(ks[3], (L, H, NKV * HD), jnp.float32) * sc, 'wo': jax.random.normal(ks[4], (L, NH * HD, H), jnp.float32) * sc, 'wr': jax.random.normal(ks[5], (L, H, E), jnp.float32) * sc, 'wg': jax.random.normal(ks[6], (L, E, H, FF), jnp.float32) * sc, 'wu': jax.random.normal(ks[7], (L, E, H, FF), jnp.float32) * sc, 'wd': jax.random.normal(ks[8], (L, E, FF, H), jnp.float32) * sc}
        return inp
    _L0_ffn_all = _L0_ffn_setup()
    _L0_ffn_in = {k: v for k, v in _L0_ffn_all.items() if k in ('ln1_w', 'ln2_w', 'wq', 'wk', 'wv', 'wo', 'wr', 'wg', 'wu', 'wd')}
    del _L0_ffn_all
    return {'x': x, 'ctx_1024': ctx_1024, 'L0_xattn_w_sim': _L0_xattn_in['w_sim'], 'L0_xattn_b_sim': _L0_xattn_in['b_sim'], 'L0_xattn_W_qv': _L0_xattn_in['W_qv'], 'L0_xattn_b_qv': _L0_xattn_in['b_qv'], 'L0_ffn_ln1_w': _L0_ffn_in['ln1_w'], 'L0_ffn_ln2_w': _L0_ffn_in['ln2_w'], 'L0_ffn_wq': _L0_ffn_in['wq'], 'L0_ffn_wk': _L0_ffn_in['wk'], 'L0_ffn_wv': _L0_ffn_in['wv'], 'L0_ffn_wo': _L0_ffn_in['wo'], 'L0_ffn_wr': _L0_ffn_in['wr'], 'L0_ffn_wg': _L0_ffn_in['wg'], 'L0_ffn_wu': _L0_ffn_in['wu'], 'L0_ffn_wd': _L0_ffn_in['wd']}

def reference(x, ctx_1024, L0_xattn_w_sim, L0_xattn_b_sim, L0_xattn_W_qv, L0_xattn_b_qv, L0_ffn_ln1_w, L0_ffn_ln2_w, L0_ffn_wq, L0_ffn_wk, L0_ffn_wv, L0_ffn_wo, L0_ffn_wr, L0_ffn_wg, L0_ffn_wu, L0_ffn_wd):
    import jax
    import jax.numpy as jnp

    def _L0_xattn_ref(encoder_hc, decoder_hq, w_sim, b_sim, W_qv, b_qv):
        import jax, jax.numpy as jnp
        import numpy as np
        B, L_ENC, L_DEC, D = (16, 128, 128, 256)
        d = encoder_hc.shape[-1]
        w1, w2, w3 = (w_sim[:d], w_sim[d:2 * d], w_sim[2 * d:])
        Sim = (encoder_hc @ w1)[:, :, None] + (decoder_hq @ w2)[:, None, :] + jnp.einsum('bid,bjd->bij', encoder_hc * w3, decoder_hq) + b_sim[0]
        A = jax.nn.softmax(Sim, axis=2)
        hq_hat = jnp.einsum('bij,bjd->bid', A, decoder_hq)
        Batt = jax.nn.softmax(jnp.max(Sim, axis=2), axis=1)
        hc_bar = jnp.einsum('bi,bid->bd', Batt, encoder_hc)[:, None, :]
        hc_hat = jnp.broadcast_to(hc_bar, encoder_hc.shape)
        feats = jnp.concatenate([encoder_hc, hq_hat, encoder_hc * hq_hat, encoder_hc * hc_hat], axis=-1)
        hcq = feats @ W_qv + b_qv
        return hcq

    def _L0_ffn_ref(hidden_states, ln1_w, ln2_w, wq, wk, wv, wo, wr, wg, wu, wd):
        import jax, jax.numpy as jnp
        import numpy as np
        L, H, NH, NKV, HD, FF, E, K = (4, 256, 16, 4, 64, 512, 8, 2)
        B, S = (2, 512)
        THETA, EPS = (10000.0, 1e-05)

        def _rms(x, w):
            return x * jax.lax.rsqrt(jnp.mean(x * x, axis=-1, keepdims=True) + EPS) * w

        def _rope_cos_sin(seq_len, head_dim, theta):
            inv = 1.0 / theta ** (jnp.arange(0, head_dim, 2, dtype=jnp.float32) / head_dim)
            f = jnp.arange(seq_len, dtype=jnp.float32)[:, None] * inv
            emb = jnp.concatenate([f, f], axis=-1)
            return (jnp.cos(emb), jnp.sin(emb))

        def _rot_half(x):
            h = x.shape[-1] // 2
            return jnp.concatenate([-x[..., h:], x[..., :h]], axis=-1)

        def _attention(x, wq, wk, wv, wo, cos, sin, causal_bias):
            b, s, _ = x.shape
            q = (x @ wq).reshape(b, s, NH, HD).transpose(0, 2, 1, 3)
            k = (x @ wk).reshape(b, s, NKV, HD).transpose(0, 2, 1, 3)
            v = (x @ wv).reshape(b, s, NKV, HD).transpose(0, 2, 1, 3)
            c = cos[None, None]
            sn = sin[None, None]
            q = q * c + _rot_half(q) * sn
            k = k * c + _rot_half(k) * sn
            rep = NH // NKV
            k = jnp.repeat(k, rep, axis=1)
            v = jnp.repeat(v, rep, axis=1)
            scores = jnp.einsum('bhqd,bhkd->bhqk', q, k) / jnp.sqrt(jnp.asarray(HD, x.dtype))
            scores = scores + causal_bias
            attn = jax.nn.softmax(scores, axis=-1)
            out = jnp.einsum('bhqk,bhkd->bhqd', attn, v)
            out = out.transpose(0, 2, 1, 3).reshape(b, s, NH * HD)
            return out @ wo

        def _moe(x, wr, wg, wu, wd):
            logits = x @ wr
            probs = jax.nn.softmax(logits, axis=-1)
            topv, topi = jax.lax.top_k(probs, K)
            topv = topv / jnp.sum(topv, axis=-1, keepdims=True)
            comb = jnp.sum(jax.nn.one_hot(topi, E, dtype=x.dtype) * topv[..., None], axis=-2)
            out = jnp.zeros_like(x)
            for e in range(E):
                h = jax.nn.silu(x @ wg[e]) * (x @ wu[e])
                out = out + comb[..., e:e + 1] * (h @ wd[e])
            return out
        s = hidden_states.shape[1]
        cos, sin = _rope_cos_sin(s, HD, THETA)
        causal_bias = jnp.where(jnp.tril(jnp.ones((s, s), bool))[None, None], 0.0, -1000000000.0).astype(hidden_states.dtype)
        x = hidden_states
        for l in range(L):
            res = x
            h = _rms(x, ln1_w[l])
            h = _attention(h, wq[l], wk[l], wv[l], wo[l], cos, sin, causal_bias)
            x = jnp.clip(res + h, -100.0, 100.0)
            res = x
            h = _rms(x, ln2_w[l])
            h = _moe(h, wr[l], wg[l], wu[l], wd[l])
            x = jnp.clip(res + h, -100.0, 100.0)
        return x
    x = x + _L0_xattn_ref(_layernorm(x, axis=-1), ctx_1024, L0_xattn_w_sim, L0_xattn_b_sim, L0_xattn_W_qv, L0_xattn_b_qv)
    x = x + _L0_ffn_ref(_layernorm(x, axis=-1), L0_ffn_ln1_w, L0_ffn_ln2_w, L0_ffn_wq, L0_ffn_wk, L0_ffn_wv, L0_ffn_wo, L0_ffn_wr, L0_ffn_wg, L0_ffn_wu, L0_ffn_wd)
    return x

_drawn_inputs = setup_inputs


def setup_inputs(seed=0):
    import zlib

    import numpy as np

    out = dict(_drawn_inputs(seed))
    spreads = {'L0_ffn_ln1_w': (1.0, 0.6), 'L0_ffn_ln2_w': (1.0, 0.6)}
    factors = {'L0_xattn_b_qv': 2.796,
     'L0_ffn_wq': 8.0,
     'L0_ffn_wk': 8.0,
     'L0_ffn_wr': 3.662,
     'L0_ffn_wg': 3.222,
     'L0_ffn_wu': 3.182,
     'L0_ffn_wd': 3.189}
    for name, (base, spread) in spreads.items():
        noise = np.random.default_rng([zlib.crc32(name.encode()), seed]).standard_normal(out[name].shape)
        drawn = base * np.exp(spread * noise) if base else spread * noise
        out[name] = jnp.asarray(drawn.astype(out[name].dtype))
    for name, factor in factors.items():
        out[name] = (out[name] * factor).astype(out[name].dtype)
    return out
```

```python
from contextlib import ExitStack

import concourse.bass as bass
from concourse import mybir

ALU = mybir.AluOpType
ACT = mybir.ActivationFunctionType
AX_X = mybir.AxisListType.X
F32 = mybir.dt.float32
BF16 = mybir.dt.bfloat16
U32 = mybir.dt.uint32
I32 = mybir.dt.int32

B, S, D = 16, 112, 256
CTX = 375
CR = 125
CB = CTX // CR
L, NH, NKV, HD = 4, 16, 4, 64
FF, E, TOPK = 512, 8, 2
KD = D // 128
QKV = (NH + 2 * NKV) * HD
GB = 4
NG = B // GB
GN = GB * S
HALF = B // 2
SLOT = 128
HT = HALF * S * TOPK // SLOT + E - 1
NT = 2 * HT
HROWS = HT * SLOT
EPT = HALF * S // SLOT
DX = D + 4
EPS = 1e-05
CLIP = 100.0
NEG = -8.0e9
SCALE = float(HD) ** -0.5

C_ID, C_COS, C_SIN, C_LOW, C_ONE = 0, 128, 240, 352, 464
C_E, C_M, C_T, C_J, C_CAUSAL, C_H, C_END = 592, 600, 607, 628, 630, 742, 750

DVE_LAYER = 188



def constants():
    import numpy as np

    c = np.zeros((128, C_END), np.float32)
    c[:, C_ID:C_ID + 128] = np.eye(128, dtype=np.float32)
    inv = (1.0 / np.float32(10000.0) ** (np.arange(0, HD, 2, dtype=np.float32) / np.float32(HD))).astype(np.float32)
    angle = (np.arange(S, dtype=np.float32)[:, None] * inv).T
    cos, sin = np.cos(angle).astype(np.float32), np.sin(angle).astype(np.float32)
    for q in range(4):
        c[32 * q:32 * q + 32, C_COS:C_COS + S] = cos
        c[32 * q:32 * q + 32, C_SIN:C_SIN + S] = -sin if q < 2 else sin
        c[32 * q:32 * q + 32, C_J + q % 2] = 1.0
    t = np.arange(S)
    c[0:S, C_LOW:C_LOW + S] = t[:, None] < t[None, :]
    c[:, C_ONE:C_ONE + 128] = 1.0
    c[:, C_E:C_E + E] = np.arange(E)
    c[:, C_M:C_M + EPT] = SLOT * np.arange(EPT)
    c[:, C_T:C_T + HT] = np.arange(HT)
    c[0:S, C_CAUSAL:C_CAUSAL + S] = np.where(t[None, :] > t[:, None], np.float32(NEG), np.float32(0))
    c[:, C_H:C_END] = -0.5
    return c


class Steps:

    def __init__(self, engine, sem, base):
        self.engine, self.sem, self.base, self.n = engine, sem, base, 0

    def __call__(self, instruction):
        self.n += 1
        instruction.then_inc(self.sem, 1)
        self.engine.wait_ge(self.sem, self.base + self.n)


def xattn_ffn(nc, x, ctx_1024, w_sim, b_sim, W_qv, b_qv, ln1_w, ln2_w, wq, wk, wv, wo, wr, wg, wu, wd, const, out):
    with ExitStack() as stack:
        def sb(name, shape, dt=F32):
            return stack.enter_context(nc.sbuf_tensor(name, shape, dt))

        def sem(name):
            return stack.enter_context(nc.semaphore(name))

        sorted_x = [nc.dram_tensor(f"sorted_x{h}", [HROWS, DX], F32, kind="Internal").ap() for h in range(2)]
        sorted_y = [nc.dram_tensor(f"sorted_y{h}", [HROWS, D], F32, kind="Internal").ap() for h in range(2)]
        res_d = nc.dram_tensor("res_d", [S, B, D], F32, kind="Internal").ap()

        arena = sb("arena", [128, 3 * E * KD * FF])
        wg_s = arena[:, 0:8192]
        wu_s = arena[:, 8192:16384]
        wd_s = arena[:, 16384:24576]
        at = [0]

        def part(width, p=128):
            at[0] += width
            assert at[0] <= 24576
            return arena[0:p, at[0] - width:at[0]]

        dec = [part(CB * D, CR).rearrange("p (c d) -> p c d", c=CB) for _ in range(2)]
        decT = part(KD * CTX).rearrange("p (k j) -> p k j", k=KD)
        encT = part(KD * B * S).rearrange("p (k n) -> p k n", k=KD)
        hqT = part(KD * B * S).rearrange("p (k n) -> p k n", k=KD)
        e3T = part(KD * S).rearrange("p (k i) -> p k i", k=KD)
        attn = part(CTX + 1, S)
        attnT = part(CB * S, CR).rearrange("p (c i) -> p c i", c=CB)
        wqv = part(8 * D).rearrange("p (c n) -> p c n", c=8)
        feat = [part(8 * S).rearrange("p (c i) -> p c i", c=8) for _ in range(2)]
        res = part(B * D, S).rearrange("p (b d) -> p b d", b=B)
        bqv = part(D, S)
        w1row = part(D, S)
        enc = [part(D, S) for _ in range(2)]
        scratch = part(D, S)
        battD = part(B * S, B).rearrange("p (b i) -> p b i", b=B)
        simrow = part(B, S)
        batt = part(S, B)
        hcT = part(KD * B).rearrange("p (k b) -> p k b", k=KD)
        prodT = part(B * S).rearrange("p (b i) -> p b i", b=B)

        wqk_s = sb("wqk_s", [128, KD, 10, 128])
        wv_s = sb("wv_s", [128, KD, NKV * HD])
        wo_s = sb("wo_s", [128, 8, D])
        x_sb = sb("x_sb", [S, B, DX])
        y_in = sb("y_in", [S, 2, TOPK, D])
        xnT = sb("xnT", [128, KD, GN])
        qarena = sb("qarena", [128, 8 * GN])
        qT = qarena[:, :].rearrange("p (n t) -> p n t", n=8)
        kz = sb("kz", [128, 2, 2, GN])
        xe = [kz[:, 0, u, 0:DX] for u in range(2)]
        xeT = [qarena[:, 512 + 256 * u:768 + 256 * u].rearrange("p (k t) -> p k t", k=KD) for u in range(2)]
        th = qarena[:, 1024:1536]
        hid = [qarena[:, 1536 + 512 * u:2048 + 512 * u] for u in range(2)]
        hidT = qarena[:, 2560:3072].rearrange("p (c t) -> p c t", c=4)
        ye = [qarena[:, 3072 + 256 * u:3328 + 256 * u] for u in range(2)]
        v_s = sb("v_s", [S, GB + 1, NKV * HD])
        parena = sb("parena", [128, 2 * NH * S])
        prob = parena[0:S, :].rearrange("q (u n k) -> q u n k", u=2, n=NH)
        raw = parena[:, 0:KD * (NH + NKV) * HD].rearrange("p (k n) -> p k n", k=KD)
        probT = sb("probT", [S, NKV, GN])
        oT = sb("oT", [128, 2, GN])
        rope_c = sb("rope_c", [128, GN])
        rope_s = sb("rope_s", [128, GN])
        xn1 = sb("xn1", [S, D])
        x2T = sb("x2T", [128, KD, S])

        cst = sb("cst", [128, C_END])
        ident = cst[:, C_ID:C_ID + 128]
        ident_b = sb("ident_b", [S, S], BF16)
        causal_b = sb("causal_b", [S, 2, S], BF16)
        low_b = sb("low_b", [S, S], BF16)
        ones_b = sb("ones_b", [S, S], BF16)
        ln1T = sb("ln1T", [128, L, KD])
        ln2T = sb("ln2T", [128, L, KD])
        wr_s = sb("wr_s", [128, L, KD, E])
        wsT = sb("wsT", [128, 3, KD])
        bsim = sb("bsim", [S, 1])
        small = sb("small", [128, 64])
        lg = sb("lg", [S, B, E])
        top = sb("top", [S, HALF, 8])
        idx = sb("idx", [S, HALF, 8], U32)
        idxf = sb("idxf", [S, HALF, TOPK])
        oh = sb("oh", [S, HALF * TOPK, E])
        oh_b = sb("oh_b", [S, HALF * TOPK, E], BF16)
        pre = [sb(f"pre{i}", [S, HALF * TOPK, E]) for i in range(2)]
        cnt = sb("cnt", [S, E, EPT])
        tiles = sb("tiles", [S, E])
        cum = [sb(f"cum{i}", [S, E]) for i in range(2)]
        posf = sb("posf", [S, HALF * TOPK])
        pos = sb("pos", [S, B, TOPK], U32)
        wts = sb("wts", [S, B, TOPK])
        tef = sb("tef", [1, HT, E])
        tes = sb("tes", [1, HT])
        tile_e = sb("tile_e", [1, 2 * HT], I32)

        rmax = sb("rmax", [S, NH])
        nmax = sb("nmax", [S, 2, NH])
        rsum = sb("rsum", [S, 2, NH])
        rrec = sb("rrec", [S, NH])
        gate = sb("gate", [S, 2, HALF])
        er = sb("er", [128, 2, 2])
        g_tmp = sb("g_tmp", [S, HALF])
        ms1, r1 = sb("ms1", [S, GB]), sb("r1", [S, GB])
        ms2, r2 = sb("ms2", [S, B]), sb("r2", [S, HALF])
        xsq = sb("xsq", [S, 2, D])
        mix_b = rope_c[0:S, 0:D]

        ps = stack.enter_context(nc.psum_tensor("ps", [128, 8, 512], F32))

        ld_const, ld_x, ld_xw, ld_ln = sem("ld_const"), sem("ld_x"), sem("ld_xw"), sem("ld_ln")
        ld_dec = [sem(f"ld_dec{i}") for i in range(2)]
        ld_aw, ld_mw, ld_raw, aw_ready = sem("ld_aw"), sem("ld_mw"), sem("ld_raw"), sem("aw_ready")
        ld_xe = [sem(f"ld_xe{i}") for i in range(2)]
        st_ye = [sem(f"st_ye{i}") for i in range(2)]
        st_res, st_zero, st_out, ld_res = sem("st_res"), sem("st_zero"), sem("st_out"), sem("ld_res")
        gathered = [sem(f"gathered{i}") for i in range(2)]
        scattered = [sem(f"scattered{i}") for i in range(2)]
        c_bf, z_ready = sem("c_bf"), sem("z_ready")
        enc_ready, xT_done, decT_a, decT_v, encT_ready, e3_ready = (sem(n) for n in ("enc_ready", "xT_done", "decT_a", "decT_v", "encT_ready", "e3_ready"))
        sim_done, max_ready, exp_done, attn_ready, aT_done, aT_ready, hq_done, hq_ready = (sem(n) for n in (
            "sim_done", "max_ready", "exp_done", "attn_ready", "aT_done", "aT_ready", "hq_done", "hq_ready"))
        batt_v, batt_a, batt_p = sem("batt_v"), sem("batt_a"), sem("batt_p")
        feat_a, feat_v, feat_done, x_ready = sem("feat_a"), sem("feat_v"), sem("feat_done"), sem("x_ready")
        p_v, p_qk, p_sc, p_pt, p_ot0, p_ot1, p_wo, p_t2, p_lg, p_t1, p_rt = (sem(n) for n in (
            "p_v", "p_qk", "p_sc", "p_pt", "p_ot0", "p_ot1", "p_wo", "p_t2", "p_lg", "p_t1", "p_rt"))
        a_v, a_exp, a_pt, a_ot, a_sq1, a_xn1, a_t1, a_sq2, a_t2, a_rt = (sem(n) for n in (
            "a_v", "a_exp", "a_pt", "a_ot", "a_sq1", "a_xn1", "a_t1", "a_sq2", "a_t2", "a_rt"))
        d_rope, d_max, d_norm, d_ot, d_wo, d_lg, d_x, d_yr, d_oh, d_rt, d_pos = (sem(n) for n in (
            "d_rope", "d_max", "d_norm", "d_ot", "d_wo", "d_lg", "d_x", "d_yr", "d_oh", "d_rt", "d_pos"))
        m_tx, m_g, m_u, m_th, m_dn, moe_done = (sem(n) for n in ("m_tx", "m_g", "m_u", "m_th", "m_dn", "moe_done"))
        m_xT, m_tanh, m_hT = (sem(n) for n in ("m_xT", "m_tanh", "m_hT"))
        m_r, m_h, m_y = (sem(n) for n in ("m_r", "m_h", "m_y"))
        dv, dm, dx, passed = sem("dv"), sem("dm"), sem("dx"), sem("passed")
        g_eps, var_ready, rstd_ready, g_r1, g_r2 = (sem(n) for n in ("g_eps", "var_ready", "rstd_ready", "g_r1", "g_r2"))

        zero = probT[:, :, :].rearrange("p a b -> p (a b)")[:, 0:6 * DX].rearrange("p (r d) -> p r d", r=6)
        rows = S * 6
        ZERO_STORES = 4 * (HROWS // rows)
        assert HROWS % rows == 0

        block = stack.enter_context(nc.Block())

        def bc(ap, axis, shape):
            return ap.unsqueeze(axis).to_broadcast(shape)

        def alone(engine):
            engine.sem_inc(passed, 1)

        def heads(b):
            return ps[0:S, 0:4, 0:GN].rearrange("q n (h k) -> q n h k", k=S)

        @block.sync
        def _(sp):
            sp.dma_start(cst[:, :], const).then_inc(ld_const, 16)
            sp.dma_start(x_sb[:, :, 0:D], x.rearrange("b s d -> s b d")).then_inc(ld_x, 16)
            sp.dma_start(w1row, w_sim[0:D].rearrange("(a d) -> a d", a=1).to_broadcast([S, D])).then_inc(ld_xw, 16)
            sp.dma_start(wsT[:, :, :], w_sim.rearrange("(g p k) -> p g k", g=3, k=KD)).then_inc(ld_xw, 16)
            sp.dma_start(bsim[:, :], b_sim.rearrange("(a d) -> a d", a=1).to_broadcast([S, 1])).then_inc(ld_xw, 16)

            def load_dec(b, u):
                sp.dma_start(dec[u], ctx_1024[b].rearrange("(c p) d -> p c d", p=CR) if isinstance(b, int) else
                             ctx_1024[bass.ds(b, 1)].rearrange("a (c p) d -> p (a c) d", p=CR)).then_inc(ld_dec[u], 16)

            load_dec(0, 0)
            load_dec(1, 1)
            sp.dma_start(wqv, W_qv.rearrange("(f p k) n -> p f k n", f=4, k=KD)).then_inc(ld_xw, 16)
            sp.dma_start(bqv, b_qv.rearrange("(a d) -> a d", a=1).to_broadcast([S, D])).then_inc(ld_xw, 16)
            sp.dma_start(ln1T[:, :, :], ln1_w.rearrange("l (p k) -> p l k", k=KD)).then_inc(ld_ln, 16)
            sp.dma_start(ln2T[:, :, :], ln2_w.rearrange("l (p k) -> p l k", k=KD)).then_inc(ld_ln, 16)
            sp.dma_start(wr_s[:, :, :, :], wr.rearrange("l (p k) e -> p l k e", k=KD)).then_inc(ld_ln, 16)
            with sp.Fori(0, B // 2 - 1) as i:
                for u in range(2):
                    sp.wait_ge(hq_done, i * 2 + u + 1)
                    load_dec(i * 2 + u + 2, u)

            def attention_weights(l):
                one = (lambda a: a[l]) if isinstance(l, int) else (lambda a: a[bass.ds(l, 1)].rearrange("a r c -> (a r) c"))
                for w, c0, c1 in ((wq, 0, NH * HD), (wk, NH * HD, (NH + NKV) * HD)):
                    sp.dma_start(raw[:, :, c0:c1], one(w).rearrange("(p k) n -> p k n", k=KD)).then_inc(ld_raw, 16)
                sp.dma_start(wv_s[:, :, :], one(wv).rearrange("(p k) n -> p k n", k=KD)).then_inc(ld_aw, 16)
                for j in range(2):
                    src = one(wo).rearrange("(p j i d) n -> j d p i n", p=2, j=2, i=4)[j]
                    for p in range(2):
                        sp.dma_start(wo_s[64 * j:64 * j + 64, 4 * p:4 * p + 4, :], src[:, p]).then_inc(ld_aw, 16)

            def expert_weights(l):
                for w, s, k in ((wg, wg_s, KD), (wu, wu_s, KD), (wd, wd_s, 4)):
                    src = w[l] if isinstance(l, int) else w[bass.ds(l, 1)].rearrange("a e r c -> (a e) r c")
                    src = src.rearrange("e (p k) n -> p e k n", k=k)
                    for e in range(E):
                        sp.dma_start(s[:, 1024 * e:1024 * e + 1024].rearrange("p (k n) -> p k n", k=k),
                                     src[:, e]).then_inc(ld_mw, 16)

            attention_weights(0)
            sp.wait_ge(st_zero, ZERO_STORES * 16)
            for u in range(2):
                sp.dma_start(sorted_y[u][0:1, :], zero[u:u + 1, 0, 0:D]).then_inc(st_ye[u], 16)
            sp.wait_ge(x_ready, B)
            sp.dma_start(res_d, res).then_inc(st_res, 16)

            def layer_io(l, last):
                sp.wait_ge(st_res, 16)
                sp.wait_ge(moe_done, l + 1)
                expert_weights(l)
                if not last:
                    sp.wait_ge(p_lg, (l + 1) * B)
                    attention_weights(l + 1)

                def load_tile(T, u, h, peeled=False):
                    if not peeled:
                        sp.wait_ge(m_tx, l * NT + T - 1)
                        sp.wait_ge(m_r, l * NT + T - 1)
                    sp.dma_start(xe[u], sorted_x[h][bass.ds((T - h * HT) * SLOT, SLOT), :]).then_inc(ld_xe[u], 16)

                def store_tile(T, u, h):
                    sp.wait_ge(m_y, l * NT + T + 1)
                    sp.dma_start(sorted_y[h][bass.ds((T - h * HT) * SLOT, SLOT), :], ye[u]).then_inc(st_ye[u], 16)

                sp.wait_ge(p_lg, (l + 1) * B)
                sp.wait_ge(scattered[0], (l + 1) * 16 * HALF * TOPK)
                load_tile(0, 0, 0, True)
                load_tile(1, 1, 0, True)

                def pair(i, load, store, first=False, end=False):
                    for u in range(2):
                        if not end:
                            if load[u] == 1 and load[0] == 0:
                                sp.wait_ge(scattered[1], (l + 1) * 16 * HALF * TOPK)
                                alone(sp)
                            load_tile(i * 2 + u + 2, u, load[u])
                        if not (first and u == 0):
                            store_tile(i * 2 + u - 1, 1 - u, store[u])

                mid = (HT - 3) // 2
                assert 2 * mid + 3 == HT
                pair(0, (0, 0), (0, 0), first=True)
                with sp.Fori(1, mid) as i:
                    pair(i, (0, 0), (0, 0))
                pair(mid, (0, 1), (0, 0))
                pair(mid + 1, (1, 1), (0, 0))
                with sp.Fori(mid + 2, NT // 2 - 1) as i:
                    pair(i, (1, 1), (1, 1))
                pair(NT // 2 - 1, (1, 1), (1, 1), end=True)
                store_tile(NT - 1, 1, 1)

            with sp.Fori(0, L - 1) as l:
                layer_io(l, False)
            layer_io(L - 1, True)
            sp.wait_ge(moe_done, L + 1)
            sp.dma_start(res, res_d).then_inc(ld_res, 16)
            sp.wait_ge(d_x, L * B + B)
            sp.dma_start(out.rearrange("b s d -> s b d"), x_sb[:, :, 0:D]).then_inc(st_out, 16)
            sp.wait_ge(st_out, 16)

        @block.gpsimd
        def _(pool):
            pool.memset(probT[:, :, :], 0.0).then_inc(z_ready, 1)
            pool.memset(pos[:, :, :], 0).then_inc(z_ready, 1)
            pool.memset(wts[:, :, :], 0.0).then_inc(z_ready, 1)
            pool.memset(x_sb[:, :, D:DX], 0.0).then_inc(z_ready, 1)
            pool.wait_ge(z_ready, 4)
            for n in range(HROWS // rows):
                for h in range(2):
                    for rows_of, width in ((sorted_x[h], DX), (sorted_y[h], D)):
                        pool.dma_start(rows_of[rows * n:rows * n + rows, :].rearrange("(r p) d -> p r d", p=S),
                                       zero[:, :, 0:width]).then_inc(st_zero, 16)
            pool.wait_ge(st_zero, ZERO_STORES * 16)

            def norm_factors(out, var, n):
                width = var.shape[-1]
                alone(pool)
                pool.tensor_scalar(g_tmp[:, 0:width], var, EPS, None, ALU.add).then_inc(g_eps, 1)
                pool.wait_ge(g_eps, n)
                return pool.tensor_tensor(out, g_tmp[:, 0:width], cst[0:S, C_H:C_H + width], ALU.pow)

            pool.wait_ge(ld_const, 16)
            with pool.Fori(0, 2 * B) as i:
                pool.wait_ge(var_ready, i + 1)
                norm_factors(small[0:S, 28:29], small[0:S, 27:28], i + 1).then_inc(rstd_ready, 1)

            def arrange_weights(n):
                pool.wait_ge(ld_raw, n * 16 * 2)
                alone(pool)
                for k in range(KD):
                    for h in range(2):
                        for p in range(2):
                            src = raw[:, k, 0:NH * HD].rearrange("x (p j i h d) -> x p h i j d", p=2, j=2, i=4, h=2)[:, p, h]
                            dst = wqk_s[:, k, 2 + 4 * p:6 + 4 * p, :].rearrange("x i (h j d) -> x h i j d", h=2, j=2)[:, h]
                            pool.tensor_copy(dst, src)
                        src = raw[:, k, NH * HD:(NH + NKV) * HD].rearrange("x (p j h d) -> x h p j d", p=2, j=2, h=2)[:, h]
                        dst = wqk_s[:, k, 0:2, :].rearrange("x p (h j d) -> x h p j d", h=2, j=2)[:, h]
                        last = pool.tensor_copy(dst, src)
                last.then_inc(aw_ready, 1)

            def gather(l, b):
                if b >= 2:
                    pool.wait_ge(d_yr, l * B + b - 1)
                alone(pool)
                for k in range(TOPK):
                    pool.indirect_dma_start(
                        out=y_in[:, b % 2, k, :], out_offset=None, in_=sorted_y[b // HALF],
                        in_offset=bass.IndirectOffsetOnAxis(ap=pos[:, b, k:k + 1], axis=0)).then_inc(gathered[b % 2], 16)

            def out_factors(l, h):
                pool.wait_ge(a_sq2, l * B + h * HALF + HALF)
                norm_factors(r2[:, :], ms2[:, h * HALF:h * HALF + HALF], 2 * B + l * 6 + (4, 6)[h]).then_inc(g_r2, 1)

            def gathers(l, last=False):
                for u in range(2):
                    pool.wait_ge(st_ye[u], l * (8 * NT) + 16)
                for b in range(B):
                    gather(l, b)
                    if last:
                        continue
                    if b % GB == GB - 1:
                        pool.wait_ge(a_sq1, l * B + b + 1)
                        norm_factors(r1[:, :], ms1[:, :], 2 * B + l * 6 + (1, 2, 3, 5)[b // GB]).then_inc(g_r1, 1)
                    if b == B - 2:
                        out_factors(l, 0)

            arrange_weights(1)

            def move_rows(l):
                for h in range(2):
                    if h == 1:
                        out_factors(l, 1)
                    pool.wait_ge(d_pos, l * 2 + h + 1)
                    alone(pool)
                    for b in range(h * HALF, h * HALF + HALF):
                        for k in range(TOPK):
                            pool.indirect_dma_start(
                                out=sorted_x[h], out_offset=bass.IndirectOffsetOnAxis(ap=pos[:, b, k:k + 1], axis=0),
                                in_=x_sb[:, b, :], in_offset=None).then_inc(scattered[h], 16)

            with pool.Fori(0, L - 1) as l:
                gathers(l)
                move_rows(l)
                arrange_weights(l + 2)
            gathers(L - 1)
            move_rows(L - 1)
            gathers(L, last=True)

        @block.tensor
        def _(pe):
            pe.wait_ge(ld_const, 16)
            pe.wait_ge(c_bf, 4)

            def turn(b, u, n):
                pe.wait_ge(ld_dec[u], n * 16)
                if not (isinstance(b, int) and b == 0):
                    pe.wait_ge(decT_a, b)
                    pe.wait_ge(decT_v, b)
                    pe.wait_ge(encT_ready, b)
                for k in range(KD):
                    for c in range(CB):
                        pe.transpose(ps[:, k, c * CR:c * CR + CR],
                                     dec[u][:, c, :].rearrange("p (m k) -> p k m", k=KD)[:, k], ident[0:CR, 0:CR])
                pe.wait_ge(enc_ready, b + 1)
                for k in range(KD):
                    last = pe.transpose(ps[:, 2, k * S:k * S + S],
                                        enc[u].rearrange("p (m k) -> p k m", k=KD)[:, k], ident[0:S, 0:S])
                last.then_inc(xT_done, 1)

            def similar(b):
                pe.wait_ge(decT_a, b + 1)
                pe.wait_ge(decT_v, b + 1)
                pe.wait_ge(e3_ready, b + 1)
                for k in range(KD):
                    last = pe.matmul(ps[0:S, 3, 0:CTX], e3T[:, k, :], decT[:, k, :], start=(k == 0), stop=(k == KD - 1))
                last.then_inc(sim_done, 1)

            def turn_attn(b):
                pe.wait_ge(attn_ready, b + 1)
                for c in range(CB):
                    last = pe.transpose(ps[0:CR, 4, c * S:c * S + S], attn[:, c * CR:c * CR + CR], ident[0:S, 0:S])
                last.then_inc(aT_done, 1)

            def attend(b, u):
                pe.wait_ge(aT_ready, b + 1)
                for k in range(KD):
                    for c in range(CB):
                        last = pe.matmul(ps[:, 5, k * S:k * S + S],
                                         dec[u][:, c, :].rearrange("p (m k) -> p k m", k=KD)[:, k],
                                         attnT[:, c, :], start=(c == 0), stop=(c == CB - 1))
                last.then_inc(hq_done, 1)

            turn(0, 0, 1)
            similar(0)

            def xpair(i, end):
                b = i * 2
                turn(b + 1, 1, i + 1)
                turn_attn(b)
                similar(b + 1)
                attend(b, 0)
                if not end:
                    turn(b + 2, 0, i + 2)
                turn_attn(b + 1)
                if not end:
                    similar(b + 2)
                attend(b + 1, 1)

            with pe.Fori(0, B // 2 - 1) as i:
                xpair(i, False)
            xpair(B // 2 - 1, True)

            pe.wait_ge(batt_v, 1)
            pe.transpose(ps[0:B, 6, 0:S], small[0:S, 0:B], ident[0:S, 0:S]).then_inc(batt_p, 1)
            pe.wait_ge(batt_v, 3)
            for n in range(4):
                last = pe.matmul(ps[:, n, 0:GN], cst[0:B, C_ONE:C_ONE + 128], battD[:, 4 * n:4 * n + 4, :],
                                 start=True, stop=True)
            last.then_inc(batt_p, 1)
            pe.wait_ge(ld_xw, 16 * 5)
            def project(b, u):
                pe.wait_ge(feat_a, b + 1)
                pe.wait_ge(feat_v, b + 1)
                if not (isinstance(b, int) and b < 2):
                    pe.wait_ge(x_ready, b - 1)
                for c in range(8):
                    last = pe.matmul(ps[0:S, 6 + u, 0:D], feat[u][:, c, :], wqv[:, c, :], start=(c == 0), stop=(c == 7))
                last.then_inc(feat_done, 1)

            for u in range(2):
                project(u, u)
            with pe.Fori(1, B // 2) as i:
                for u in range(2):
                    project(i * 2 + u, u)
            pe.wait_ge(x_ready, B)
            pe.wait_ge(ld_ln, 48)
            pe.sem_inc(moe_done, 1)

            def layer(l):
                def norm_turn(b):
                    pe.wait_ge(a_xn1, l * B + b + 1)
                    for k in range(KD):
                        last = pe.transpose(ps[:, 6, k * S:k * S + S],
                                            xn1[:, :].rearrange("p (m k) -> p k m", k=KD)[:, k], ident[0:S, 0:S])
                    last.then_inc(p_t1, 1)

                def project_group(g):
                    pe.wait_ge(a_t1, l * B + 4 * g + 4)
                    if g:
                        pe.wait_ge(a_exp, l * B + 4 * g)
                    for bb in range(GB):
                        for k in range(KD):
                            last = pe.matmul(ps[0:S, bb, 0:NKV * HD], xnT[:, k, bb * S:bb * S + S],
                                             wv_s[:, k, :], start=(k == 0), stop=(k == KD - 1))
                        last.then_inc(p_v, 1)
                    for n in range(10):
                        if n < 4:
                            pe.wait_ge(a_v, l * B + 4 * g + n + 1)
                        else:
                            pe.wait_ge(d_rope, l * 40 + g * 10 + n - 3)
                        for k in range(KD):
                            last = pe.matmul(ps[:, n % 4, 0:GN], wqk_s[:, k, n, :], xnT[:, k, :], start=(k == 0), stop=(k == KD - 1))
                        last.then_inc(p_qk, 1)

                def scores(b):
                    g, bb = b // 4, b % 4
                    pe.wait_ge(d_rope, l * 40 + g * 10 + 10)
                    if bb:
                        pe.wait_ge(a_exp, l * B + b)
                    for p in range(2):
                        for i in range(4):
                            n, c = 2 * p + i // 2, i % 2 * 2 * S
                            pe.matmul(ps[0:S, n, c:c + 2 * S], ident_b[:, :], causal_b[:, :, :], start=True, stop=False)
                            last = pe.matmul(ps[0:S, n, c:c + 2 * S], qT[:, 4 * p + i, bb * S:bb * S + S],
                                             kz[:, p, :, bb * S:bb * S + S], start=False, stop=True)
                    last.then_inc(p_sc, 1)

                def turn_probs(b, unit):
                    p, j = unit // 2, unit % 2
                    if unit == 0:
                        pe.wait_ge(d_norm, l * B + b + 1)
                    if unit >= 2:
                        pe.wait_ge(a_pt, l * 64 + b * 4 + unit - 1)
                    for i in range(4):
                        last = pe.transpose(ps[0:S, 4 + unit % 2, i * S:i * S + S],
                                            prob[:, b % 2, p * 8 + i * 2 + j, :], ident[0:S, 0:S])
                    last.then_inc(p_pt, 1)

                def weigh(b, unit):
                    p, j = unit // 2, unit % 2
                    pe.wait_ge(a_pt, l * 64 + b * 4 + unit + 1)
                    last = pe.matmul(ps[64 * j:64 * j + 64, 6 + p, 0:GN], v_s[:, VALUES[b], unit * HD:unit * HD + HD],
                                     probT[:, unit, :], start=True, stop=True)
                    if j == 1:
                        last.then_inc((p_ot0, p_ot1)[p], 1)

                def attend_values(b):
                    turn_probs(b, 0)
                    turn_probs(b, 1)
                    for unit in range(4):
                        weigh(b, unit)
                        if unit < 2:
                            turn_probs(b, unit + 2)

                def turn_x(b):
                    pe.wait_ge(d_wo, l * B + b + 1)
                    for k in range(KD):
                        last = pe.transpose(ps[:, 5, k * S:k * S + S],
                                            x_sb[:, b, 0:D].rearrange("p (m k) -> p k m", k=KD)[:, k], ident[0:S, 0:S])
                    last.then_inc(p_t2, 1)

                def route_logits(b):
                    pe.wait_ge(a_t2, l * B + b + 1)
                    for k in range(KD):
                        last = pe.matmul(ps[0:S, 7, 0:E], x2T[:, k, :], wr_l[:, k, :],
                                         start=(k == 0), stop=(k == KD - 1))
                    last.then_inc(p_lg, 1)

                def out_project(b):
                    pe.wait_ge(a_ot, l * B + b + 1)
                    for i in range(4):
                        pe.matmul(ps[0:S, 6, 0:D], oT[:, 0, i * S:i * S + S], wo_s[:, i, :], start=(i == 0), stop=False)
                    pe.wait_ge(d_ot, l * B + b + 1)
                    for i in range(4):
                        last = pe.matmul(ps[0:S, 6, 0:D], oT[:, 1, i * S:i * S + S], wo_s[:, 4 + i, :],
                                         start=False, stop=(i == 3))
                    last.then_inc(p_wo, 1)

                def count_rows(h):
                    pe.wait_ge(d_oh, l * 2 + h + 1)
                    flat = oh_b[:, :, :].rearrange("p a e -> p (a e)")
                    pe.matmul(ps[0:S, 7, 128:256], low_b[:, :], flat, start=True, stop=True)
                    pe.matmul(ps[0:S, 7, 256:384], ones_b[:, :], flat, start=True, stop=True).then_inc(p_rt, 1)

                wr_l = small_wr
                for b in range(GB):
                    norm_turn(b)
                    pe.wait_ge(a_t1, l * B + b + 1)
                pe.wait_ge(ld_aw, (l + 1) * 16 * 5)
                pe.wait_ge(aw_ready, l + 1)
                project_group(0)
                scores(0)
                for g in range(NG):
                    for bb in range(GB):
                        b = g * 4 + bb
                        if bb < 3:
                            scores(b + 1)
                        elif g < NG - 1:
                            project_group(g + 1)
                        attend_values(b)
                        if bb == 3 and g < NG - 1:
                            scores(b + 1)
                        if b:
                            turn_x(b - 1)
                        out_project(b)
                        if g < NG - 1:
                            for nb in TURN[bb]:
                                pe.wait_ge(d_wo, l * B + b + 1)
                                if nb:
                                    pe.wait_ge(a_t1, l * B + 4 * g + 4 + nb)
                                norm_turn(4 * g + 4 + nb)
                        if b:
                            route_logits(b - 1)
                            pe.wait_ge(d_lg, l * B + b)
                        if b == 10:
                            count_rows(0)
                            pe.wait_ge(d_rt, l * 2 + 1)
                turn_x(B - 1)
                route_logits(B - 1)
                count_rows(1)
                pe.wait_ge(d_rt, l * 2 + 2)

                pe.wait_ge(ld_mw, (l + 1) * 16 * 3 * E)

                def turn_tile(T, u, n):
                    pe.wait_ge(ld_xe[u], l * (8 * NT) + n * 16)
                    if not (isinstance(T, int) and T == 0):
                        pe.wait_ge(m_xT, l * NT + T)
                    for k in range(KD):
                        last = pe.transpose(ps[:, 5, k * SLOT:k * SLOT + SLOT],
                                            xe[u][:, 0:D].rearrange("p (m k) -> p k m", k=KD)[:, k], ident)
                    last.then_inc(m_tx, 1)

                def up(T, u, e, w, bank, done):
                    for k in range(KD):
                        last = pe.matmul(ps[:, bank, :], xeT[u][:, k, :], w[:, bass.ds(e * 1024 + k * 512, 512)],
                                         start=(k == 0), stop=(k == KD - 1))
                    last.then_inc(done, 1)

                def turn_hidden(T, u):
                    pe.wait_ge(m_h, l * NT + T + 1)
                    if not (isinstance(T, int) and T == 0):
                        pe.wait_ge(m_hT, l * NT + T)
                    for c in range(4):
                        last = pe.transpose(ps[:, 4, c * SLOT:c * SLOT + SLOT],
                                            hid[u].rearrange("p (m c) -> p c m", c=4)[:, c], ident)
                    last.then_inc(m_th, 1)

                def down(T, u, e):
                    pe.wait_ge(m_hT, l * NT + T + 1)
                    if not (isinstance(T, int) and T == 0):
                        pe.wait_ge(m_y, l * NT + T)
                    for c in range(4):
                        last = pe.matmul(ps[:, 6 + u, 0:D], hidT[:, c, :], wd_s[:, bass.ds(e * 1024 + c * D, D)],
                                         start=(c == 0), stop=(c == 3))
                    last.then_inc(m_dn, 1)

                def expert_of(T):
                    return pe.value_load(tile_e[0:1, bass.ds(T, 1)], min_val=0, max_val=E - 1)

                def pair(i, first=False, end=False):
                    for u in range(2):
                        T = i * 2 + u
                        e = expert_of(T)
                        pe.wait_ge(m_xT, l * NT + T + 1)
                        if not first:
                            pe.wait_ge(m_h, l * NT + T - 1)
                        up(T, u, e, wg_s, 2 * u, m_g)
                        if not (first and u == 0):
                            turn_hidden(T - 1, 1 - u)
                        up(T, u, e, wu_s, 2 * u + 1, m_u)
                        if not (end and u == 1):
                            turn_tile(T + 1, 1 - u, i + 1 + u)
                        if not (first and u == 0):
                            down(T - 1, 1 - u, expert_of(T - 1))

                turn_tile(0, 0, 1)
                pair(0, first=True)
                with pe.Fori(1, NT // 2 - 1) as i:
                    pair(i)
                pair(NT // 2 - 1, end=True)
                turn_hidden(NT - 1, 1)
                down(NT - 1, 1, expert_of(NT - 1))
                pe.wait_ge(m_y, (l + 1) * NT)
                pe.sem_inc(moe_done, 1)

            with pe.Fori(0, L) as l:
                small_wr = wr_s[:, bass.ds(l, 1), :, :].rearrange("p a k e -> p (a k) e")
                layer(l)

        @block.scalar
        def _(act):
            act.wait_ge(ld_const, 16)
            act.activation(ident_b[:, :], cst[0:S, C_ID:C_ID + S], ACT.Copy).then_inc(c_bf, 1)
            act.activation(causal_b[:, :, :], bc(cst[0:S, C_CAUSAL:C_CAUSAL + S], 1, [S, 2, S]), ACT.Copy).then_inc(c_bf, 1)
            act.activation(low_b[:, :], cst[0:S, C_LOW:C_LOW + S], ACT.Copy).then_inc(c_bf, 1)
            act.activation(ones_b[:, :], cst[0:S, C_ONE:C_ONE + S], ACT.Copy).then_inc(c_bf, 1)

            def copy_turned(b):
                act.wait_ge(xT_done, b + 1)
                act.activation(decT[:, 0, :], ps[:, 0, 0:CTX], ACT.Copy).then_inc(decT_a, 1)
                act.activation(encT[:, :, bass.ds(b * S, S)], ps[:, 2, 0:KD * S].rearrange("p (k i) -> p k i", k=KD),
                               ACT.Copy).then_inc(encT_ready, 1)

            def exponents(b):
                act.wait_ge(max_ready, b + 1)
                act.activation(attn[:, 0:CTX], ps[0:S, 3, 0:CTX], ACT.Exp, bias=small[0:S, 33:34],
                               accum_out=small[0:S, 34:35]).then_inc(exp_done, 1)

            def copy_attn(b):
                act.wait_ge(aT_done, b + 1)
                act.activation(attnT, ps[0:CR, 4, 0:CB * S].rearrange("p (c i) -> p c i", c=CB), ACT.Copy).then_inc(aT_ready, 1)

            copy_turned(0)
            exponents(0)

            def xstep(b):
                copy_turned(b + 1)
                copy_attn(b)
                exponents(b + 1)

            with act.Fori(0, B - 1) as b:
                xstep(b)
            copy_attn(B - 1)

            act.wait_ge(batt_v, 2)
            act.activation(battD[:, 0, :], ps[0:B, 6, 0:S], ACT.Exp, bias=small[0:B, 41:42],
                           accum_out=small[0:B, 42:43]).then_inc(batt_a, 1)

            def features(b, u):
                if isinstance(b, int) and b < 2:
                    act.wait_ge(hq_ready, B)
                else:
                    act.wait_ge(feat_done, b - 1)
                act.activation(feat[u][:, 0:2, :], encT[:, :, bass.ds(b * S, S)], ACT.Copy)
                act.activation(feat[u][:, 2:4, :], hqT[:, :, bass.ds(b * S, S)], ACT.Copy).then_inc(feat_a, 1)

            for u in range(2):
                features(u, u)
            with act.Fori(1, B // 2) as i:
                for u in range(2):
                    features(i * 2 + u, u)
            act.wait_ge(ld_ln, 48)

            def layer(l):
                def square_in(b):
                    act.wait_ge(d_x, l * B + b + 1)
                    if b:
                        act.wait_ge(a_sq1, l * B + b)
                    act.activation(xsq[:, 0, :], x_sb[:, b, 0:D], ACT.Square, scale=1.0 / 16,
                                   accum_out=ms1[:, b % 4:b % 4 + 1]).then_inc(a_sq1, 1)

                def norm_in(b):
                    act.wait_ge(g_r1, l * NG + b // 4 + 1)
                    act.activation(xn1[:, :], x_sb[:, b, 0:D], ACT.Copy, scale=r1[:, b % 4:b % 4 + 1]).then_inc(a_xn1, 1)

                def copy_in(b):
                    act.wait_ge(p_t1, l * B + b + 1)
                    alone(act)
                    for k in range(KD):
                        last = act.activation(xnT[:, k, (b % 4) * S:(b % 4) * S + S], ps[:, 6, k * S:k * S + S],
                                              ACT.Copy, scale=ln1T[:, bass.ds(l, 1), k])
                    last.then_inc(a_t1, 1)

                def copy_values(g):
                    for bb in range(GB):
                        act.wait_ge(p_v, l * B + 4 * g + bb + 1)
                        act.activation(v_s[:, VALUES[4 * g + bb], :], ps[0:S, bb, 0:NKV * HD], ACT.Copy).then_inc(a_v, 1)

                def exponents(b):
                    act.wait_ge(d_max, l * B + b + 1)
                    for n in range(NH):
                        bank, h = n // 4, n % 4
                        last = act.activation(prob[:, b % 2, n, :], ps[0:S, bank, h * S:h * S + S], ACT.Exp,
                                              bias=nmax[:, b % 2, n:n + 1], scale=SCALE, accum_out=rsum[:, b % 2, n:n + 1])
                    last.then_inc(a_exp, 1)

                def copy_probs(b):
                    for unit in range(4):
                        act.wait_ge(p_pt, l * 64 + b * 4 + unit + 1)
                        act.activation(probT[:, unit, :], ps[0:S, 4 + unit % 2, 0:GN], ACT.Copy).then_inc(a_pt, 1)

                def copy_outputs(b):
                    act.wait_ge(p_ot0, l * B + b + 1)
                    act.activation(oT[:, 0, :], ps[:, 6, 0:GN], ACT.Copy).then_inc(a_ot, 1)

                def square_out(b):
                    act.wait_ge(d_wo, l * B + b + 1)
                    if b:
                        act.wait_ge(a_sq2, l * B + b)
                    act.activation(xsq[:, 1, :], x_sb[:, b, 0:D], ACT.Square, scale=1.0 / 16,
                                   accum_out=ms2[:, b:b + 1]).then_inc(a_sq2, 1)

                def copy_out(b):
                    act.wait_ge(p_t2, l * B + b + 1)
                    alone(act)
                    for k in range(KD):
                        last = act.activation(x2T[:, k, :], ps[:, 5, k * S:k * S + S], ACT.Copy,
                                              scale=ln2T[:, bass.ds(l, 1), k])
                    last.then_inc(a_t2, 1)

                def gate_exponents(h):
                    act.wait_ge(d_oh, l * 2 + h + 1)
                    act.activation(gate[:, 1, :], gate[:, 0, :], ACT.Exp).then_inc(a_rt, 1)

                for b in range(GB):
                    square_in(b)
                for b in range(GB):
                    norm_in(b)
                    copy_in(b)
                copy_values(0)
                exponents(0)
                for g in range(NG):
                    for bb in range(GB):
                        b = g * 4 + bb
                        if bb == 3 and g < NG - 1:
                            copy_values(g + 1)
                        copy_probs(b)
                        copy_outputs(b)
                        if bb < 3 or g < NG - 1:
                            if bb < 3:
                                exponents(b + 1)
                        if b:
                            copy_out(b - 1)
                        if bb == 3 and g < NG - 1:
                            exponents(b + 1)
                        if g < NG - 1:
                            for nb in PREP[bb]:
                                square_in(4 * g + 4 + nb)
                            for nb in TURN[bb]:
                                norm_in(4 * g + 4 + nb)
                                copy_in(4 * g + 4 + nb)
                        square_out(b)
                        if b == 9:
                            gate_exponents(0)
                copy_out(B - 1)
                gate_exponents(1)

                def copy_tile(T, u):
                    act.wait_ge(m_tx, l * NT + T + 1)
                    alone(act)
                    for k in range(KD):
                        last = act.activation(xeT[u][:, k, :], ps[:, 5, k * SLOT:k * SLOT + SLOT], ACT.Copy,
                                              scale=ln2T[:, bass.ds(l, 1), k])
                    last.then_inc(m_xT, 1)

                def tanh(T, u):
                    act.wait_ge(m_g, l * NT + T + 1)
                    act.wait_ge(m_r, l * NT + T + 1)
                    if not (isinstance(T, int) and T == 0):
                        act.wait_ge(m_h, l * NT + T)
                    act.activation(th, ps[:, 2 * u, :], ACT.Tanh, scale=er[:, u, 0:1]).then_inc(m_tanh, 1)

                def copy_hidden(T):
                    act.wait_ge(m_th, l * NT + T + 1)
                    if not (isinstance(T, int) and T == 0):
                        act.wait_ge(m_dn, l * NT + T)
                    act.activation(hidT, ps[:, 4, :].rearrange("p (c t) -> p c t", c=4), ACT.Copy).then_inc(m_hT, 1)

                def pair(i, first=False, end=False):
                    for u in range(2):
                        T = i * 2 + u
                        tanh(T, u)
                        if not (first and u == 0):
                            copy_hidden(T - 1)
                        if not (end and u == 1):
                            copy_tile(T + 1, 1 - u)

                copy_tile(0, 0)
                pair(0, first=True)
                with act.Fori(1, NT // 2 - 1) as i:
                    pair(i)
                pair(NT // 2 - 1, end=True)
                copy_hidden(NT - 1)

            with act.Fori(0, L) as l:
                layer(l)

        @block.vector
        def _(dve):
            dve.wait_ge(ld_x, 16)
            dve.wait_ge(ld_xw, 16 * 5)

            def normed(step, src, dst, n, done):
                alone(dve)
                step(dve.bn_stats(small[0:S, 20:26], src))
                alone(dve)
                step(dve.bn_aggr(small[0:S, 26:28], small[0:S, 20:26]))
                dve.sem_inc(var_ready, 1)
                dve.wait_ge(rstd_ready, n)
                dve.tensor_scalar(dst, src, small[0:S, 26:27], small[0:S, 28:29],
                                  ALU.subtract, ALU.mult).then_inc(done, 1)

            def xrow(b):
                return x_sb[:, bass.ds(b, 1), 0:D].rearrange("p a d -> p (a d)")

            def encode(b, u, base):
                step = Steps(dve, dx, base)
                normed(step, xrow(b), enc[u], b + 1, enc_ready)
                dve.wait_ge(enc_ready, b + 1)
                step(dve.scalar_tensor_tensor(out=scratch, in0=enc[u], scalar=1.0, in1=w1row, op0=ALU.mult, op1=ALU.mult,
                                              accum_out=simrow[:, bass.ds(b, 1)]))
                assert step.n == 3

            def copy_turned(b):
                dve.wait_ge(xT_done, b + 1)
                dve.tensor_copy(decT[:, 1, :], ps[:, 1, 0:CTX]).then_inc(decT_v, 1)
                dve.wait_ge(encT_ready, b + 1)
                for k in range(KD):
                    last = dve.tensor_scalar(e3T[:, k, :], encT[:, k, bass.ds(b * S, S)], wsT[:, 2, k:k + 1],
                                             wsT[:, 1, k:k + 1], ALU.mult, ALU.add)
                last.then_inc(e3_ready, 1)

            def row_max(b, base):
                step = Steps(dve, dx, base)
                dve.wait_ge(sim_done, b + 1)
                step(dve.tensor_reduce(small[0:S, 32:33], ps[0:S, 3, 0:CTX], AX_X, ALU.max))
                dve.tensor_scalar(small[0:S, 33:34], small[0:S, 32:33], -1.0, None, ALU.mult).then_inc(max_ready, 1)
                step(dve.scalar_tensor_tensor(out=simmax[:, bass.ds(b, 1)], in0=small[0:S, 32:33], scalar=bsim[:, :],
                                              in1=simrow[:, bass.ds(b, 1)], op0=ALU.add, op1=ALU.add))
                assert step.n == 2

            def scale_attn(b, base):
                step = Steps(dve, dx, base)
                dve.wait_ge(exp_done, b + 1)
                step(dve.reciprocal(small[0:S, 35:36], small[0:S, 34:35]))
                dve.tensor_scalar(attn[:, 0:CTX], attn[:, 0:CTX], small[0:S, 35:36], None, ALU.mult).then_inc(attn_ready, 1)

            def copy_hq(b):
                dve.wait_ge(hq_done, b + 1)
                dve.tensor_copy(hqT[:, :, bass.ds(b * S, S)],
                                ps[:, 5, 0:KD * S].rearrange("p (k i) -> p k i", k=KD)).then_inc(hq_ready, 1)

            simmax = small[0:S, 0:B]
            encode(0, 0, 0)
            copy_turned(0)
            encode(1, 1, 3)
            row_max(0, 6)
            scale_attn(0, 8)

            def xstep(b, u, base, more):
                copy_turned(b + 1)
                n = 0
                if more:
                    encode(b + 2, u, base)
                    n = 3
                row_max(b + 1, base + n)
                copy_hq(b)
                scale_attn(b + 1, base + n + 2)

            with dve.Fori(0, B // 2 - 1) as i:
                for u in range(2):
                    xstep(i * 2 + u, u, i * 12 + 9 + 6 * u, True)
            base = 9 + 12 * (B // 2 - 1)
            xstep(B - 2, 0, base, False)
            copy_hq(B - 1)
            step = Steps(dve, dx, base + 3)
            dve.sem_inc(batt_v, 1)
            dve.wait_ge(batt_p, 1)
            step(dve.tensor_reduce(small[0:B, 40:41], ps[0:B, 6, 0:S], AX_X, ALU.max))
            step(dve.tensor_scalar(small[0:B, 41:42], small[0:B, 40:41], -1.0, None, ALU.mult))
            dve.sem_inc(batt_v, 1)
            dve.wait_ge(batt_a, 1)
            step(dve.reciprocal(small[0:B, 43:44], small[0:B, 42:43]))
            step(dve.tensor_scalar(batt, battD[:, 0, :], small[0:B, 43:44], None, ALU.mult))
            step(dve.tensor_tensor(battD, bc(cst[0:B, C_ID:C_ID + B], 2, [B, B, S]), bc(batt, 1, [B, B, S]), ALU.mult))
            dve.sem_inc(batt_v, 1)
            dve.wait_ge(batt_p, 2)
            for k in range(KD):
                for n in range(4):
                    ins = dve.tensor_tensor(prodT[:, 4 * n:4 * n + 4, :],
                                            encT[:, k, n * GN:n * GN + GN].rearrange("p (b i) -> p b i", b=4),
                                            ps[:, n, 0:GN].rearrange("p (b i) -> p b i", b=4), ALU.mult)
                step(ins)
                step(dve.tensor_reduce(hcT[:, k, :], prodT, AX_X, ALU.add))
            base = base + 3 + step.n

            def features(b, u, base):
                step = Steps(dve, dx, base)
                if not (isinstance(b, int) and b < 2):
                    dve.wait_ge(feat_done, b - 1)
                e = encT[:, :, bass.ds(b * S, S)]
                dve.tensor_tensor(feat[u][:, 4:6, :], e, hqT[:, :, bass.ds(b * S, S)], ALU.mult)
                for k in range(KD):
                    last = dve.tensor_scalar(feat[u][:, 6 + k, :], encT[:, k, bass.ds(b * S, S)],
                                             hcT[:, k, bass.ds(b, 1)], None, ALU.mult)
                last.then_inc(feat_v, 1)

            def finish_x(b, u, base):
                step = Steps(dve, dx, base)
                r = res[:, bass.ds(b, 1), :].rearrange("p a d -> p (a d)")
                dve.wait_ge(feat_done, b + 1)
                step(dve.tensor_tensor(r, ps[0:S, 6 + u, 0:D], bqv, ALU.add))
                step(dve.tensor_tensor(r, r, xrow(b), ALU.add))
                normed(step, r, xrow(b), b + B + 1, x_ready)
                assert step.n == 4

            features(0, 0, 0)
            features(1, 1, 0)
            with dve.Fori(0, B // 2 - 1) as i:
                for u in range(2):
                    finish_x(i * 2 + u, u, i * 8 + 4 * u + base)
                    features(i * 2 + u + 2, u, 0)
            base += 8 * (B // 2 - 1)
            finish_x(B - 2, 0, base)
            finish_x(B - 1, 1, base + 4)
            dve.wait_ge(z_ready, 4)
            dve.wait_ge(x_ready, B)

            def combine(step, l, b):
                dve.wait_ge(gathered[b % 2], l * (16 * TOPK * B // 2) + (b // 2 + 1) * 16 * TOPK)
                step(dve.tensor_scalar(mix_b, y_in[:, b % 2, 0, :], wts[:, b, 0:1], None, ALU.mult))
                ins = dve.scalar_tensor_tensor(out=mix_b, in0=y_in[:, b % 2, 1, :], scalar=wts[:, b, 1:2], in1=mix_b,
                                               op0=ALU.mult, op1=ALU.add)
                ins.then_inc(d_yr, 1)
                dve.wait_ge(d_yr, l * B + b + 1)
                step(dve.tensor_tensor(x_sb[:, b, 0:D], x_sb[:, b, 0:D], mix_b, ALU.add))

            def layer(l):
                step = Steps(dve, dv, l * DVE_LAYER)

                def rows_in(b):
                    combine(step, l, b)
                    dve.tensor_scalar(x_sb[:, b, 0:D], x_sb[:, b, 0:D], CLIP, -CLIP, ALU.min, ALU.max).then_inc(d_x, 1)

                def rotate(g):
                    for n in range(10):
                        dve.wait_ge(p_qk, l * 40 + g * 10 + n + 1)
                        if g or n:
                            dve.wait_ge(d_rope, l * 40 + g * 10 + n)
                        src = ps[:, n % 4, 0:GN].rearrange("p (b t) -> p b t", b=GB)
                        c = rope_c[:, :].rearrange("p (b t) -> p b t", b=GB)
                        s = rope_s[:, :].rearrange("p (b t) -> p b t", b=GB)
                        dve.tensor_tensor(c, src, bc(cst[:, C_COS:C_COS + S], 1, [128, GB, S]), ALU.mult)
                        for a, z in ((0, 64), (64, 0)):
                            ins = dve.tensor_tensor(s[a:a + 64], src[z:z + 64],
                                                    bc(cst[a:a + 64, C_SIN:C_SIN + S], 1, [64, GB, S]), ALU.mult)
                        step(ins)
                        if n < 2:
                            step(dve.tensor_tensor(rope_c[:, :], rope_c[:, :], rope_s[:, :], ALU.add))
                            for j in range(2):
                                ins = dve.tensor_scalar(kz[:, n, j, :], rope_c[:, :], cst[:, C_J + j:C_J + j + 1],
                                                        None, ALU.mult)
                        else:
                            ins = dve.tensor_tensor(qT[:, n - 2, :], rope_c[:, :], rope_s[:, :], ALU.add)
                        ins.then_inc(d_rope, 1)

                def maxima(b):
                    dve.wait_ge(p_sc, l * B + b + 1)
                    step(dve.tensor_reduce(rmax[:, :].rearrange("p (n h) -> p n h", n=4), heads(b), AX_X, ALU.max))
                    dve.tensor_scalar(nmax[:, b % 2, :], rmax[:, :], -SCALE, None, ALU.mult).then_inc(d_max, 1)

                def scale_probs(b):
                    dve.wait_ge(a_exp, l * B + b + 1)
                    step(dve.reciprocal(rrec[:, :], rsum[:, b % 2, :]))
                    dve.tensor_tensor(prob[:, b % 2], prob[:, b % 2], bc(rrec[:, :], 2, [S, NH, S]), ALU.mult).then_inc(d_norm, 1)

                def copy_outputs(b):
                    dve.wait_ge(p_ot1, l * B + b + 1)
                    dve.tensor_copy(oT[:, 1, :], ps[:, 7, 0:GN]).then_inc(d_ot, 1)

                def add_attention(b):
                    dve.wait_ge(p_wo, l * B + b + 1)
                    step(dve.tensor_tensor(x_sb[:, b, 0:D], ps[0:S, 6, 0:D], x_sb[:, b, 0:D], ALU.add))
                    dve.tensor_scalar(x_sb[:, b, 0:D], x_sb[:, b, 0:D], CLIP, -CLIP, ALU.min, ALU.max).then_inc(d_wo, 1)

                def logits(b):
                    dve.wait_ge(p_lg, l * B + b + 1)
                    dve.tensor_copy(lg[:, b, :], ps[0:S, 7, 0:E]).then_inc(d_lg, 1)

                def choose(h):
                    dve.wait_ge(d_lg, l * B + h * HALF + HALF)
                    dve.wait_ge(g_r2, l * 2 + h + 1)
                    hs = slice(h * HALF, h * HALF + HALF)
                    dve.tensor_tensor(lg[:, hs, :], lg[:, hs, :], bc(r2[:, :], 2, [S, HALF, E]), ALU.mult)
                    dve.tensor_copy(x_sb[:, hs, D], r2[:, :])
                    step(dve.tensor_scalar(x_sb[:, hs, D + 1], r2[:, :], 0.5, None, ALU.mult))
                    step(dve.tensor_tensor(x_sb[:, hs, D + 2], r2[:, :], x_sb[:, hs, D + 1], ALU.mult))
                    alone(dve)
                    for b in range(HALF):
                        ins = dve.max(top[:, b, :], lg[:, h * HALF + b, :])
                    step(ins)
                    alone(dve)
                    for b in range(HALF):
                        ins = dve.max_index(idx[:, b, :], top[:, b, :], lg[:, h * HALF + b, :])
                    step(ins)
                    step(dve.tensor_copy(idxf[:, :, :], idx[:, :, 0:TOPK]))
                    N = HALF * TOPK
                    step(dve.tensor_tensor(oh[:, :, :], bc(idxf[:, :, :].rearrange("p b k -> p (b k)"), 2, [S, N, E]),
                                           bc(cst[0:S, C_E:C_E + E], 1, [S, N, E]), ALU.is_equal))
                    step(dve.tensor_tensor(gate[:, 0, :], top[:, :, 1], top[:, :, 0], ALU.subtract))
                    dve.tensor_copy(oh_b[:, :, :], oh[:, :, :]).then_inc(d_oh, 1)

                def place(h):
                    N = HALF * TOPK
                    dve.wait_ge(p_rt, l * 2 + h + 1)
                    before = ps[0:S, 7, 128:256].rearrange("p (a e) -> p a e", e=E)
                    total = ps[0:S, 7, 256:384].rearrange("p (a e) -> p a e", e=E)
                    step(dve.tensor_copy(pre[0][:, :, :], total))
                    a = 0
                    for s in (1, 2, 4, 8):
                        dve.tensor_copy(pre[1 - a][:, 0:s, :], pre[a][:, 0:s, :])
                        step(dve.tensor_tensor(pre[1 - a][:, s:N, :], pre[a][:, s:N, :], pre[a][:, 0:N - s, :], ALU.add))
                        a = 1 - a
                    step(dve.tensor_tensor(cnt[:, :, :], bc(pre[a][:, N - 1, :], 2, [S, E, EPT]),
                                           bc(cst[0:S, C_M:C_M + EPT], 1, [S, E, EPT]), ALU.is_gt))
                    step(dve.tensor_reduce(tiles[:, :], cnt[:, :, :], AX_X, ALU.add))
                    step(dve.tensor_copy(cum[0][:, :], tiles[:, :]))
                    c = 0
                    for s in (1, 2, 4):
                        dve.tensor_copy(cum[1 - c][:, 0:s], cum[c][:, 0:s])
                        step(dve.tensor_tensor(cum[1 - c][:, s:E], cum[c][:, s:E], cum[c][:, 0:E - s], ALU.add))
                        c = 1 - c
                    step(dve.tensor_tensor(tef[:, :, :], bc(cum[c][0:1, :], 1, [1, HT, E]),
                                           bc(cst[0:1, C_T:C_T + HT], 2, [1, HT, E]), ALU.is_le))
                    step(dve.tensor_reduce(tes[:, :], tef[:, :, :], AX_X, ALU.add))
                    step(dve.tensor_scalar(tile_e[:, h * HT:h * HT + HT], tes[:, :], float(E - 1), None, ALU.min))
                    step(dve.tensor_tensor(tiles[:, :], cum[c][:, :], tiles[:, :], ALU.subtract))
                    step(dve.tensor_tensor(pre[a][:, :, :], pre[a][:, :, :], total, ALU.subtract))
                    step(dve.scalar_tensor_tensor(out=pre[a][:, :, :], in0=bc(tiles[:, :], 1, [S, N, E]), scalar=float(SLOT),
                                                  in1=pre[a][:, :, :], op0=ALU.mult, op1=ALU.add))
                    step(dve.tensor_tensor(pre[a][:, :, :], before, pre[a][:, :, :], ALU.add))
                    dve.sem_inc(d_rt, 1)
                    step(dve.tensor_tensor(pre[a][:, :, :], pre[a][:, :, :], oh[:, :, :], ALU.mult))
                    step(dve.tensor_reduce(posf[:, :], pre[a][:, :, :], AX_X, ALU.add))
                    hs = slice(h * HALF, h * HALF + HALF)
                    dve.tensor_copy(pos[:, hs, :].rearrange("p b k -> p (b k)"), posf[:, :]).then_inc(d_pos, 1)
                    dve.wait_ge(a_rt, l * 2 + h + 1)
                    step(dve.tensor_scalar(gate[:, 0, :], gate[:, 1, :], 1.0, None, ALU.add))
                    step(dve.reciprocal(wts[:, hs, 0], gate[:, 0, :]))
                    step(dve.tensor_tensor(wts[:, hs, 1], wts[:, hs, 0], gate[:, 1, :], ALU.mult))

                for b in range(GB):
                    rows_in(b)
                rotate(0)
                maxima(0)
                scale_probs(0)
                for g in range(NG):
                    for bb in range(GB):
                        b = g * 4 + bb
                        if bb < 3:
                            maxima(b + 1)
                        elif g < NG - 1:
                            rotate(g + 1)
                        copy_outputs(b)
                        if bb == 3 and g < NG - 1:
                            maxima(b + 1)
                        add_attention(b)
                        if g < NG - 1:
                            for nb in PREP[bb]:
                                rows_in(4 * g + 4 + nb)
                        if b:
                            logits(b - 1)
                        if bb < 3 or g < NG - 1:
                            scale_probs(b + 1)
                        if b == 8:
                            choose(0)
                        if b == 10:
                            place(0)
                logits(B - 1)
                choose(1)
                place(1)
                assert step.n == DVE_LAYER, step.n

                def copy_factors(T, u):
                    dve.wait_ge(m_tx, l * NT + T + 1)
                    dve.tensor_copy(er[:, u, :], xe[u][:, D + 1:D + 3]).then_inc(m_r, 1)

                def hidden(T, u, base):
                    step = Steps(dve, dm, base)
                    dve.wait_ge(m_tanh, l * NT + T + 1)
                    step(dve.scalar_tensor_tensor(out=th, in0=th, scalar=1.0, in1=ps[:, 2 * u, :], op0=ALU.add, op1=ALU.mult))
                    dve.wait_ge(m_u, l * NT + T + 1)
                    dve.scalar_tensor_tensor(out=hid[u], in0=th, scalar=er[:, u, 1:2], in1=ps[:, 2 * u + 1, :],
                                             op0=ALU.mult, op1=ALU.mult).then_inc(m_h, 1)

                def copy_result(T, u, n):
                    dve.wait_ge(m_dn, l * NT + T + 1)
                    dve.wait_ge(st_ye[u], l * (8 * NT) + n * 16)
                    dve.tensor_copy(ye[u], ps[:, 6 + u, 0:D]).then_inc(m_y, 1)

                mbase = l * NT

                def pair(i, first=False, end=False):
                    for u in range(2):
                        T = i * 2 + u
                        hidden(T, u, mbase + T)
                        if not (end and u == 1):
                            copy_factors(T + 1, 1 - u)
                        if not (first and u == 0):
                            copy_result(T - 1, 1 - u, i + u)

                copy_factors(0, 0)
                pair(0, first=True)
                with dve.Fori(1, NT // 2 - 1) as i:
                    pair(i)
                pair(NT // 2 - 1, end=True)
                copy_result(NT - 1, 1, NT // 2)

            with dve.Fori(0, L) as l:
                layer(l)

            step = Steps(dve, dv, L * DVE_LAYER)
            dve.wait_ge(ld_res, 16)
            for b in range(B):
                combine(step, L, b)
                step(dve.tensor_scalar(x_sb[:, b, 0:D], x_sb[:, b, 0:D], CLIP, -CLIP, ALU.min, ALU.max))
                dve.tensor_tensor(x_sb[:, b, 0:D], x_sb[:, b, 0:D], res[:, b, :], ALU.add).then_inc(d_x, 1)


VALUES = [b % 4 if b % 4 < 3 else 3 + b // 4 % 2 for b in range(B)]

PREP = {0: [0, 1], 1: [2, 3], 2: [], 3: []}
TURN = {0: [], 1: [], 2: [0, 1, 2, 3], 3: []}

_INS = ["x", "ctx_1024", "L0_xattn_w_sim", "L0_xattn_b_sim", "L0_xattn_W_qv", "L0_xattn_b_qv", "L0_ffn_ln1_w",
        "L0_ffn_ln2_w", "L0_ffn_wq", "L0_ffn_wk", "L0_ffn_wv", "L0_ffn_wo", "L0_ffn_wr", "L0_ffn_wg", "L0_ffn_wu",
        "L0_ffn_wd"]


def kernel(**inputs):
    import numpy as _np
    import concourse.bacc as _bacc
    from concourse import mybir as _mybir
    from concourse.bass_utils import run_bass_kernel_spmd as _run

    nc = _bacc.Bacc("TRN2", target_bir_lowering=False, num_devices=1)
    arrays, args = {}, []
    given = {name: _np.ascontiguousarray(inputs[name]) for name in _INS}
    given["constants"] = constants()
    for name, a in given.items():
        arrays[f"in_{name}_dram"] = a
        args.append(nc.dram_tensor(f"in_{name}_dram", a.shape, _mybir.dt.from_np(a.dtype), kind="ExternalInput").ap())
    args.append(nc.dram_tensor("out_0_dram", (B, S, D), _mybir.dt.float32, kind="ExternalOutput").ap())
    xattn_ffn(nc, *args)
    r = _run(nc, [arrays], core_ids=[0])
    return r.results[0]["out_0_dram"]
```

```python
from contextlib import ExitStack

import concourse.bass as bass
from concourse import mybir

ALU = mybir.AluOpType
ACT = mybir.ActivationFunctionType
AX_X = mybir.AxisListType.X
F32 = mybir.dt.float32
BF16 = mybir.dt.bfloat16
U32 = mybir.dt.uint32
I32 = mybir.dt.int32

B, S, D = 16, 112, 256
CTX = 375
CR = 125
CB = CTX // CR
L, NH, NKV, HD = 4, 16, 4, 64
FF, E, TOPK = 512, 8, 2
KD = D // 128
QKV = (NH + 2 * NKV) * HD
GB = 4
NG = B // GB
GN = GB * S
HALF = B // 2
SLOT = 128
HT = HALF * S * TOPK // SLOT + E - 1
NT = 2 * HT
HROWS = HT * SLOT
EPT = HALF * S // SLOT
DX = D + 4
EPS = 1e-05
CLIP = 100.0
NEG = -8.0e9
SCALE = float(HD) ** -0.5

C_ID, C_COS, C_SIN, C_LOW, C_ONE = 0, 128, 240, 352, 464
C_E, C_M, C_T, C_J, C_CAUSAL, C_H, C_END = 592, 600, 607, 628, 630, 742, 750

DVE_LAYER = 196



def constants():
    import numpy as np

    c = np.zeros((128, C_END), np.float32)
    c[:, C_ID:C_ID + 128] = np.eye(128, dtype=np.float32)
    inv = (1.0 / np.float32(10000.0) ** (np.arange(0, HD, 2, dtype=np.float32) / np.float32(HD))).astype(np.float32)
    angle = (np.arange(S, dtype=np.float32)[:, None] * inv).T
    cos, sin = np.cos(angle).astype(np.float32), np.sin(angle).astype(np.float32)
    for q in range(4):
        c[32 * q:32 * q + 32, C_COS:C_COS + S] = cos
        c[32 * q:32 * q + 32, C_SIN:C_SIN + S] = -sin if q < 2 else sin
        c[32 * q:32 * q + 32, C_J + q % 2] = 1.0
    t = np.arange(S)
    c[0:S, C_LOW:C_LOW + S] = t[:, None] < t[None, :]
    c[:, C_ONE:C_ONE + 128] = 1.0
    c[:, C_E:C_E + E] = np.arange(E)
    c[:, C_M:C_M + EPT] = SLOT * np.arange(EPT)
    c[:, C_T:C_T + HT] = np.arange(HT)
    c[0:S, C_CAUSAL:C_CAUSAL + S] = np.where(t[None, :] > t[:, None], np.float32(NEG), np.float32(0))
    c[:, C_H:C_END] = -0.5
    return c


class Steps:

    def __init__(self, engine, sem, base):
        self.engine, self.sem, self.base, self.n = engine, sem, base, 0

    def __call__(self, instruction):
        self.n += 1
        instruction.then_inc(self.sem, 1)
        self.engine.wait_ge(self.sem, self.base + self.n)


def xattn_ffn(nc, x, ctx_1024, w_sim, b_sim, W_qv, b_qv, ln1_w, ln2_w, wq, wk, wv, wo, wr, wg, wu, wd, const, out):
    with ExitStack() as stack:
        def sb(name, shape, dt=F32):
            return stack.enter_context(nc.sbuf_tensor(name, shape, dt))

        def sem(name):
            return stack.enter_context(nc.semaphore(name))

        sorted_x = [nc.dram_tensor(f"sorted_x{h}", [HROWS, DX], F32, kind="Internal").ap() for h in range(2)]
        sorted_y = [nc.dram_tensor(f"sorted_y{h}", [HROWS, D], F32, kind="Internal").ap() for h in range(2)]
        res_d = nc.dram_tensor("res_d", [S, B, D], F32, kind="Internal").ap()

        arena = sb("arena", [128, 3 * E * KD * FF])
        wg_s = arena[:, 0:8192]
        wu_s = arena[:, 8192:16384]
        wd_s = arena[:, 16384:24576]
        at = [0]

        def part(width, p=128):
            at[0] += width
            assert at[0] <= 24576
            return arena[0:p, at[0] - width:at[0]]

        dec = [part(CB * D, CR).rearrange("p (c d) -> p c d", c=CB) for _ in range(2)]
        decT = part(KD * CTX).rearrange("p (k j) -> p k j", k=KD)
        encT = part(KD * B * S).rearrange("p (k n) -> p k n", k=KD)
        hqT = part(KD * B * S).rearrange("p (k n) -> p k n", k=KD)
        e3T = part(KD * S).rearrange("p (k i) -> p k i", k=KD)
        attn = part(CTX + 1, S)
        attnT = part(CB * S, CR).rearrange("p (c i) -> p c i", c=CB)
        wqv = part(8 * D).rearrange("p (c n) -> p c n", c=8)
        feat = [part(8 * S).rearrange("p (c i) -> p c i", c=8) for _ in range(2)]
        res = part(B * D, S).rearrange("p (b d) -> p b d", b=B)
        bqv = part(D, S)
        w1row = part(D, S)
        enc = [part(D, S) for _ in range(2)]
        scratch = part(D, S)
        battD = part(B * S, B).rearrange("p (b i) -> p b i", b=B)
        simrow = part(B, S)
        batt = part(S, B)
        hcT = part(KD * B).rearrange("p (k b) -> p k b", k=KD)
        prodT = part(B * S).rearrange("p (b i) -> p b i", b=B)

        wqk_s = sb("wqk_s", [128, KD, 10, 128])
        wv_s = sb("wv_s", [128, KD, NKV * HD])
        wo_s = sb("wo_s", [128, 8, D])
        x_sb = sb("x_sb", [S, B, DX])
        y_in = sb("y_in", [S, 2, TOPK, D])
        xnT = sb("xnT", [128, KD, GN])
        qarena = sb("qarena", [128, 8 * GN])
        qT = qarena[:, :].rearrange("p (n t) -> p n t", n=8)
        kz = sb("kz", [128, 2, 2, GN])
        xe = [kz[:, 0, u, 0:DX] for u in range(2)]
        xeT = [qarena[:, 512 + 256 * u:768 + 256 * u].rearrange("p (k t) -> p k t", k=KD) for u in range(2)]
        th = qarena[:, 1024:1536]
        hid = [qarena[:, 1536 + 512 * u:2048 + 512 * u] for u in range(2)]
        hidT = qarena[:, 2560:3072].rearrange("p (c t) -> p c t", c=4)
        ye = [qarena[:, 3072 + 256 * u:3328 + 256 * u] for u in range(2)]
        v_s = sb("v_s", [S, GB + 1, NKV * HD])
        parena = sb("parena", [128, 2 * NH * S])
        prob = parena[0:S, :].rearrange("q (u n k) -> q u n k", u=2, n=NH)
        raw = parena[:, 0:KD * (NH + NKV) * HD].rearrange("p (k n) -> p k n", k=KD)
        probT = sb("probT", [S, NKV, GN])
        oT = sb("oT", [128, 2, GN])
        rope = [sb(f"rope{i}", [128, GN]) for i in range(2)]
        xn1 = sb("xn1", [S, 2, D])
        x2T = sb("x2T", [128, KD, S])

        cst = sb("cst", [128, C_END])
        ident = cst[:, C_ID:C_ID + 128]
        ident_b = sb("ident_b", [S, S], BF16)
        causal_b = sb("causal_b", [S, 2, S], BF16)
        low_b = sb("low_b", [S, S], BF16)
        ones_b = sb("ones_b", [S, S], BF16)
        ln1T = sb("ln1T", [128, L, KD])
        ln2T = sb("ln2T", [128, L, KD])
        wr_s = sb("wr_s", [128, L, KD, E])
        wsT = sb("wsT", [128, 3, KD])
        bsim = sb("bsim", [S, 1])
        small = sb("small", [128, 64])
        lg = sb("lg", [S, B, E])
        top = sb("top", [S, HALF, 8])
        idx = sb("idx", [S, HALF, 8], U32)
        idxf = sb("idxf", [S, HALF, TOPK])
        oh = sb("oh", [S, HALF * TOPK, E])
        oh_b = sb("oh_b", [S, HALF * TOPK, E], BF16)
        pre = [sb(f"pre{i}", [S, HALF * TOPK, E]) for i in range(2)]
        cnt = sb("cnt", [S, E, EPT])
        tiles = sb("tiles", [S, E])
        cum = [sb(f"cum{i}", [S, E]) for i in range(2)]
        posf = sb("posf", [S, HALF * TOPK])
        pos = sb("pos", [S, B, TOPK], U32)
        wts = sb("wts", [S, B, TOPK])
        tef = sb("tef", [1, HT, E])
        tes = sb("tes", [1, HT])
        tile_e = sb("tile_e", [1, 2 * HT], I32)

        rmax = sb("rmax", [S, NH])
        nmax = sb("nmax", [S, 2, NH])
        rsum = sb("rsum", [S, 2, NH])
        rrec = sb("rrec", [S, NH])
        gate = sb("gate", [S, 2, HALF])
        er = sb("er", [128, 2, 2])
        g_tmp = sb("g_tmp", [S, GB + HALF])
        ms1, r1 = sb("ms1", [S, GB]), sb("r1", [S, GB])
        ms2, r2 = sb("ms2", [S, B]), sb("r2", [S, HALF])
        xsq = sb("xsq", [S, 2, D], BF16)
        mix_b = rope[0][0:S, 0:D]

        ps = stack.enter_context(nc.psum_tensor("ps", [128, 8, 512], F32))

        ld_const, ld_x, ld_xw, ld_ln = sem("ld_const"), sem("ld_x"), sem("ld_xw"), sem("ld_ln")
        ld_dec = [sem(f"ld_dec{i}") for i in range(2)]
        ld_aw, ld_mw, ld_raw, aw_ready = sem("ld_aw"), sem("ld_mw"), sem("ld_raw"), sem("aw_ready")
        ld_xe = [sem(f"ld_xe{i}") for i in range(2)]
        st_ye = [sem(f"st_ye{i}") for i in range(2)]
        st_res, st_zero, st_out, ld_res = sem("st_res"), sem("st_zero"), sem("st_out"), sem("ld_res")
        gathered = [sem(f"gathered{i}") for i in range(2)]
        scattered = [sem(f"scattered{i}") for i in range(2)]
        c_bf, z_ready = sem("c_bf"), sem("z_ready")
        enc_ready, xT_done, decT_a, decT_v, encT_ready, e3_ready = (sem(n) for n in ("enc_ready", "xT_done", "decT_a", "decT_v", "encT_ready", "e3_ready"))
        sim_done, max_ready, exp_done, attn_ready, aT_done, aT_ready, hq_done, hq_ready = (sem(n) for n in (
            "sim_done", "max_ready", "exp_done", "attn_ready", "aT_done", "aT_ready", "hq_done", "hq_ready"))
        batt_v, batt_a, batt_p = sem("batt_v"), sem("batt_a"), sem("batt_p")
        feat_a, feat_v, feat_done, x_ready = sem("feat_a"), sem("feat_v"), sem("feat_done"), sem("x_ready")
        p_v, p_qk, p_sc, p_pt, p_ot0, p_ot1, p_wo, p_t2, p_lg, p_t1, p_rt = (sem(n) for n in (
            "p_v", "p_qk", "p_sc", "p_pt", "p_ot0", "p_ot1", "p_wo", "p_t2", "p_lg", "p_t1", "p_rt"))
        a_v, a_exp, a_pt, a_ot, a_sq1, a_xn1, a_t1, a_sq2, a_t2, a_rt = (sem(n) for n in (
            "a_v", "a_exp", "a_pt", "a_ot", "a_sq1", "a_xn1", "a_t1", "a_sq2", "a_t2", "a_rt"))
        d_rope, d_max, d_norm, d_ot, d_wo, d_lg, d_x, d_yr, d_oh, d_rt, d_pos = (sem(n) for n in (
            "d_rope", "d_max", "d_norm", "d_ot", "d_wo", "d_lg", "d_x", "d_yr", "d_oh", "d_rt", "d_pos"))
        m_tx, m_g, m_u, m_th, m_dn, moe_done = (sem(n) for n in ("m_tx", "m_g", "m_u", "m_th", "m_dn", "moe_done"))
        m_xT, m_tanh, m_hT = (sem(n) for n in ("m_xT", "m_tanh", "m_hT"))
        m_r, m_h, m_y = (sem(n) for n in ("m_r", "m_h", "m_y"))
        dv, dm, dx, passed = sem("dv"), sem("dm"), sem("dx"), sem("passed")
        g_eps, var_ready, rstd_ready, g_r1, g_r2, g_rope = (sem(n) for n in ("g_eps", "var_ready", "rstd_ready", "g_r1", "g_r2", "g_rope"))

        zero = probT[:, :, :].rearrange("p a b -> p (a b)")[:, 0:6 * DX].rearrange("p (r d) -> p r d", r=6)
        rows = S * 6
        ZERO_STORES = 4 * (HROWS // rows)
        assert HROWS % rows == 0

        block = stack.enter_context(nc.Block())

        def bc(ap, axis, shape):
            return ap.unsqueeze(axis).to_broadcast(shape)

        def alone(engine):
            engine.sem_inc(passed, 1)

        def heads(p):
            return ps[0:S, 2 * p:2 * p + 2, 0:GN].rearrange("q n (h k) -> q n h k", k=S)

        @block.sync
        def _(sp):
            sp.dma_start(cst[:, :], const).then_inc(ld_const, 16)
            sp.dma_start(x_sb[:, :, 0:D], x.rearrange("b s d -> s b d")).then_inc(ld_x, 16)
            sp.dma_start(w1row, w_sim[0:D].rearrange("(a d) -> a d", a=1).to_broadcast([S, D])).then_inc(ld_xw, 16)
            sp.dma_start(wsT[:, :, :], w_sim.rearrange("(g p k) -> p g k", g=3, k=KD)).then_inc(ld_xw, 16)
            sp.dma_start(bsim[:, :], b_sim.rearrange("(a d) -> a d", a=1).to_broadcast([S, 1])).then_inc(ld_xw, 16)

            def load_dec(b, u):
                sp.dma_start(dec[u], ctx_1024[b].rearrange("(c p) d -> p c d", p=CR) if isinstance(b, int) else
                             ctx_1024[bass.ds(b, 1)].rearrange("a (c p) d -> p (a c) d", p=CR)).then_inc(ld_dec[u], 16)

            load_dec(0, 0)
            load_dec(1, 1)
            sp.dma_start(wqv, W_qv.rearrange("(f p k) n -> p f k n", f=4, k=KD)).then_inc(ld_xw, 16)
            sp.dma_start(bqv, b_qv.rearrange("(a d) -> a d", a=1).to_broadcast([S, D])).then_inc(ld_xw, 16)
            sp.dma_start(ln1T[:, :, :], ln1_w.rearrange("l (p k) -> p l k", k=KD)).then_inc(ld_ln, 16)
            sp.dma_start(ln2T[:, :, :], ln2_w.rearrange("l (p k) -> p l k", k=KD)).then_inc(ld_ln, 16)
            sp.dma_start(wr_s[:, :, :, :], wr.rearrange("l (p k) e -> p l k e", k=KD)).then_inc(ld_ln, 16)
            with sp.Fori(0, B // 2 - 1) as i:
                for u in range(2):
                    sp.wait_ge(hq_done, i * 2 + u + 1)
                    load_dec(i * 2 + u + 2, u)

            def attention_weights(l):
                one = (lambda a: a[l]) if isinstance(l, int) else (lambda a: a[bass.ds(l, 1)].rearrange("a r c -> (a r) c"))
                for w, c0, c1 in ((wq, 0, NH * HD), (wk, NH * HD, (NH + NKV) * HD)):
                    sp.dma_start(raw[:, :, c0:c1], one(w).rearrange("(p k) n -> p k n", k=KD)).then_inc(ld_raw, 16)
                sp.dma_start(wv_s[:, :, :], one(wv).rearrange("(p k) n -> p k n", k=KD)).then_inc(ld_aw, 16)
                for j in range(2):
                    src = one(wo).rearrange("(p j i d) n -> j d p i n", p=2, j=2, i=4)[j]
                    for p in range(2):
                        sp.dma_start(wo_s[64 * j:64 * j + 64, 4 * p:4 * p + 4, :], src[:, p]).then_inc(ld_aw, 16)

            def expert_weights(l):
                for e in range(E):
                    sp.wait_ge(p_wo, l * B + e + 1)
                    for w, s, k in ((wg, wg_s, KD), (wu, wu_s, KD), (wd, wd_s, 4)):
                        src = w[l] if isinstance(l, int) else w[bass.ds(l, 1)].rearrange("a e r c -> (a e) r c")
                        src = src.rearrange("e (p k) n -> p e k n", k=k)
                        sp.dma_start(s[:, 1024 * e:1024 * e + 1024].rearrange("p (k n) -> p k n", k=k),
                                     src[:, e]).then_inc(ld_mw, 16)

            attention_weights(0)
            sp.wait_ge(st_zero, ZERO_STORES * 16)
            for u in range(2):
                sp.dma_start(sorted_y[u][0:1, :], zero[u:u + 1, 0, 0:D]).then_inc(st_ye[u], 16)
            sp.wait_ge(x_ready, B)
            sp.dma_start(res_d, res).then_inc(st_res, 16)

            def layer_io(l, last):
                sp.wait_ge(st_res, 16)
                sp.wait_ge(moe_done, l + 1)
                expert_weights(l)
                if not last:
                    sp.wait_ge(p_lg, (l + 1) * B)
                    attention_weights(l + 1)

                def load_tile(T, u, h, peeled=False):
                    if not peeled:
                        sp.wait_ge(m_tx, l * NT + T - 1)
                        sp.wait_ge(m_r, l * NT + T - 1)
                    sp.dma_start(xe[u], sorted_x[h][bass.ds((T - h * HT) * SLOT, SLOT), :]).then_inc(ld_xe[u], 16)

                def store_tile(T, u, h):
                    sp.wait_ge(m_y, l * NT + T + 1)
                    sp.dma_start(sorted_y[h][bass.ds((T - h * HT) * SLOT, SLOT), :], ye[u]).then_inc(st_ye[u], 16)

                sp.wait_ge(p_lg, (l + 1) * B)
                sp.wait_ge(scattered[0], (l + 1) * 16 * HALF * TOPK)
                load_tile(0, 0, 0, True)
                load_tile(1, 1, 0, True)

                def pair(i, load, store, first=False, end=False):
                    for u in range(2):
                        if not end:
                            if load[u] == 1 and load[0] == 0:
                                sp.wait_ge(scattered[1], (l + 1) * 16 * HALF * TOPK)
                                alone(sp)
                            load_tile(i * 2 + u + 2, u, load[u])
                        if not (first and u == 0):
                            store_tile(i * 2 + u - 1, 1 - u, store[u])

                mid = (HT - 3) // 2
                assert 2 * mid + 3 == HT
                pair(0, (0, 0), (0, 0), first=True)
                with sp.Fori(1, mid) as i:
                    pair(i, (0, 0), (0, 0))
                pair(mid, (0, 1), (0, 0))
                pair(mid + 1, (1, 1), (0, 0))
                with sp.Fori(mid + 2, NT // 2 - 1) as i:
                    pair(i, (1, 1), (1, 1))
                pair(NT // 2 - 1, (1, 1), (1, 1), end=True)
                store_tile(NT - 1, 1, 1)

            with sp.Fori(0, L - 1) as l:
                layer_io(l, False)
            layer_io(L - 1, True)
            sp.wait_ge(moe_done, L + 1)
            sp.dma_start(res, res_d).then_inc(ld_res, 16)
            sp.wait_ge(d_x, L * B + B)
            sp.dma_start(out.rearrange("b s d -> s b d"), x_sb[:, :, 0:D]).then_inc(st_out, 16)
            sp.wait_ge(st_out, 16)

        @block.gpsimd
        def _(pool):
            pool.memset(probT[:, :, :], 0.0).then_inc(z_ready, 1)
            pool.memset(pos[:, :, :], 0).then_inc(z_ready, 1)
            pool.memset(wts[:, :, :], 0.0).then_inc(z_ready, 1)
            pool.memset(x_sb[:, :, D:DX], 0.0).then_inc(z_ready, 1)
            pool.wait_ge(z_ready, 4)
            zeroed = [(t, n) for n in range(HROWS // rows) for t in (*sorted_x, *sorted_y)]
            assert len(zeroed) <= B

            def norm_factors(out, var, n, at=0):
                width = var.shape[-1]
                alone(pool)
                pool.tensor_scalar(g_tmp[:, at:at + width], var, EPS, None, ALU.add).then_inc(g_eps, 1)
                pool.wait_ge(g_eps, n)
                return pool.tensor_tensor(out, g_tmp[:, at:at + width], cst[0:S, C_H:C_H + width], ALU.pow)

            pool.wait_ge(ld_const, 16)
            for i in range(B):
                pool.wait_ge(var_ready, i + 1)
                norm_factors(small[0:S, 28:29], small[0:S, 27:28], i + 1).then_inc(rstd_ready, 1)
                if i < len(zeroed):
                    t, n = zeroed[i]
                    pool.dma_start(t[rows * n:rows * n + rows, :].rearrange("(r p) d -> p r d", p=S),
                                   zero[:, :, 0:t.shape[-1]]).then_inc(st_zero, 16)
            with pool.Fori(B, 2 * B) as i:
                pool.wait_ge(var_ready, i + 1)
                norm_factors(small[0:S, 28:29], small[0:S, 27:28], i + 1).then_inc(rstd_ready, 1)

            def arrange_weights(n):
                pool.wait_ge(ld_raw, n * 16 * 2)
                alone(pool)
                for k in range(KD):
                    for h in range(2):
                        for p in range(2):
                            src = raw[:, k, 0:NH * HD].rearrange("x (p j i h d) -> x p h i j d", p=2, j=2, i=4, h=2)[:, p, h]
                            dst = wqk_s[:, k, 2 + 4 * p:6 + 4 * p, :].rearrange("x i (h j d) -> x h i j d", h=2, j=2)[:, h]
                            pool.tensor_copy(dst, src)
                        src = raw[:, k, NH * HD:(NH + NKV) * HD].rearrange("x (p j h d) -> x h p j d", p=2, j=2, h=2)[:, h]
                        dst = wqk_s[:, k, 0:2, :].rearrange("x p (h j d) -> x h p j d", h=2, j=2)[:, h]
                        last = pool.tensor_copy(dst, src)
                last.then_inc(aw_ready, 1)

            def gather(l, b):
                if b >= 2:
                    pool.wait_ge(d_yr, l * B + b - 1)
                alone(pool)
                for k in range(TOPK):
                    pool.indirect_dma_start(
                        out=y_in[:, b % 2, k, :], out_offset=None, in_=sorted_y[b // HALF],
                        in_offset=bass.IndirectOffsetOnAxis(ap=pos[:, b, k:k + 1], axis=0)).then_inc(gathered[b % 2], 16)

            def out_factors(l, h):
                pool.wait_ge(a_sq2, l * B + h * HALF + HALF)
                norm_factors(r2[:, :], ms2[:, h * HALF:h * HALF + HALF], 2 * B + l * 10 + (8, 10)[h], GB).then_inc(g_r2, 1)

            def add_rotated(l, g):
                for n in range(8):
                    pool.wait_ge(d_rope, l * 40 + g * 10 + n + 3)
                    pool.tensor_tensor(qT[:, n, :], qT[:, n, :], rope[n % 2][:, :], ALU.add).then_inc(g_rope, 1)

            def in_factors(l, pair):
                pool.wait_ge(a_sq1, l * B + 2 * pair + 2)
                c = pair % 2 * 2
                norm_factors(r1[:, c:c + 2], ms1[:, c:c + 2], 2 * B + l * 10 + pair + 1 + (pair > 6), c).then_inc(g_r1, 1)

            def attention(l):
                for u in range(2):
                    pool.wait_ge(st_ye[u], l * (8 * NT) + 16)
                gather(l, 0)
                gather(l, 1)
                for g in range(NG):
                    gather(l, 4 * g + 2)
                    in_factors(l, 2 * g)
                    if g == 3:
                        out_factors(l, 0)
                    gather(l, 4 * g + 3)
                    in_factors(l, 2 * g + 1)
                    if g < NG - 1:
                        gather(l, 4 * g + 4)
                        gather(l, 4 * g + 5)
                    add_rotated(l, g)

            def last_gathers():
                for u in range(2):
                    pool.wait_ge(st_ye[u], L * (8 * NT) + 16)
                for b in range(B):
                    gather(L, b)

            arrange_weights(1)

            def move_rows(l):
                for h in range(2):
                    if h == 1:
                        out_factors(l, 1)
                    pool.wait_ge(d_pos, l * 2 + h + 1)
                    alone(pool)
                    for b in range(h * HALF, h * HALF + HALF):
                        for k in range(TOPK):
                            pool.indirect_dma_start(
                                out=sorted_x[h], out_offset=bass.IndirectOffsetOnAxis(ap=pos[:, b, k:k + 1], axis=0),
                                in_=x_sb[:, b, :], in_offset=None).then_inc(scattered[h], 16)

            with pool.Fori(0, L - 1) as l:
                attention(l)
                move_rows(l)
                arrange_weights(l + 2)
            attention(L - 1)
            move_rows(L - 1)
            last_gathers()

        @block.tensor
        def _(pe):
            pe.wait_ge(ld_const, 16)
            pe.wait_ge(c_bf, 4)

            def turn(b, u, n):
                pe.wait_ge(ld_dec[u], n * 16)
                if not (isinstance(b, int) and b == 0):
                    pe.wait_ge(decT_a, b)
                    pe.wait_ge(decT_v, b)
                    pe.wait_ge(encT_ready, b)
                for k in range(KD):
                    for c in range(CB):
                        pe.transpose(ps[:, k, c * CR:c * CR + CR],
                                     dec[u][:, c, :].rearrange("p (m k) -> p k m", k=KD)[:, k], ident[0:CR, 0:CR])
                pe.wait_ge(enc_ready, b + 1)
                for k in range(KD):
                    last = pe.transpose(ps[:, 2, k * S:k * S + S],
                                        enc[u].rearrange("p (m k) -> p k m", k=KD)[:, k], ident[0:S, 0:S])
                last.then_inc(xT_done, 1)

            def similar(b):
                pe.wait_ge(decT_a, b + 1)
                pe.wait_ge(decT_v, b + 1)
                pe.wait_ge(e3_ready, b + 1)
                for k in range(KD):
                    last = pe.matmul(ps[0:S, 3, 0:CTX], e3T[:, k, :], decT[:, k, :], start=(k == 0), stop=(k == KD - 1))
                last.then_inc(sim_done, 1)

            def turn_attn(b):
                pe.wait_ge(attn_ready, b + 1)
                for c in range(CB):
                    last = pe.transpose(ps[0:CR, 4, c * S:c * S + S], attn[:, c * CR:c * CR + CR], ident[0:S, 0:S])
                last.then_inc(aT_done, 1)

            def attend(b, u):
                pe.wait_ge(aT_ready, b + 1)
                for k in range(KD):
                    for c in range(CB):
                        last = pe.matmul(ps[:, 5, k * S:k * S + S],
                                         dec[u][:, c, :].rearrange("p (m k) -> p k m", k=KD)[:, k],
                                         attnT[:, c, :], start=(c == 0), stop=(c == CB - 1))
                last.then_inc(hq_done, 1)

            turn(0, 0, 1)
            similar(0)

            def xpair(i, end):
                b = i * 2
                turn(b + 1, 1, i + 1)
                turn_attn(b)
                similar(b + 1)
                attend(b, 0)
                if not end:
                    turn(b + 2, 0, i + 2)
                turn_attn(b + 1)
                if not end:
                    similar(b + 2)
                attend(b + 1, 1)

            with pe.Fori(0, B // 2 - 1) as i:
                xpair(i, False)
            xpair(B // 2 - 1, True)

            pe.wait_ge(batt_v, 1)
            pe.transpose(ps[0:B, 6, 0:S], small[0:S, 0:B], ident[0:S, 0:S]).then_inc(batt_p, 1)
            pe.wait_ge(batt_v, 3)
            for n in range(4):
                last = pe.matmul(ps[:, n, 0:GN], cst[0:B, C_ONE:C_ONE + 128], battD[:, 4 * n:4 * n + 4, :],
                                 start=True, stop=True)
            last.then_inc(batt_p, 1)
            pe.wait_ge(ld_xw, 16 * 5)
            def project(b, u):
                pe.wait_ge(feat_a, b + 1)
                pe.wait_ge(feat_v, b + 1)
                if not (isinstance(b, int) and b < 2):
                    pe.wait_ge(x_ready, b - 1)
                for c in range(8):
                    last = pe.matmul(ps[0:S, 6 + u, 0:D], feat[u][:, c, :], wqv[:, c, :], start=(c == 0), stop=(c == 7))
                last.then_inc(feat_done, 1)

            for u in range(2):
                project(u, u)
            with pe.Fori(1, B // 2) as i:
                for u in range(2):
                    project(i * 2 + u, u)
            pe.wait_ge(x_ready, B)
            pe.wait_ge(ld_ln, 48)
            pe.sem_inc(moe_done, 1)

            def layer(l):
                def norm_turn(pair):
                    pe.wait_ge(a_xn1, l * B + 2 * pair + 2)
                    for k in range(KD):
                        for u in range(2):
                            last = pe.transpose(ps[:, 6, (2 * k + u) * S:(2 * k + u + 1) * S],
                                                xn1[:, u, :].rearrange("p (m k) -> p k m", k=KD)[:, k], ident[0:S, 0:S])
                    last.then_inc(p_t1, 1)

                def project_group(g):
                    pe.wait_ge(a_t1, l * (B // 2) + 2 * g + 2)
                    if g:
                        pe.wait_ge(a_exp, (l * B + 4 * g) * 2)
                    for bb in range(GB):
                        for k in range(KD):
                            last = pe.matmul(ps[0:S, bb, 0:NKV * HD], xnT[:, k, bb * S:bb * S + S],
                                             wv_s[:, k, :], start=(k == 0), stop=(k == KD - 1))
                        last.then_inc(p_v, 1)
                    for n in range(10):
                        if n < 4:
                            pe.wait_ge(a_v, l * B + 4 * g + n + 1)
                        else:
                            pe.wait_ge(d_rope, l * 40 + g * 10 + n - 3)
                        for k in range(KD):
                            last = pe.matmul(ps[:, n % 4, 0:GN], wqk_s[:, k, n, :], xnT[:, k, :], start=(k == 0), stop=(k == KD - 1))
                        last.then_inc(p_qk, 1)

                def scores(b, p):
                    g, bb = b // 4, b % 4
                    pe.wait_ge(d_rope, l * 40 + g * 10 + 10)
                    pe.wait_ge(g_rope, l * 32 + g * 8 + 8)
                    if bb:
                        pe.wait_ge(a_exp, (l * B + b - 1) * 2 + p + 1)
                    for i in range(4):
                        n, c = 2 * p + i // 2, i % 2 * 2 * S
                        pe.matmul(ps[0:S, n, c:c + 2 * S], ident_b[:, :], causal_b[:, :, :], start=True, stop=False)
                        last = pe.matmul(ps[0:S, n, c:c + 2 * S], qT[:, 4 * p + i, bb * S:bb * S + S],
                                         kz[:, p, :, bb * S:bb * S + S], start=False, stop=True)
                    last.then_inc(p_sc, 1)

                def turn_probs(b, unit):
                    p, j = unit // 2, unit % 2
                    if j == 0:
                        pe.wait_ge(d_norm, (l * B + b) * 2 + p + 1)
                    if unit >= 2:
                        pe.wait_ge(a_pt, l * 64 + b * 4 + unit - 1)
                    for i in range(4):
                        last = pe.transpose(ps[0:S, 4 + unit % 2, i * S:i * S + S],
                                            prob[:, b % 2, p * 8 + i * 2 + j, :], ident[0:S, 0:S])
                    last.then_inc(p_pt, 1)

                def weigh(b, unit):
                    p, j = unit // 2, unit % 2
                    pe.wait_ge(a_pt, l * 64 + b * 4 + unit + 1)
                    if unit == 0 and b:
                        pe.wait_ge(d_wo, l * B + b)
                    if unit == 0 and b < B - GB and b % 4 > 1:
                        pe.wait_ge(a_t1, l * (B // 2) + 2 * (b // 4) + 1 + b % 4)
                    if unit == 2 and b > 1:
                        pe.wait_ge(d_lg, l * B + b - 1)
                    last = pe.matmul(ps[64 * j:64 * j + 64, 6 + p, 0:GN], v_s[:, VALUES[b], unit * HD:unit * HD + HD],
                                     probT[:, unit, :], start=True, stop=True)
                    if j == 1:
                        last.then_inc((p_ot0, p_ot1)[p], 1)

                def turn_x(b):
                    pe.wait_ge(d_wo, l * B + b + 1)
                    for k in range(KD):
                        last = pe.transpose(ps[:, 5, k * S:k * S + S],
                                            x_sb[:, b, 0:D].rearrange("p (m k) -> p k m", k=KD)[:, k], ident[0:S, 0:S])
                    last.then_inc(p_t2, 1)

                def route_logits(b):
                    pe.wait_ge(a_t2, l * B + b + 1)
                    for k in range(KD):
                        last = pe.matmul(ps[0:S, 7, 0:E], x2T[:, k, :], wr_l[:, k, :],
                                         start=(k == 0), stop=(k == KD - 1))
                    last.then_inc(p_lg, 1)

                def out_project(b):
                    pe.wait_ge(a_ot, l * B + b + 1)
                    for i in range(4):
                        pe.matmul(ps[0:S, 6, 0:D], oT[:, 0, i * S:i * S + S], wo_s[:, i, :], start=(i == 0), stop=False)
                    pe.wait_ge(d_ot, l * B + b + 1)
                    for i in range(4):
                        last = pe.matmul(ps[0:S, 6, 0:D], oT[:, 1, i * S:i * S + S], wo_s[:, 4 + i, :],
                                         start=False, stop=(i == 3))
                    last.then_inc(p_wo, 1)

                def count_rows(h):
                    pe.wait_ge(d_oh, l * 2 + h + 1)
                    flat = oh_b[:, :, :].rearrange("p a e -> p (a e)")
                    pe.matmul(ps[0:S, 7, 128:256], low_b[:, :], flat, start=True, stop=True)
                    pe.matmul(ps[0:S, 7, 256:384], ones_b[:, :], flat, start=True, stop=True).then_inc(p_rt, 1)

                wr_l = small_wr
                for pair_ in range(GB // 2):
                    norm_turn(pair_)
                    pe.wait_ge(a_t1, l * (B // 2) + pair_ + 1)
                pe.wait_ge(ld_aw, (l + 1) * 16 * 5)
                pe.wait_ge(aw_ready, l + 1)
                project_group(0)
                scores(0, 0)
                scores(0, 1)
                for g in range(NG):
                    for bb in range(GB):
                        b = g * 4 + bb
                        if bb == 3 and g < NG - 1:
                            project_group(g + 1)
                        elif bb < 3:
                            scores(b + 1, 0)
                        turn_probs(b, 0)
                        turn_probs(b, 1)
                        if bb < 3:
                            scores(b + 1, 1)
                        weigh(b, 0)
                        turn_probs(b, 2)
                        weigh(b, 1)
                        turn_probs(b, 3)
                        if bb == 3 and g < NG - 1:
                            scores(b + 1, 0)
                            scores(b + 1, 1)
                        weigh(b, 2)
                        weigh(b, 3)
                        if b:
                            turn_x(b - 1)
                        out_project(b)
                        if b:
                            route_logits(b - 1)
                        if g < NG - 1:
                            for nb in TURN[bb]:
                                pe.wait_ge(d_wo, l * B + b + 1)
                                norm_turn(2 * g + 2 + nb)
                        if b == 10:
                            pe.wait_ge(d_lg, l * B + b)
                            count_rows(0)
                            pe.wait_ge(d_rt, l * 2 + 1)
                turn_x(B - 1)
                pe.wait_ge(d_lg, l * B + B - 1)
                route_logits(B - 1)
                pe.wait_ge(d_lg, l * B + B)
                count_rows(1)
                pe.wait_ge(d_rt, l * 2 + 2)

                pe.wait_ge(ld_mw, (l + 1) * 16 * 3 * E)

                def turn_tile(T, u, n):
                    pe.wait_ge(ld_xe[u], l * (8 * NT) + n * 16)
                    if not (isinstance(T, int) and T == 0):
                        pe.wait_ge(m_xT, l * NT + T)
                    for k in range(KD):
                        last = pe.transpose(ps[:, 5, k * SLOT:k * SLOT + SLOT],
                                            xe[u][:, 0:D].rearrange("p (m k) -> p k m", k=KD)[:, k], ident)
                    last.then_inc(m_tx, 1)

                def up(T, u, e, w, bank, done):
                    for k in range(KD):
                        last = pe.matmul(ps[:, bank, :], xeT[u][:, k, :], w[:, bass.ds(e * 1024 + k * 512, 512)],
                                         start=(k == 0), stop=(k == KD - 1))
                    last.then_inc(done, 1)

                def turn_hidden(T, u):
                    pe.wait_ge(m_h, l * NT + T + 1)
                    if not (isinstance(T, int) and T == 0):
                        pe.wait_ge(m_hT, l * NT + T)
                    for c in range(4):
                        last = pe.transpose(ps[:, 4, c * SLOT:c * SLOT + SLOT],
                                            hid[u].rearrange("p (m c) -> p c m", c=4)[:, c], ident)
                    last.then_inc(m_th, 1)

                def down(T, u, e):
                    pe.wait_ge(m_hT, l * NT + T + 1)
                    if not (isinstance(T, int) and T == 0):
                        pe.wait_ge(m_y, l * NT + T)
                    for c in range(4):
                        last = pe.matmul(ps[:, 6 + u, 0:D], hidT[:, c, :], wd_s[:, bass.ds(e * 1024 + c * D, D)],
                                         start=(c == 0), stop=(c == 3))
                    last.then_inc(m_dn, 1)

                def expert_of(T):
                    return pe.value_load(tile_e[0:1, bass.ds(T, 1)], min_val=0, max_val=E - 1)

                def pair(i, first=False, end=False):
                    for u in range(2):
                        T = i * 2 + u
                        e = expert_of(T)
                        pe.wait_ge(m_xT, l * NT + T + 1)
                        if not first:
                            pe.wait_ge(m_h, l * NT + T - 1)
                        up(T, u, e, wg_s, 2 * u, m_g)
                        if not (first and u == 0):
                            turn_hidden(T - 1, 1 - u)
                        up(T, u, e, wu_s, 2 * u + 1, m_u)
                        if not (end and u == 1):
                            turn_tile(T + 1, 1 - u, i + 1 + u)
                        if not (first and u == 0):
                            down(T - 1, 1 - u, expert_of(T - 1))

                turn_tile(0, 0, 1)
                pair(0, first=True)
                with pe.Fori(1, NT // 2 - 1) as i:
                    pair(i)
                pair(NT // 2 - 1, end=True)
                turn_hidden(NT - 1, 1)
                down(NT - 1, 1, expert_of(NT - 1))
                pe.wait_ge(m_y, (l + 1) * NT)
                pe.sem_inc(moe_done, 1)

            with pe.Fori(0, L) as l:
                small_wr = wr_s[:, bass.ds(l, 1), :, :].rearrange("p a k e -> p (a k) e")
                layer(l)

        @block.scalar
        def _(act):
            act.wait_ge(ld_const, 16)
            act.activation(ident_b[:, :], cst[0:S, C_ID:C_ID + S], ACT.Copy).then_inc(c_bf, 1)
            act.activation(causal_b[:, :, :], bc(cst[0:S, C_CAUSAL:C_CAUSAL + S], 1, [S, 2, S]), ACT.Copy).then_inc(c_bf, 1)
            act.activation(low_b[:, :], cst[0:S, C_LOW:C_LOW + S], ACT.Copy).then_inc(c_bf, 1)
            act.activation(ones_b[:, :], cst[0:S, C_ONE:C_ONE + S], ACT.Copy).then_inc(c_bf, 1)

            def copy_turned(b):
                act.wait_ge(xT_done, b + 1)
                act.activation(decT[:, 0, :], ps[:, 0, 0:CTX], ACT.Copy).then_inc(decT_a, 1)
                act.activation(encT[:, :, bass.ds(b * S, S)], ps[:, 2, 0:KD * S].rearrange("p (k i) -> p k i", k=KD),
                               ACT.Copy).then_inc(encT_ready, 1)

            def exponents(b):
                act.wait_ge(max_ready, b + 1)
                act.activation(attn[:, 0:CTX], ps[0:S, 3, 0:CTX], ACT.Exp, bias=small[0:S, 33:34],
                               accum_out=small[0:S, 34:35]).then_inc(exp_done, 1)

            def copy_attn(b):
                act.wait_ge(aT_done, b + 1)
                act.activation(attnT, ps[0:CR, 4, 0:CB * S].rearrange("p (c i) -> p c i", c=CB), ACT.Copy).then_inc(aT_ready, 1)

            copy_turned(0)
            exponents(0)

            def xstep(b):
                copy_turned(b + 1)
                copy_attn(b)
                exponents(b + 1)

            with act.Fori(0, B - 1) as b:
                xstep(b)
            copy_attn(B - 1)

            act.wait_ge(batt_v, 2)
            act.activation(battD[:, 0, :], ps[0:B, 6, 0:S], ACT.Exp, bias=small[0:B, 41:42],
                           accum_out=small[0:B, 42:43]).then_inc(batt_a, 1)

            def features(b, u):
                if isinstance(b, int) and b < 2:
                    act.wait_ge(hq_ready, B)
                else:
                    act.wait_ge(feat_done, b - 1)
                act.activation(feat[u][:, 0:2, :], encT[:, :, bass.ds(b * S, S)], ACT.Copy)
                act.activation(feat[u][:, 2:4, :], hqT[:, :, bass.ds(b * S, S)], ACT.Copy).then_inc(feat_a, 1)

            for u in range(2):
                features(u, u)
            with act.Fori(1, B // 2) as i:
                for u in range(2):
                    features(i * 2 + u, u)
            act.wait_ge(ld_ln, 48)

            def layer(l):
                def square_in(b):
                    act.wait_ge(d_x, l * B + b + 1)
                    if b:
                        act.wait_ge(a_sq1, l * B + b)
                    act.activation(xsq[:, 0, :], x_sb[:, b, 0:D], ACT.Square, scale=1.0 / 16,
                                   accum_out=ms1[:, b % 4:b % 4 + 1]).then_inc(a_sq1, 1)

                def norm_in(pair):
                    act.wait_ge(g_r1, l * (B // 2) + pair + 1)
                    for u in range(2):
                        b = 2 * pair + u
                        act.activation(xn1[:, u, :], x_sb[:, b, 0:D], ACT.Copy, scale=r1[:, b % 4:b % 4 + 1]).then_inc(a_xn1, 1)

                def copy_in(pair):
                    act.wait_ge(p_t1, l * (B // 2) + pair + 1)
                    alone(act)
                    c = pair % 2 * 2 * S
                    for k in range(KD):
                        last = act.activation(xnT[:, k, c:c + 2 * S], ps[:, 6, k * 2 * S:(k + 1) * 2 * S],
                                              ACT.Copy, scale=ln1T[:, bass.ds(l, 1), k])
                    last.then_inc(a_t1, 1)

                def copy_values(g):
                    for bb in range(GB):
                        act.wait_ge(p_v, l * B + 4 * g + bb + 1)
                        act.activation(v_s[:, VALUES[4 * g + bb], :], ps[0:S, bb, 0:NKV * HD], ACT.Copy).then_inc(a_v, 1)

                def exponents(b, p):
                    act.wait_ge(d_max, (l * B + b) * 2 + p + 1)
                    for n in range(8 * p, 8 * p + 8):
                        bank, h = n // 4, n % 4
                        last = act.activation(prob[:, b % 2, n, :], ps[0:S, bank, h * S:h * S + S], ACT.Exp,
                                              bias=nmax[:, b % 2, n:n + 1], scale=SCALE, accum_out=rsum[:, b % 2, n:n + 1])
                    last.then_inc(a_exp, 1)

                def copy_probs(b, unit):
                    act.wait_ge(p_pt, l * 64 + b * 4 + unit + 1)
                    act.activation(probT[:, unit, :], ps[0:S, 4 + unit % 2, 0:GN], ACT.Copy).then_inc(a_pt, 1)

                def copy_outputs(b):
                    act.wait_ge(p_ot0, l * B + b + 1)
                    act.activation(oT[:, 0, :], ps[:, 6, 0:GN], ACT.Copy).then_inc(a_ot, 1)

                def square_out(b):
                    act.wait_ge(d_wo, l * B + b + 1)
                    if b:
                        act.wait_ge(a_sq2, l * B + b)
                    act.activation(xsq[:, 1, :], x_sb[:, b, 0:D], ACT.Square, scale=1.0 / 16,
                                   accum_out=ms2[:, b:b + 1]).then_inc(a_sq2, 1)

                def copy_out(b):
                    act.wait_ge(p_t2, l * B + b + 1)
                    alone(act)
                    for k in range(KD):
                        last = act.activation(x2T[:, k, :], ps[:, 5, k * S:k * S + S], ACT.Copy,
                                              scale=ln2T[:, bass.ds(l, 1), k])
                    last.then_inc(a_t2, 1)

                def gate_exponents(h):
                    act.wait_ge(d_oh, l * 2 + h + 1)
                    act.activation(gate[:, 1, :], gate[:, 0, :], ACT.Exp).then_inc(a_rt, 1)

                for b in range(GB):
                    square_in(b)
                for n in range(GB // 2):
                    norm_in(n)
                    copy_in(n)
                copy_values(0)
                exponents(0, 0)
                exponents(0, 1)
                for g in range(NG):
                    for bb in range(GB):
                        b = g * 4 + bb
                        if bb == 3 and g < NG - 1:
                            copy_values(g + 1)
                        copy_probs(b, 0)
                        copy_probs(b, 1)
                        if b < B - 1 and bb < 3:
                            exponents(b + 1, 0)
                        copy_probs(b, 2)
                        copy_probs(b, 3)
                        copy_outputs(b)
                        if b < B - 1 and bb == 3:
                            exponents(b + 1, 0)
                        if b < B - 1:
                            exponents(b + 1, 1)
                        if b:
                            copy_out(b - 1)
                        if g < NG - 1:
                            for nb in PREP[bb]:
                                square_in(4 * g + 4 + nb)
                            for nb in TURN[bb]:
                                norm_in(2 * g + 2 + nb)
                                copy_in(2 * g + 2 + nb)
                        square_out(b)
                        if b == 9:
                            gate_exponents(0)
                copy_out(B - 1)
                gate_exponents(1)

                def copy_tile(T, u):
                    act.wait_ge(m_tx, l * NT + T + 1)
                    alone(act)
                    for k in range(KD):
                        last = act.activation(xeT[u][:, k, :], ps[:, 5, k * SLOT:k * SLOT + SLOT], ACT.Copy,
                                              scale=ln2T[:, bass.ds(l, 1), k])
                    last.then_inc(m_xT, 1)

                def tanh(T, u):
                    act.wait_ge(m_g, l * NT + T + 1)
                    act.wait_ge(m_r, l * NT + T + 1)
                    if not (isinstance(T, int) and T == 0):
                        act.wait_ge(m_h, l * NT + T)
                    act.activation(th, ps[:, 2 * u, :], ACT.Tanh, scale=er[:, u, 0:1]).then_inc(m_tanh, 1)

                def copy_hidden(T):
                    act.wait_ge(m_th, l * NT + T + 1)
                    if not (isinstance(T, int) and T == 0):
                        act.wait_ge(m_dn, l * NT + T)
                    act.activation(hidT, ps[:, 4, :].rearrange("p (c t) -> p c t", c=4), ACT.Copy).then_inc(m_hT, 1)

                def pair(i, first=False, end=False):
                    for u in range(2):
                        T = i * 2 + u
                        tanh(T, u)
                        if not (first and u == 0):
                            copy_hidden(T - 1)
                        if not (end and u == 1):
                            copy_tile(T + 1, 1 - u)

                copy_tile(0, 0)
                pair(0, first=True)
                with act.Fori(1, NT // 2 - 1) as i:
                    pair(i)
                pair(NT // 2 - 1, end=True)
                copy_hidden(NT - 1)

            with act.Fori(0, L) as l:
                layer(l)

        @block.vector
        def _(dve):
            dve.wait_ge(ld_x, 16)
            dve.wait_ge(ld_xw, 16 * 5)

            def normed(step, src, dst, n, done):
                alone(dve)
                step(dve.bn_stats(small[0:S, 20:26], src))
                alone(dve)
                step(dve.bn_aggr(small[0:S, 26:28], small[0:S, 20:26]))
                dve.sem_inc(var_ready, 1)
                dve.wait_ge(rstd_ready, n)
                dve.tensor_scalar(dst, src, small[0:S, 26:27], small[0:S, 28:29],
                                  ALU.subtract, ALU.mult).then_inc(done, 1)

            def xrow(b):
                return x_sb[:, bass.ds(b, 1), 0:D].rearrange("p a d -> p (a d)")

            def encode(b, u, base):
                step = Steps(dve, dx, base)
                normed(step, xrow(b), enc[u], b + 1, enc_ready)
                dve.wait_ge(enc_ready, b + 1)
                step(dve.scalar_tensor_tensor(out=scratch, in0=enc[u], scalar=1.0, in1=w1row, op0=ALU.mult, op1=ALU.mult,
                                              accum_out=simrow[:, bass.ds(b, 1)]))
                assert step.n == 3

            def copy_turned(b):
                dve.wait_ge(xT_done, b + 1)
                dve.tensor_copy(decT[:, 1, :], ps[:, 1, 0:CTX]).then_inc(decT_v, 1)
                dve.wait_ge(encT_ready, b + 1)
                for k in range(KD):
                    last = dve.tensor_scalar(e3T[:, k, :], encT[:, k, bass.ds(b * S, S)], wsT[:, 2, k:k + 1],
                                             wsT[:, 1, k:k + 1], ALU.mult, ALU.add)
                last.then_inc(e3_ready, 1)

            def row_max(b, base):
                step = Steps(dve, dx, base)
                dve.wait_ge(sim_done, b + 1)
                step(dve.tensor_reduce(small[0:S, 32:33], ps[0:S, 3, 0:CTX], AX_X, ALU.max))
                dve.tensor_scalar(small[0:S, 33:34], small[0:S, 32:33], -1.0, None, ALU.mult).then_inc(max_ready, 1)
                step(dve.scalar_tensor_tensor(out=simmax[:, bass.ds(b, 1)], in0=small[0:S, 32:33], scalar=bsim[:, :],
                                              in1=simrow[:, bass.ds(b, 1)], op0=ALU.add, op1=ALU.add))
                assert step.n == 2

            def scale_attn(b, base):
                step = Steps(dve, dx, base)
                dve.wait_ge(exp_done, b + 1)
                step(dve.reciprocal(small[0:S, 35:36], small[0:S, 34:35]))
                dve.tensor_scalar(attn[:, 0:CTX], attn[:, 0:CTX], small[0:S, 35:36], None, ALU.mult).then_inc(attn_ready, 1)

            def copy_hq(b):
                dve.wait_ge(hq_done, b + 1)
                dve.tensor_copy(hqT[:, :, bass.ds(b * S, S)],
                                ps[:, 5, 0:KD * S].rearrange("p (k i) -> p k i", k=KD)).then_inc(hq_ready, 1)

            simmax = small[0:S, 0:B]
            encode(0, 0, 0)
            copy_turned(0)
            encode(1, 1, 3)
            row_max(0, 6)
            scale_attn(0, 8)

            def xstep(b, u, base, more):
                copy_turned(b + 1)
                n = 0
                if more:
                    encode(b + 2, u, base)
                    n = 3
                row_max(b + 1, base + n)
                copy_hq(b)
                scale_attn(b + 1, base + n + 2)

            with dve.Fori(0, B // 2 - 1) as i:
                for u in range(2):
                    xstep(i * 2 + u, u, i * 12 + 9 + 6 * u, True)
            base = 9 + 12 * (B // 2 - 1)
            xstep(B - 2, 0, base, False)
            copy_hq(B - 1)
            step = Steps(dve, dx, base + 3)
            dve.sem_inc(batt_v, 1)
            dve.wait_ge(batt_p, 1)
            step(dve.tensor_reduce(small[0:B, 40:41], ps[0:B, 6, 0:S], AX_X, ALU.max))
            step(dve.tensor_scalar(small[0:B, 41:42], small[0:B, 40:41], -1.0, None, ALU.mult))
            dve.sem_inc(batt_v, 1)
            dve.wait_ge(batt_a, 1)
            step(dve.reciprocal(small[0:B, 43:44], small[0:B, 42:43]))
            step(dve.tensor_scalar(batt, battD[:, 0, :], small[0:B, 43:44], None, ALU.mult))
            step(dve.tensor_tensor(battD, bc(cst[0:B, C_ID:C_ID + B], 2, [B, B, S]), bc(batt, 1, [B, B, S]), ALU.mult))
            dve.sem_inc(batt_v, 1)
            dve.wait_ge(batt_p, 2)
            for k in range(KD):
                for n in range(4):
                    ins = dve.tensor_tensor(prodT[:, 4 * n:4 * n + 4, :],
                                            encT[:, k, n * GN:n * GN + GN].rearrange("p (b i) -> p b i", b=4),
                                            ps[:, n, 0:GN].rearrange("p (b i) -> p b i", b=4), ALU.mult)
                step(ins)
                step(dve.tensor_reduce(hcT[:, k, :], prodT, AX_X, ALU.add))
            base = base + 3 + step.n

            def features(b, u, base):
                step = Steps(dve, dx, base)
                if not (isinstance(b, int) and b < 2):
                    dve.wait_ge(feat_done, b - 1)
                e = encT[:, :, bass.ds(b * S, S)]
                dve.tensor_tensor(feat[u][:, 4:6, :], e, hqT[:, :, bass.ds(b * S, S)], ALU.mult)
                for k in range(KD):
                    last = dve.tensor_scalar(feat[u][:, 6 + k, :], encT[:, k, bass.ds(b * S, S)],
                                             hcT[:, k, bass.ds(b, 1)], None, ALU.mult)
                last.then_inc(feat_v, 1)

            def finish_x(b, u, base):
                step = Steps(dve, dx, base)
                r = res[:, bass.ds(b, 1), :].rearrange("p a d -> p (a d)")
                dve.wait_ge(feat_done, b + 1)
                step(dve.tensor_tensor(r, ps[0:S, 6 + u, 0:D], bqv, ALU.add))
                step(dve.tensor_tensor(r, r, xrow(b), ALU.add))
                normed(step, r, xrow(b), b + B + 1, x_ready)
                assert step.n == 4

            features(0, 0, 0)
            features(1, 1, 0)
            with dve.Fori(0, B // 2 - 1) as i:
                for u in range(2):
                    finish_x(i * 2 + u, u, i * 8 + 4 * u + base)
                    features(i * 2 + u + 2, u, 0)
            base += 8 * (B // 2 - 1)
            finish_x(B - 2, 0, base)
            finish_x(B - 1, 1, base + 4)
            dve.wait_ge(z_ready, 4)
            dve.wait_ge(x_ready, B)

            def combine(step, l, b):
                dve.wait_ge(gathered[b % 2], l * (16 * TOPK * B // 2) + (b // 2 + 1) * 16 * TOPK)
                step(dve.tensor_scalar(mix_b, y_in[:, b % 2, 0, :], wts[:, b, 0:1], None, ALU.mult))
                ins = dve.scalar_tensor_tensor(out=mix_b, in0=y_in[:, b % 2, 1, :], scalar=wts[:, b, 1:2], in1=mix_b,
                                               op0=ALU.mult, op1=ALU.add)
                ins.then_inc(d_yr, 1)
                dve.wait_ge(d_yr, l * B + b + 1)
                step(dve.tensor_tensor(x_sb[:, b, 0:D], x_sb[:, b, 0:D], mix_b, ALU.add))

            def layer(l):
                step = Steps(dve, dv, l * DVE_LAYER)

                def rows_in(b):
                    combine(step, l, b)
                    dve.tensor_scalar(x_sb[:, b, 0:D], x_sb[:, b, 0:D], CLIP, -CLIP, ALU.min, ALU.max).then_inc(d_x, 1)

                def rotate(g):
                    for n in range(10):
                        dve.wait_ge(p_qk, l * 40 + g * 10 + n + 1)
                        out_c = kz[:, n, 0, :] if n < 2 else qT[:, n - 2, :]
                        src = ps[:, n % 4, 0:GN].rearrange("p (b t) -> p b t", b=GB)
                        s = rope[n % 2][:, :].rearrange("p (b t) -> p b t", b=GB)
                        dve.tensor_tensor(out_c.rearrange("p (b t) -> p b t", b=GB), src,
                                          bc(cst[:, C_COS:C_COS + S], 1, [128, GB, S]), ALU.mult)
                        if n > 3:
                            dve.wait_ge(g_rope, l * 32 + g * 8 + n - 3)
                        for a, z in ((0, 64), (64, 0)):
                            ins = dve.tensor_tensor(s[a:a + 64], src[z:z + 64],
                                                    bc(cst[a:a + 64, C_SIN:C_SIN + S], 1, [64, GB, S]), ALU.mult)
                        if n < 2:
                            step(ins)
                            step(dve.tensor_tensor(out_c, out_c, rope[n % 2][:, :], ALU.add))
                            step(dve.tensor_scalar(kz[:, n, 1, :], out_c, cst[:, C_J + 1:C_J + 2], None, ALU.mult))
                            ins = dve.tensor_scalar(out_c, out_c, cst[:, C_J:C_J + 1], None, ALU.mult)
                        ins.then_inc(d_rope, 1)

                def maxima(b, p):
                    dve.wait_ge(p_sc, (l * B + b) * 2 + p + 1)
                    hs = slice(8 * p, 8 * p + 8)
                    step(dve.tensor_reduce(rmax[:, hs].rearrange("p (n h) -> p n h", n=2), heads(p), AX_X, ALU.max))
                    dve.tensor_scalar(nmax[:, b % 2, hs], rmax[:, hs], -SCALE, None, ALU.mult).then_inc(d_max, 1)

                def scale_probs(b, p):
                    dve.wait_ge(a_exp, (l * B + b) * 2 + p + 1)
                    hs = slice(8 * p, 8 * p + 8)
                    step(dve.reciprocal(rrec[:, hs], rsum[:, b % 2, hs]))
                    dve.tensor_tensor(prob[:, b % 2, hs, :], prob[:, b % 2, hs, :], bc(rrec[:, hs], 2, [S, 8, S]),
                                      ALU.mult).then_inc(d_norm, 1)

                def copy_outputs(b):
                    dve.wait_ge(p_ot1, l * B + b + 1)
                    dve.tensor_copy(oT[:, 1, :], ps[:, 7, 0:GN]).then_inc(d_ot, 1)

                def add_attention(b):
                    dve.wait_ge(p_wo, l * B + b + 1)
                    step(dve.tensor_tensor(x_sb[:, b, 0:D], ps[0:S, 6, 0:D], x_sb[:, b, 0:D], ALU.add))
                    dve.tensor_scalar(x_sb[:, b, 0:D], x_sb[:, b, 0:D], CLIP, -CLIP, ALU.min, ALU.max).then_inc(d_wo, 1)

                def logits(b):
                    dve.wait_ge(p_lg, l * B + b + 1)
                    dve.tensor_copy(lg[:, b, :], ps[0:S, 7, 0:E]).then_inc(d_lg, 1)

                def choose(h):
                    dve.wait_ge(d_lg, l * B + h * HALF + HALF)
                    dve.wait_ge(g_r2, l * 2 + h + 1)
                    hs = slice(h * HALF, h * HALF + HALF)
                    dve.tensor_tensor(lg[:, hs, :], lg[:, hs, :], bc(r2[:, :], 2, [S, HALF, E]), ALU.mult)
                    dve.tensor_copy(x_sb[:, hs, D], r2[:, :])
                    step(dve.tensor_scalar(x_sb[:, hs, D + 1], r2[:, :], 0.5, None, ALU.mult))
                    step(dve.tensor_tensor(x_sb[:, hs, D + 2], r2[:, :], x_sb[:, hs, D + 1], ALU.mult))
                    alone(dve)
                    for b in range(HALF):
                        ins = dve.max(top[:, b, :], lg[:, h * HALF + b, :])
                    step(ins)
                    alone(dve)
                    for b in range(HALF):
                        ins = dve.max_index(idx[:, b, :], top[:, b, :], lg[:, h * HALF + b, :])
                    step(ins)
                    step(dve.tensor_copy(idxf[:, :, :], idx[:, :, 0:TOPK]))
                    N = HALF * TOPK
                    step(dve.tensor_tensor(oh[:, :, :], bc(idxf[:, :, :].rearrange("p b k -> p (b k)"), 2, [S, N, E]),
                                           bc(cst[0:S, C_E:C_E + E], 1, [S, N, E]), ALU.is_equal))
                    step(dve.tensor_tensor(gate[:, 0, :], top[:, :, 1], top[:, :, 0], ALU.subtract))
                    dve.tensor_copy(oh_b[:, :, :], oh[:, :, :]).then_inc(d_oh, 1)

                def place(h):
                    N = HALF * TOPK
                    dve.wait_ge(p_rt, l * 2 + h + 1)
                    before = ps[0:S, 7, 128:256].rearrange("p (a e) -> p a e", e=E)
                    total = ps[0:S, 7, 256:384].rearrange("p (a e) -> p a e", e=E)
                    step(dve.tensor_copy(pre[0][:, :, :], total))
                    a = 0
                    for s in (1, 2, 4, 8):
                        dve.tensor_copy(pre[1 - a][:, 0:s, :], pre[a][:, 0:s, :])
                        step(dve.tensor_tensor(pre[1 - a][:, s:N, :], pre[a][:, s:N, :], pre[a][:, 0:N - s, :], ALU.add))
                        a = 1 - a
                    step(dve.tensor_tensor(cnt[:, :, :], bc(pre[a][:, N - 1, :], 2, [S, E, EPT]),
                                           bc(cst[0:S, C_M:C_M + EPT], 1, [S, E, EPT]), ALU.is_gt))
                    step(dve.tensor_reduce(tiles[:, :], cnt[:, :, :], AX_X, ALU.add))
                    step(dve.tensor_copy(cum[0][:, :], tiles[:, :]))
                    c = 0
                    for s in (1, 2, 4):
                        dve.tensor_copy(cum[1 - c][:, 0:s], cum[c][:, 0:s])
                        step(dve.tensor_tensor(cum[1 - c][:, s:E], cum[c][:, s:E], cum[c][:, 0:E - s], ALU.add))
                        c = 1 - c
                    step(dve.tensor_tensor(tef[:, :, :], bc(cum[c][0:1, :], 1, [1, HT, E]),
                                           bc(cst[0:1, C_T:C_T + HT], 2, [1, HT, E]), ALU.is_le))
                    step(dve.tensor_reduce(tes[:, :], tef[:, :, :], AX_X, ALU.add))
                    step(dve.tensor_scalar(tile_e[:, h * HT:h * HT + HT], tes[:, :], float(E - 1), None, ALU.min))
                    step(dve.tensor_tensor(tiles[:, :], cum[c][:, :], tiles[:, :], ALU.subtract))
                    step(dve.tensor_tensor(pre[a][:, :, :], pre[a][:, :, :], total, ALU.subtract))
                    step(dve.scalar_tensor_tensor(out=pre[a][:, :, :], in0=bc(tiles[:, :], 1, [S, N, E]), scalar=float(SLOT),
                                                  in1=pre[a][:, :, :], op0=ALU.mult, op1=ALU.add))
                    step(dve.tensor_tensor(pre[a][:, :, :], before, pre[a][:, :, :], ALU.add))
                    dve.sem_inc(d_rt, 1)
                    step(dve.tensor_tensor(pre[a][:, :, :], pre[a][:, :, :], oh[:, :, :], ALU.mult))
                    step(dve.tensor_reduce(posf[:, :], pre[a][:, :, :], AX_X, ALU.add))
                    hs = slice(h * HALF, h * HALF + HALF)
                    dve.tensor_copy(pos[:, hs, :].rearrange("p b k -> p (b k)"), posf[:, :]).then_inc(d_pos, 1)
                    dve.wait_ge(a_rt, l * 2 + h + 1)
                    step(dve.tensor_scalar(gate[:, 0, :], gate[:, 1, :], 1.0, None, ALU.add))
                    step(dve.reciprocal(wts[:, hs, 0], gate[:, 0, :]))
                    step(dve.tensor_tensor(wts[:, hs, 1], wts[:, hs, 0], gate[:, 1, :], ALU.mult))

                for b in range(GB):
                    rows_in(b)
                rotate(0)
                for p in range(2):
                    maxima(0, p)
                for p in range(2):
                    scale_probs(0, p)
                for g in range(NG):
                    for bb in range(GB):
                        b = g * 4 + bb
                        if bb == 3 and g < NG - 1:
                            rotate(g + 1)
                        if b < B - 1:
                            maxima(b + 1, 0)
                            maxima(b + 1, 1)
                        copy_outputs(b)
                        if b < B - 1 and bb < 3:
                            scale_probs(b + 1, 0)
                        add_attention(b)
                        if b < B - 1 and bb == 3:
                            scale_probs(b + 1, 0)
                        if b < B - 1:
                            scale_probs(b + 1, 1)
                        if g < NG - 1:
                            for nb in PREP[bb]:
                                rows_in(4 * g + 4 + nb)
                        if b:
                            logits(b - 1)
                        if b == 8:
                            choose(0)
                        if b == 10:
                            place(0)
                logits(B - 1)
                choose(1)
                place(1)
                assert step.n == DVE_LAYER, step.n

                def copy_factors(T, u):
                    dve.wait_ge(m_tx, l * NT + T + 1)
                    dve.tensor_copy(er[:, u, :], xe[u][:, D + 1:D + 3]).then_inc(m_r, 1)

                def hidden(T, u, base):
                    step = Steps(dve, dm, base)
                    dve.wait_ge(m_tanh, l * NT + T + 1)
                    step(dve.scalar_tensor_tensor(out=th, in0=th, scalar=1.0, in1=ps[:, 2 * u, :], op0=ALU.add, op1=ALU.mult))
                    dve.wait_ge(m_u, l * NT + T + 1)
                    dve.scalar_tensor_tensor(out=hid[u], in0=th, scalar=er[:, u, 1:2], in1=ps[:, 2 * u + 1, :],
                                             op0=ALU.mult, op1=ALU.mult).then_inc(m_h, 1)

                def copy_result(T, u, n):
                    dve.wait_ge(m_dn, l * NT + T + 1)
                    dve.wait_ge(st_ye[u], l * (8 * NT) + n * 16)
                    dve.tensor_copy(ye[u], ps[:, 6 + u, 0:D]).then_inc(m_y, 1)

                mbase = l * NT

                def pair(i, first=False, end=False):
                    for u in range(2):
                        T = i * 2 + u
                        hidden(T, u, mbase + T)
                        if not (end and u == 1):
                            copy_factors(T + 1, 1 - u)
                        if not (first and u == 0):
                            copy_result(T - 1, 1 - u, i + u)

                copy_factors(0, 0)
                pair(0, first=True)
                with dve.Fori(1, NT // 2 - 1) as i:
                    pair(i)
                pair(NT // 2 - 1, end=True)
                copy_result(NT - 1, 1, NT // 2)

            with dve.Fori(0, L) as l:
                layer(l)

            step = Steps(dve, dv, L * DVE_LAYER)
            dve.wait_ge(ld_res, 16)
            for b in range(B):
                combine(step, L, b)
                step(dve.tensor_scalar(x_sb[:, b, 0:D], x_sb[:, b, 0:D], CLIP, -CLIP, ALU.min, ALU.max))
                dve.tensor_tensor(x_sb[:, b, 0:D], x_sb[:, b, 0:D], res[:, b, :], ALU.add).then_inc(d_x, 1)


VALUES = [b % 4 if b % 4 < 3 else 3 + b // 4 % 2 for b in range(B)]

PREP = {0: [0, 1], 1: [2, 3], 2: [], 3: []}
TURN = {0: [], 1: [0], 2: [1], 3: []}

_INS = ["x", "ctx_1024", "L0_xattn_w_sim", "L0_xattn_b_sim", "L0_xattn_W_qv", "L0_xattn_b_qv", "L0_ffn_ln1_w",
        "L0_ffn_ln2_w", "L0_ffn_wq", "L0_ffn_wk", "L0_ffn_wv", "L0_ffn_wo", "L0_ffn_wr", "L0_ffn_wg", "L0_ffn_wu",
        "L0_ffn_wd"]


def kernel(**inputs):
    import numpy as _np
    import concourse.bacc as _bacc
    from concourse import mybir as _mybir
    from concourse.bass_utils import run_bass_kernel_spmd as _run

    nc = _bacc.Bacc("TRN2", target_bir_lowering=False, num_devices=1)
    arrays, args = {}, []
    given = {name: _np.ascontiguousarray(inputs[name]) for name in _INS}
    given["constants"] = constants()
    for name, a in given.items():
        arrays[f"in_{name}_dram"] = a
        args.append(nc.dram_tensor(f"in_{name}_dram", a.shape, _mybir.dt.from_np(a.dtype), kind="ExternalInput").ap())
    args.append(nc.dram_tensor("out_0_dram", (B, S, D), _mybir.dt.float32, kind="ExternalOutput").ap())
    xattn_ffn(nc, *args)
    r = _run(nc, [arrays], core_ids=[0])
    return r.results[0]["out_0_dram"]
```

```python
from contextlib import ExitStack

import concourse.bass as bass
from concourse import mybir

ALU = mybir.AluOpType
ACT = mybir.ActivationFunctionType
AX_X = mybir.AxisListType.X
F32 = mybir.dt.float32
BF16 = mybir.dt.bfloat16
U32 = mybir.dt.uint32
I32 = mybir.dt.int32

B, S, D = 16, 112, 256
CTX = 375
CR = 125
CB = CTX // CR
L, NH, NKV, HD = 4, 16, 4, 64
FF, E, TOPK = 512, 8, 2
KD = D // 128
GB = 4
NG = B // GB
GN = GB * S
SLOT = 128
PARTS = ((0, 10), (10, 16))
PN = max(z - a for a, z in PARTS)
WHOLE = -(-(PARTS[0][1] * S * TOPK - E * (SLOT - 1)) // SLOT)
NT = B * S * TOPK // SLOT + E
FIRST = PARTS[0][1] * S * TOPK // SLOT + E
NK = NT - E
MA = PARTS[0][1] * S // SLOT
MB = ((B - PARTS[0][1]) * S + SLOT - 1) // SLOT
HROWS = NT * SLOT
assert NT % 2 == 0 and WHOLE % 2 == 0
DX = D + 4
EPS = 1e-05
CLIP = 100.0
NEG = -8.0e9
SCALE = float(HD) ** -0.5

C_ID, C_COS, C_SIN, C_LOW, C_ONE = 0, 128, 240, 352, 464
C_E = C_ONE + 128
C_M = C_E + E
C_T = C_M + MA
C_J = C_T + NK
C_CAUSAL = C_J + 2
C_H = C_CAUSAL + S
C_G = C_H + PN
C_TRI = C_G + E
C_END = C_TRI + E * E

DVE_LAYER = 215


def constants():
    import numpy as np

    c = np.zeros((128, C_END), np.float32)
    c[:, C_ID:C_ID + 128] = np.eye(128, dtype=np.float32)
    inv = (1.0 / np.float32(10000.0) ** (np.arange(0, HD, 2, dtype=np.float32) / np.float32(HD))).astype(np.float32)
    angle = (np.arange(S, dtype=np.float32)[:, None] * inv).T
    cos, sin = np.cos(angle).astype(np.float32), np.sin(angle).astype(np.float32)
    for q in range(4):
        c[32 * q:32 * q + 32, C_COS:C_COS + S] = cos
        c[32 * q:32 * q + 32, C_SIN:C_SIN + S] = -sin if q < 2 else sin
        c[32 * q:32 * q + 32, C_J + q % 2] = 1.0
    t = np.arange(S)
    c[0:S, C_LOW:C_LOW + S] = t[:, None] < t[None, :]
    c[:, C_ONE:C_ONE + 128] = 1.0
    c[:, C_E:C_E + E] = np.arange(E)
    c[:, C_M:C_M + MA] = SLOT * (1 + np.arange(MA))
    c[:, C_T:C_T + NK] = np.arange(NK)
    c[:, C_G:C_G + E] = SLOT * (WHOLE + np.arange(E))
    c[:, C_TRI:C_END] = (np.arange(E)[None, :] <= np.arange(E)[:, None]).reshape(-1)
    c[0:S, C_CAUSAL:C_CAUSAL + S] = np.where(t[None, :] > t[:, None], np.float32(NEG), np.float32(0))
    c[:, C_H:C_H + PN] = -0.5
    return c


class Steps:

    def __init__(self, engine, sem, base):
        self.engine, self.sem, self.base, self.n = engine, sem, base, 0

    def __call__(self, instruction):
        self.n += 1
        instruction.then_inc(self.sem, 1)
        self.engine.wait_ge(self.sem, self.base + self.n)


def xattn_ffn(nc, x, ctx_1024, w_sim, b_sim, W_qv, b_qv, ln1_w, ln2_w, wq, wk, wv, wo, wr, wg, wu, wd, const, out):
    with ExitStack() as stack:
        def sb(name, shape, dt=F32):
            return stack.enter_context(nc.sbuf_tensor(name, shape, dt))

        def sem(name):
            return stack.enter_context(nc.semaphore(name))

        sorted_x = nc.dram_tensor("sorted_x", [HROWS, DX], F32, kind="Internal").ap()
        sorted_y = nc.dram_tensor("sorted_y", [HROWS, D], F32, kind="Internal").ap()
        res_d = nc.dram_tensor("res_d", [S, B, D], F32, kind="Internal").ap()

        arena = sb("arena", [128, 3 * E * KD * FF])
        wg_s = arena[:, 0:8192]
        wu_s = arena[:, 8192:16384]
        wd_s = arena[:, 16384:24576]
        at = [0]

        def part(width, p=128):
            at[0] += width
            assert at[0] <= 24576
            return arena[0:p, at[0] - width:at[0]]

        dec = [part(CB * D, CR).rearrange("p (c d) -> p c d", c=CB) for _ in range(2)]
        decT = part(KD * CTX).rearrange("p (k j) -> p k j", k=KD)
        encT = part(KD * B * S).rearrange("p (k n) -> p k n", k=KD)
        hqT = part(KD * B * S).rearrange("p (k n) -> p k n", k=KD)
        e3T = part(KD * S).rearrange("p (k i) -> p k i", k=KD)
        attn = part(CTX + 1, S)
        attnT = part(CB * S, CR).rearrange("p (c i) -> p c i", c=CB)
        wqv = part(8 * D).rearrange("p (c n) -> p c n", c=8)
        dec += [arena[0:CR, at[0] + u * CB * D:at[0] + (u + 1) * CB * D].rearrange("p (c d) -> p c d", c=CB) for u in range(2)]
        feat = [part(8 * S).rearrange("p (c i) -> p c i", c=8) for _ in range(2)]
        res = part(B * D, S).rearrange("p (b d) -> p b d", b=B)
        bqv = part(D, S)
        w1row = part(D, S)
        enc = [part(D, S) for _ in range(2)]
        scratch = part(D, S)
        battD = part(B * S, B).rearrange("p (b i) -> p b i", b=B)
        simrow = part(B, S)
        batt = part(S, B)
        hcT = part(KD * B).rearrange("p (k b) -> p k b", k=KD)
        prodT = part(B * S).rearrange("p (b i) -> p b i", b=B)

        wqk_s = sb("wqk_s", [128, KD, 10, 128])
        wv_s = sb("wv_s", [128, KD, NKV * HD])
        wo_s = sb("wo_s", [128, 8, D])
        x_sb = sb("x_sb", [S, B, DX])
        y_in = sb("y_in", [S, 2, TOPK, D])
        xnT = sb("xnT", [128, KD, GN])
        qarena = sb("qarena", [128, 8 * GN])
        qT = qarena[:, :].rearrange("p (n t) -> p n t", n=8)
        kz = sb("kz", [128, 2, 2, GN])
        xe = [kz[:, 0, u, 0:DX] for u in range(2)]
        xeT = [qarena[:, 512 + 256 * u:768 + 256 * u].rearrange("p (k t) -> p k t", k=KD) for u in range(2)]
        th = qarena[:, 1024:1536]
        hid = [qarena[:, 1536 + 512 * u:2048 + 512 * u] for u in range(2)]
        hidT = qarena[:, 2560:3072].rearrange("p (c t) -> p c t", c=4)
        ye = [qarena[:, 3072 + 256 * u:3328 + 256 * u] for u in range(2)]
        v_s = sb("v_s", [S, GB + 1, NKV * HD])
        parena = sb("parena", [128, 2 * NH * S])
        prob = parena[0:S, :].rearrange("q (u n k) -> q u n k", u=2, n=NH)
        raw = parena[:, 0:KD * (NH + NKV) * HD].rearrange("p (k n) -> p k n", k=KD)
        probT = sb("probT", [S, NKV, GN])
        oT = sb("oT", [128, 2, GN])
        rope = [sb(f"rope{i}", [128, GN]) for i in range(2)]
        xn1 = sb("xn1", [S, 2, D])
        x2T = sb("x2T", [128, KD, S])

        cst = sb("cst", [128, C_END])
        ident = cst[:, C_ID:C_ID + 128]
        ident_b = sb("ident_b", [S, S], BF16)
        causal_b = sb("causal_b", [S, S], BF16)
        low_b = sb("low_b", [S, S], BF16)
        ones_b = sb("ones_b", [S, S], BF16)
        ln1T = sb("ln1T", [128, L + 1, KD])
        ln2T = sb("ln2T", [128, L, KD])
        wr_s = sb("wr_s", [128, L, KD, E])
        wsT = sb("wsT", [128, 3, KD])
        bsim = sb("bsim", [S, 1])
        small = sb("small", [128, 64])
        lg = sb("lg", [S, 2, E])
        top = sb("top", [S, B, 8])
        idx = sb("idx", [S, B, 8], U32)
        at[0] = 0

        def route_part(width):
            at[0] += width
            assert at[0] <= 2 * TOPK * D
            return y_in[:, :, :, :].rearrange("p u k d -> p (u k d)")[:, at[0] - width:at[0]]

        hot_all, jump_all, mask_all = (route_part(PN * TOPK * E) for _ in range(3))
        rank_all = route_part((PN * TOPK + 1) * E)
        idxf_all = route_part(PN * TOPK)
        oh_b = [sb(f"oh_b{h}", [S, (z - a) * TOPK + 2, E], BF16) for h, (a, z) in enumerate(PARTS)]
        cnt = sb("cnt", [S, E, MA])
        tri = sb("tri", [S, E, E])
        ends = sb("ends", [S, 2, E])
        whole, over, first, jump = (sb(n, [S, E]) for n in ("whole", "over", "first", "jump"))
        posf = sb("posf", [S, PN * TOPK])
        posn = sb("posn", [S, PN * TOPK], U32)
        pos = sb("pos", [S, B, TOPK], U32)
        pos_x = sb("pos_x", [S, B, TOPK], U32)
        wts = sb("wts", [S, B, TOPK])
        tef = sb("tef", [1, NK - WHOLE, 2 * E])
        tes = sb("tes", [1, NK - WHOLE])
        tew = sb("tew", [1, NK - WHOLE])
        tile_e = sb("tile_e", [1, NT], I32)

        rmax = sb("rmax", [S, NH])
        nmax = sb("nmax", [S, 2, NH])
        rsum = sb("rsum", [S, 2, NH])
        rrec = sb("rrec", [S, NH])
        gate = sb("gate", [S, 2, PN])
        er = sb("er", [128, 2, 2])
        g_tmp = sb("g_tmp", [S, GB + PN])
        ms1, r1 = sb("ms1", [S, GB]), sb("r1", [S, GB])
        ms2, r2 = sb("ms2", [S, B]), sb("r2", [S, PN])
        xsq = sb("xsq", [S, 2, D], BF16)
        mix_b = rope[0][0:S, 0:D]

        ps = stack.enter_context(nc.psum_tensor("ps", [128, 8, 512], F32))

        ld_const, ld_x, ld_xw, ld_ln = sem("ld_const"), sem("ld_x"), sem("ld_xw"), sem("ld_ln")
        ld_dec = [sem(f"ld_dec{i}") for i in range(4)]
        ld_x0, ld_wq = sem("ld_x0"), sem("ld_wq")
        ld_aw, ld_mw, ld_raw, aw_ready = sem("ld_aw"), sem("ld_mw"), sem("ld_raw"), sem("aw_ready")
        ld_xe = [sem(f"ld_xe{i}") for i in range(2)]
        st_ye = [sem(f"st_ye{i}") for i in range(2)]
        st_res, st_zero, st_out, ld_res = sem("st_res"), sem("st_zero"), sem("st_out"), sem("ld_res")
        gathered = [sem(f"gathered{i}") for i in range(2)]
        scattered = [sem(f"scattered{i}") for i in range(2)]
        c_bf, z_ready = sem("c_bf"), sem("z_ready")
        enc_ready, xT_done, decT_a, decT_v, encT_ready, e3_ready = (sem(n) for n in ("enc_ready", "xT_done", "decT_a", "decT_v", "encT_ready", "e3_ready"))
        sim_done, max_ready, exp_done, attn_ready, aT_done, aT_ready, hq_done, hq_ready = (sem(n) for n in (
            "sim_done", "max_ready", "exp_done", "attn_ready", "aT_done", "aT_ready", "hq_done", "hq_ready"))
        batt_v, batt_a, batt_p = sem("batt_v"), sem("batt_a"), sem("batt_p")
        feat_a, feat_v, feat_done, x_ready = sem("feat_a"), sem("feat_v"), sem("feat_done"), sem("x_ready")
        p_v, p_qk, p_sc, p_pt, p_ot0, p_ot1, p_wo, p_t2, p_lg, p_t1, p_rt = (sem(n) for n in (
            "p_v", "p_qk", "p_sc", "p_pt", "p_ot0", "p_ot1", "p_wo", "p_t2", "p_lg", "p_t1", "p_rt"))
        a_key, d_pt = sem("a_key"), sem("d_pt")
        a_v, a_exp, a_pt, a_ot, a_sq1, a_xn1, a_t1, a_sq2, a_t2, a_rt = (sem(n) for n in (
            "a_v", "a_exp", "a_pt", "a_ot", "a_sq1", "a_xn1", "a_t1", "a_sq2", "a_t2", "a_rt"))
        d_rope, d_max, d_norm, d_ot, d_wo, d_lg, d_x, d_yr, d_oh, d_rt, d_pos, d_te, d_out, d_gate = (sem(n) for n in (
            "d_rope", "d_max", "d_norm", "d_ot", "d_wo", "d_lg", "d_x", "d_yr", "d_oh", "d_rt", "d_pos", "d_te", "d_out", "d_gate"))
        m_tx, m_g, m_u, m_th, m_dn, moe_done = (sem(n) for n in ("m_tx", "m_g", "m_u", "m_th", "m_dn", "moe_done"))
        m_xT, m_tanh, m_hT = (sem(n) for n in ("m_xT", "m_tanh", "m_hT"))
        m_r, m_h, m_y = (sem(n) for n in ("m_r", "m_h", "m_y"))
        dv, dm, dx, passed = sem("dv"), sem("dm"), sem("dx"), sem("passed")
        g_eps, var_ready, rstd_ready, g_r1, g_r2, g_rope = (sem(n) for n in ("g_eps", "var_ready", "rstd_ready", "g_r1", "g_r2", "g_rope"))

        ZP = 96
        zero = probT[0:ZP, :, :].rearrange("p a b -> p (a b)")[:, 0:6 * DX].rearrange("p (r d) -> p r d", r=6)
        rows = ZP * 6
        ZERO_STORES = 2 * (HROWS // rows)
        assert HROWS % rows == 0

        block = stack.enter_context(nc.Block())

        def bc(ap, axis, shape):
            return ap.unsqueeze(axis).to_broadcast(shape)

        def alone(engine):
            engine.sem_inc(passed, 1)

        def heads(p):
            return ps[0:S, 2 * p:2 * p + 2, 0:GN].rearrange("q n (h k) -> q n h k", k=S)

        @block.sync
        def _(sp):
            sp.dma_start(cst[:, :], const).then_inc(ld_const, 16)
            sp.dma_start(x_sb[:, 0:2, 0:D], x[0:2].rearrange("b s d -> s b d")).then_inc(ld_x0, 16)
            sp.dma_start(w1row, w_sim[0:D].rearrange("(a d) -> a d", a=1).to_broadcast([S, D])).then_inc(ld_xw, 16)
            sp.dma_start(wsT[:, :, :], w_sim.rearrange("(g p k) -> p g k", g=3, k=KD)).then_inc(ld_xw, 16)
            sp.dma_start(bsim[:, :], b_sim.rearrange("(a d) -> a d", a=1).to_broadcast([S, 1])).then_inc(ld_xw, 16)

            def load_dec(b, u):
                sp.dma_start(dec[u], ctx_1024[b].rearrange("(c p) d -> p c d", p=CR) if isinstance(b, int) else
                             ctx_1024[bass.ds(b, 1)].rearrange("a (c p) d -> p (a c) d", p=CR)).then_inc(ld_dec[u], 16)

            load_dec(0, 0)
            load_dec(1, 1)
            sp.dma_start(x_sb[:, 2:B, 0:D], x[2:B].rearrange("b s d -> s b d")).then_inc(ld_x, 16)
            load_dec(2, 2)
            load_dec(3, 3)
            sp.dma_start(wqv, W_qv.rearrange("(f p k) n -> p f k n", f=4, k=KD)).then_inc(ld_wq, 16)
            sp.dma_start(bqv, b_qv.rearrange("(a d) -> a d", a=1).to_broadcast([S, D])).then_inc(ld_wq, 16)
            sp.dma_start(ln1T[:, 0:L, :], ln1_w.rearrange("l (p k) -> p l k", k=KD)).then_inc(ld_ln, 16)
            sp.dma_start(ln1T[:, L, :], ln1_w[0].rearrange("(p k) -> p k", k=KD)).then_inc(ld_ln, 16)
            sp.dma_start(ln2T[:, :, :], ln2_w.rearrange("l (p k) -> p l k", k=KD)).then_inc(ld_ln, 16)
            sp.dma_start(wr_s[:, :, :, :], wr.rearrange("l (p k) e -> p l k e", k=KD)).then_inc(ld_ln, 16)
            with sp.Fori(0, B // 4 - 1) as i:
                for u in range(4):
                    sp.wait_ge(hq_done, i * 4 + u + 1)
                    load_dec(i * 4 + u + 4, u)

            def attention_weights(l):
                one = (lambda a: a[l]) if isinstance(l, int) else (lambda a: a[bass.ds(l, 1)].rearrange("a r c -> (a r) c"))
                for w, c0, c1 in ((wq, 0, NH * HD), (wk, NH * HD, (NH + NKV) * HD)):
                    sp.dma_start(raw[:, :, c0:c1], one(w).rearrange("(p k) n -> p k n", k=KD)).then_inc(ld_raw, 16)
                sp.dma_start(wv_s[:, :, :], one(wv).rearrange("(p k) n -> p k n", k=KD)).then_inc(ld_aw, 16)
                for j in range(2):
                    src = one(wo).rearrange("(p j i d) n -> j d p i n", p=2, j=2, i=4)[j]
                    for p in range(2):
                        sp.dma_start(wo_s[64 * j:64 * j + 64, 4 * p:4 * p + 4, :], src[:, p]).then_inc(ld_aw, 16)

            def expert_weights(l):
                for e in range(E):
                    sp.wait_ge(p_wo, l * B + e + 1)
                    for w, s, k in ((wg, wg_s, KD), (wu, wu_s, KD), (wd, wd_s, 4)):
                        src = w[l] if isinstance(l, int) else w[bass.ds(l, 1)].rearrange("a e r c -> (a e) r c")
                        src = src.rearrange("e (p k) n -> p e k n", k=k)
                        sp.dma_start(s[:, 1024 * e:1024 * e + 1024].rearrange("p (k n) -> p k n", k=k),
                                     src[:, e]).then_inc(ld_mw, 16)

            attention_weights(0)
            sp.wait_ge(st_zero, ZERO_STORES * 16)
            for u in range(2):
                sp.dma_start(sorted_y[u:u + 1, :], zero[u:u + 1, 0, 0:D]).then_inc(st_ye[u], 16)
            sp.wait_ge(x_ready, B)
            sp.dma_start(res_d, res).then_inc(st_res, 16)

            def layer_io(l, last):
                sp.wait_ge(st_res, 16)
                sp.wait_ge(moe_done, l + 1)
                expert_weights(l)

                def load_tile(T, u, peeled=False):
                    if not peeled:
                        sp.wait_ge(m_r, l * NT + T - 1)
                        alone(sp)
                    sp.dma_start(xe[u], sorted_x[bass.ds((NT - 1) * SLOT - T * SLOT, SLOT), :]).then_inc(ld_xe[u], 16)

                def store_tile(T, u):
                    sp.wait_ge(m_y, l * NT + T + 1)
                    sp.dma_start(sorted_y[bass.ds(T * SLOT, SLOT), :], ye[u]).then_inc(st_ye[u], 16)

                sp.wait_ge(p_sc, (l + 1) * B * 2)
                sp.wait_ge(scattered[0], (l + 1) * 16 * PARTS[0][1] * TOPK)
                load_tile(0, 0, True)
                load_tile(1, 1, True)

                def pair(i, first=False, end=False):
                    for u in range(2):
                        if not end:
                            load_tile(i * 2 + u + 2, u)
                        if not (first and u == 0):
                            store_tile(i * 2 + u - 1, 1 - u)

                pair(0, first=True)
                if not last:
                    sp.wait_ge(p_lg, (l + 1) * B)
                    attention_weights(l + 1)
                with sp.Fori(1, WHOLE // 2 - 1) as i:
                    pair(i)
                sp.wait_ge(scattered[1], (l + 1) * 16 * (B - PARTS[0][1]) * TOPK)
                alone(sp)
                with sp.Fori(WHOLE // 2 - 1, NT // 2 - 1) as i:
                    pair(i)
                pair(NT // 2 - 1, end=True)
                store_tile(NT - 1, 1)

            with sp.Fori(0, L - 1) as l:
                layer_io(l, False)
            layer_io(L - 1, True)
            sp.wait_ge(moe_done, L + 1)
            sp.dma_start(res, res_d).then_inc(ld_res, 16)
            for g in range(NG):
                sp.wait_ge(d_out, GB * g + GB)
                gs = slice(GB * g, GB * g + GB)
                sp.dma_start(out[gs].rearrange("b s d -> s b d"), x_sb[:, gs, 0:D]).then_inc(st_out, 16)
            sp.wait_ge(st_out, 16 * NG)

        @block.gpsimd
        def _(pool):
            pool.memset(probT[:, :, :], 0.0).then_inc(z_ready, 1)
            pool.memset(pos[:, :, :], 0).then_inc(z_ready, 1)
            for h in range(2):
                pool.memset(oh_b[h][:, :, :], 0.0).then_inc(z_ready, 1)
            pool.memset(wts[:, :, :], 0.0).then_inc(z_ready, 1)
            pool.memset(x_sb[:, :, D:DX], 0.0).then_inc(z_ready, 1)
            pool.wait_ge(z_ready, 6)
            zeroed = [(t, n) for n in range(HROWS // rows) for t in (sorted_x, sorted_y)]
            assert len(zeroed) <= B

            def norm_factors(out, var, n, at=0):
                width = var.shape[-1]
                alone(pool)
                pool.tensor_scalar(g_tmp[:, at:at + width], var, EPS, None, ALU.add).then_inc(g_eps, 1)
                pool.wait_ge(g_eps, n)
                return pool.tensor_tensor(out, g_tmp[:, at:at + width], cst[0:S, C_H:C_H + width], ALU.pow)

            pool.wait_ge(ld_const, 16)
            for i in range(B):
                pool.wait_ge(var_ready, i + 1)
                norm_factors(small[0:S, 28:29], small[0:S, 27:28], i + 1).then_inc(rstd_ready, 1)
                if i < len(zeroed):
                    t, n = zeroed[i]
                    pool.dma_start(t[rows * n:rows * n + rows, :].rearrange("(r p) d -> p r d", p=ZP),
                                   zero[:, :, 0:t.shape[-1]]).then_inc(st_zero, 16)

            def arrange_weights(n):
                pool.wait_ge(ld_raw, n * 16 * 2)
                alone(pool)
                for k in range(KD):
                    for h in range(2):
                        for p in range(2):
                            src = raw[:, k, 0:NH * HD].rearrange("x (p j i h d) -> x p h i j d", p=2, j=2, i=4, h=2)[:, p, h]
                            dst = wqk_s[:, k, 2 + 4 * p:6 + 4 * p, :].rearrange("x i (h j d) -> x h i j d", h=2, j=2)[:, h]
                            pool.tensor_copy(dst, src)
                        src = raw[:, k, NH * HD:(NH + NKV) * HD].rearrange("x (p j h d) -> x h p j d", p=2, j=2, h=2)[:, h]
                        dst = wqk_s[:, k, 0:2, :].rearrange("x p (h j d) -> x h p j d", h=2, j=2)[:, h]
                        last = pool.tensor_copy(dst, src)
                last.then_inc(aw_ready, 1)

            arrange_weights(1)
            def gather(l, b):
                if b >= 2:
                    pool.wait_ge(d_yr, l * B + b - 1)
                alone(pool)
                for k in range(TOPK):
                    pool.indirect_dma_start(
                        out=y_in[:, b % 2, k, :], out_offset=None, in_=sorted_y[0:FIRST * SLOT, :] if b < GB else sorted_y,
                        in_offset=bass.IndirectOffsetOnAxis(ap=pos[:, b, k:k + 1], axis=0)).then_inc(gathered[b % 2], 16)

            for u in range(2):
                pool.wait_ge(st_ye[u], 16)
            gather(0, 0)
            gather(0, 1)
            with pool.Fori(B, 2 * B - 2) as i:
                pool.wait_ge(var_ready, i + 1)
                norm_factors(small[0:S, 28:29], small[0:S, 27:28], i + 1).then_inc(rstd_ready, 1)
            gather(0, 2)
            gather(0, 3)
            for i in range(2 * B - 2, 2 * B):
                pool.wait_ge(var_ready, i + 1)
                norm_factors(small[0:S, 28:29], small[0:S, 27:28], i + 1).then_inc(rstd_ready, 1)

            def out_factors(l, h):
                a, z = PARTS[h]
                pool.wait_ge(a_sq2, l * B + z)
                norm_factors(r2[:, 0:z - a], ms2[:, a:z], 2 * B + l * 10 + 9 + h, GB).then_inc(g_r2, 1)

            def add_rotated(l, g):
                for n in range(8):
                    pool.wait_ge(d_rope, l * 40 + g * 10 + n + 3)
                    pool.tensor_tensor(qT[:, n, :], qT[:, n, :], rope[n % 2][:, :], ALU.add).then_inc(g_rope, 1)

            def in_factors(l, pair):
                pool.wait_ge(a_sq1, l * B + 2 * pair + 2)
                c = pair % 2 * 2
                norm_factors(r1[:, c:c + 2], ms1[:, c:c + 2], 2 * B + l * 10 + pair + 1, c).then_inc(g_r1, 1)

            def stored(l, tiles):
                for u in range(2):
                    pool.wait_ge(st_ye[u], l * (8 * NT) + (tiles + 1 - u) // 2 * 16 + 16 - 8 * NT)

            def prepare(l, start=0):
                for b in range(start, GB):
                    gather(l, b)
                for pair in range(GB // 2):
                    in_factors(l, pair)

            def attention(l):
                add_rotated(l, 0)
                stored(l, NT)
                gather(l, 4)
                gather(l, 5)
                for g in range(1, NG):
                    gather(l, 4 * g + 2)
                    in_factors(l, 2 * g)
                    gather(l, 4 * g + 3)
                    in_factors(l, 2 * g + 1)
                    if g < NG - 1:
                        gather(l, 4 * g + 4)
                        gather(l, 4 * g + 5)
                    else:
                        out_factors(l, 0)
                    add_rotated(l, g)

            def move_rows(l):
                for h, (a, z) in enumerate(PARTS):
                    if h == 1:
                        out_factors(l, 1)
                    pool.wait_ge(d_pos, l * 2 + h + 1)
                    alone(pool)
                    for b in range(a, z):
                        for k in range(TOPK):
                            pool.indirect_dma_start(
                                out=sorted_x if h == 0 else sorted_x[0:HROWS - WHOLE * SLOT, :],
                                out_offset=bass.IndirectOffsetOnAxis(ap=pos_x[:, b, k:k + 1], axis=0),
                                in_=x_sb[:, b, :], in_offset=None).then_inc(scattered[h], 16)

            pool.wait_ge(rstd_ready, 2 * B)
            prepare(0, GB)
            with pool.Fori(0, L - 1) as l:
                attention(l)
                move_rows(l)
                arrange_weights(l + 2)
                stored(l + 1, FIRST)
                prepare(l + 1)
            attention(L - 1)
            move_rows(L - 1)
            stored(L, FIRST)
            prepare(L)
            stored(L, NT)
            for b in range(GB, B):
                gather(L, b)

        @block.tensor
        def _(pe):
            pe.wait_ge(ld_const, 16)
            pe.wait_ge(c_bf, 4)

            def turn(b, u, n):
                pe.wait_ge(ld_dec[u], n * 16)
                if not (isinstance(b, int) and b == 0):
                    pe.wait_ge(decT_a, b)
                    pe.wait_ge(decT_v, b)
                    pe.wait_ge(encT_ready, b)
                for k in range(KD):
                    for c in range(CB):
                        pe.transpose(ps[:, k, c * CR:c * CR + CR],
                                     dec[u][:, c, :].rearrange("p (m k) -> p k m", k=KD)[:, k], ident[0:CR, 0:CR])
                pe.wait_ge(enc_ready, b + 1)
                for k in range(KD):
                    last = pe.transpose(ps[:, 2, k * S:k * S + S],
                                        enc[u % 2].rearrange("p (m k) -> p k m", k=KD)[:, k], ident[0:S, 0:S])
                last.then_inc(xT_done, 1)

            def similar(b):
                pe.wait_ge(decT_a, b + 1)
                pe.wait_ge(decT_v, b + 1)
                pe.wait_ge(e3_ready, b + 1)
                for k in range(KD):
                    last = pe.matmul(ps[0:S, 3, 0:CTX], e3T[:, k, :], decT[:, k, :], start=(k == 0), stop=(k == KD - 1))
                last.then_inc(sim_done, 1)

            def turn_attn(b):
                pe.wait_ge(attn_ready, b + 1)
                for c in range(CB):
                    last = pe.transpose(ps[0:CR, 4, c * S:c * S + S], attn[:, c * CR:c * CR + CR], ident[0:S, 0:S])
                last.then_inc(aT_done, 1)

            def attend(b, u):
                pe.wait_ge(aT_ready, b + 1)
                for k in range(KD):
                    for c in range(CB):
                        last = pe.matmul(ps[:, 5, k * S:k * S + S],
                                         dec[u][:, c, :].rearrange("p (m k) -> p k m", k=KD)[:, k],
                                         attnT[:, c, :], start=(c == 0), stop=(c == CB - 1))
                last.then_inc(hq_done, 1)

            turn(0, 0, 1)
            similar(0)

            def four(i, end):
                for u in range(4):
                    b = i * 4 + u
                    last = end and u == 3
                    if not last:
                        turn(b + 1, (u + 1) % 4, i + 1 + (u + 1) // 4)
                    turn_attn(b)
                    if not last:
                        similar(b + 1)
                    attend(b, u)

            with pe.Fori(0, B // 4 - 1) as i:
                four(i, False)
            four(B // 4 - 1, True)

            pe.wait_ge(batt_v, 1)
            pe.transpose(ps[0:B, 6, 0:S], small[0:S, 0:B], ident[0:S, 0:S]).then_inc(batt_p, 1)
            pe.wait_ge(batt_v, 3)
            for n in range(4):
                last = pe.matmul(ps[:, n, 0:GN], cst[0:B, C_ONE:C_ONE + 128], battD[:, 4 * n:4 * n + 4, :],
                                 start=True, stop=True)
            last.then_inc(batt_p, 1)
            pe.wait_ge(ld_wq, 32)
            def project(b, u):
                pe.wait_ge(feat_a, b + 1)
                pe.wait_ge(feat_v, b + 1)
                if not (isinstance(b, int) and b < 2):
                    pe.wait_ge(x_ready, b - 1)
                for c in range(8):
                    last = pe.matmul(ps[0:S, 6 + u, 0:D], feat[u][:, c, :], wqv[:, c, :], start=(c == 0), stop=(c == 7))
                last.then_inc(feat_done, 1)

            for u in range(2):
                project(u, u)
            with pe.Fori(1, B // 2) as i:
                for u in range(2):
                    project(i * 2 + u, u)
            pe.wait_ge(x_ready, B)
            pe.wait_ge(ld_ln, 64)
            pe.sem_inc(moe_done, 1)

            def norm_turn(l, pair, bank):
                pe.wait_ge(a_xn1, l * B + 2 * pair + 2)
                for k in range(KD):
                    for u in range(2):
                        last = pe.transpose(ps[:, bank, (2 * k + u) * S:(2 * k + u + 1) * S],
                                            xn1[:, u, :].rearrange("p (m k) -> p k m", k=KD)[:, k], ident[0:S, 0:S])
                last.then_inc(p_t1, 1)

            def layer(l):
                def project_values(g):
                    pe.wait_ge(a_t1, l * (B // 2) + 2 * g + 2)
                    for pair in range(GB // 2):
                        for u in range(2):
                            bb = 2 * pair + u
                            for k in range(KD):
                                last = pe.matmul(ps[0:S, 4 + pair, u * D:u * D + NKV * HD], xnT[:, k, bb * S:bb * S + S],
                                                 wv_s[:, k, :], start=(k == 0), stop=(k == KD - 1))
                        last.then_inc(p_v, 1)

                def project_heads(g, blocks):
                    for n in blocks:
                        if n == 0:
                            pe.wait_ge(a_t1, l * (B // 2) + 2 * g + 2)
                        if n in (0, 2) and g:
                            pe.wait_ge(a_exp, (l * B + 4 * g - 1) * 2 + n // 2 + 1)
                        if n > 3:
                            pe.wait_ge(d_rope, l * 40 + g * 10 + n - 3)
                        for k in range(KD):
                            last = pe.matmul(ps[:, n % 4, 0:GN], wqk_s[:, k, n, :], xnT[:, k, :], start=(k == 0), stop=(k == KD - 1))
                        last.then_inc(p_qk, 1)

                def scores(b, p):
                    g, bb = b // 4, b % 4
                    pe.wait_ge(a_key, l * 8 + g * 2 + 2)
                    pe.wait_ge(g_rope, l * 32 + g * 8 + 8)
                    if bb:
                        pe.wait_ge(a_exp, (l * B + b - 1) * 2 + p + 1)
                    for n in range(2 * p, 2 * p + 2):
                        pe.matmul(ps[0:S, n, 0:4 * S], ident_b[:, :], bc(causal_b[:, :], 1, [S, 4, S]), start=True, stop=False)
                        for i in range(2):
                            last = pe.matmul(ps[0:S, n, i * 2 * S:(i + 1) * 2 * S], qT[:, 2 * n + i, bb * S:bb * S + S],
                                             kz[:, p, :, bb * S:bb * S + S], start=False, stop=(i == 1))
                    last.then_inc(p_sc, 1)

                def turn_probs(b, unit):
                    p, j = unit // 2, unit % 2
                    if unit < 2 and b % 4 == 0:
                        pe.wait_ge(a_v, l * (B // 2) + b // 2 + unit + 1)
                    if j == 0:
                        pe.wait_ge(d_norm, (l * B + b) * 2 + p + 1)
                    if unit >= 2:
                        pe.wait_ge(a_pt, (l * B + b) * 2 + unit - 1)
                    for i in range(4):
                        last = pe.transpose(ps[0:S, 4 + unit % 2, i * S:i * S + S],
                                            prob[:, b % 2, p * 8 + i * 2 + j, :], ident[0:S, 0:S])
                    last.then_inc(p_pt, 1)

                def weigh(b, unit):
                    p, j = unit // 2, unit % 2
                    pe.wait_ge((a_pt, d_pt)[p], (l * B + b) * 2 + j + 1)
                    if unit == 0 and b:
                        pe.wait_ge(d_wo, l * B + b)
                    if unit == 2 and b > 1:
                        pe.wait_ge(d_lg, l * B + b - 1)
                    if unit == 2 and b < B - GB and b % 4 == 2:
                        pe.wait_ge(a_t1, l * (B // 2) + b // 4 * 2 + 3)
                    if unit == 2 and b == RANK_STEP + 1:
                        pe.wait_ge(d_rt, l * 2 + 1)
                    last = pe.matmul(ps[64 * j:64 * j + 64, 6 + p, 0:GN], v_s[:, VALUES[b], unit * HD:unit * HD + HD],
                                     probT[:, unit, :], start=True, stop=True)
                    if j == 1:
                        last.then_inc((p_ot0, p_ot1)[p], 1)

                def turn_x(b):
                    pe.wait_ge(d_wo, l * B + b + 1)
                    for k in range(KD):
                        last = pe.transpose(ps[:, 5, k * S:k * S + S],
                                            x_sb[:, b, 0:D].rearrange("p (m k) -> p k m", k=KD)[:, k], ident[0:S, 0:S])
                    last.then_inc(p_t2, 1)

                def route_logits(b):
                    pe.wait_ge(a_t2, l * B + b + 1)
                    for k in range(KD):
                        last = pe.matmul(ps[0:S, 7, 0:E], x2T[:, k, :], wr_l[:, k, :],
                                         start=(k == 0), stop=(k == KD - 1))
                    last.then_inc(p_lg, 1)

                def out_project_first(b):
                    pe.wait_ge(a_ot, l * B + b + 1)
                    for i in range(4):
                        pe.matmul(ps[0:S, 6, 0:D], oT[:, 0, i * S:i * S + S], wo_s[:, i, :], start=(i == 0), stop=False)

                def out_project_second(b):
                    pe.wait_ge(d_ot, l * B + b + 1)
                    for i in range(4):
                        last = pe.matmul(ps[0:S, 6, 0:D], oT[:, 1, i * S:i * S + S], wo_s[:, 4 + i, :],
                                         start=False, stop=(i == 3))
                    last.then_inc(p_wo, 1)

                def count_rows(h):
                    pe.wait_ge(d_oh, l * 2 + h + 1)
                    N = (PARTS[h][1] - PARTS[h][0]) * TOPK
                    out_w = (N + 1) * E
                    hot = oh_b[h][:, :, :].rearrange("p a e -> p (a e)")
                    pe.matmul(ps[0:S, 7, 128:128 + out_w], ones_b[:, :], hot[:, 0:out_w], start=True, stop=False)
                    for n in range(2, N + 1):
                        pe.matmul(ps[0:S, 7, 128 + n * E:128 + out_w], ones_b[:, :], hot[:, E:E + out_w - n * E],
                                  start=False, stop=False)
                    pe.matmul(ps[0:S, 7, 128:128 + out_w], low_b[:, :], hot[:, E:E + out_w], start=False, stop=True).then_inc(p_rt, 1)

                wr_l = small_wr
                pe.wait_ge(ld_aw, (l + 1) * 16 * 5)
                pe.wait_ge(aw_ready, l + 1)
                project_heads(0, range(10))
                project_values(0)
                scores(0, 0)
                scores(0, 1)
                for g in range(NG):
                    for bb in range(GB):
                        b = g * 4 + bb
                        turning = g < NG - 1 and bb > 1
                        if bb < 3:
                            scores(b + 1, 0)
                        if b == RANK_STEP + 1:
                            pe.wait_ge(d_lg, l * B + b - 1)
                            count_rows(0)
                        if turning:
                            pe.wait_ge(d_lg, l * B + b - 1)
                            norm_turn(l, 2 * g + bb, 7)
                        turn_probs(b, 0)
                        turn_probs(b, 1)
                        if bb < 3:
                            scores(b + 1, 1)
                        if bb == 3 and g < NG - 1:
                            project_heads(g + 1, range(0, 2))
                            weigh(b, 0)
                            weigh(b, 1)
                            project_heads(g + 1, range(2, 4))
                            turn_probs(b, 2)
                            turn_probs(b, 3)
                            project_heads(g + 1, range(4, 6))
                            weigh(b, 2)
                            weigh(b, 3)
                            project_heads(g + 1, range(6, 10))
                            project_values(g + 1)
                            scores(b + 1, 0)
                            scores(b + 1, 1)
                            pe.wait_ge(a_v, l * (B // 2) + 2 * g + 4)
                            turn_x(b - 1)
                            out_project_first(b)
                            out_project_second(b)
                            route_logits(b - 1)
                        else:
                            weigh(b, 0)
                            turn_probs(b, 2)
                            weigh(b, 1)
                            turn_probs(b, 3)
                            weigh(b, 2)
                            weigh(b, 3)
                            if b:
                                turn_x(b - 1)
                            out_project_first(b)
                            out_project_second(b)
                            if b:
                                route_logits(b - 1)
                pe.wait_ge(ld_mw, (l + 1) * 16 * 3 * E)

                def turn_tile(T, u, n):
                    pe.wait_ge(ld_xe[u], l * (8 * NT) + n * 16)
                    if not (isinstance(T, int) and T == 0):
                        pe.wait_ge(m_xT, l * NT + T)
                    for k in range(KD):
                        last = pe.transpose(ps[:, 5, k * SLOT:k * SLOT + SLOT],
                                            xe[u][:, 0:D].rearrange("p (m k) -> p k m", k=KD)[:, k], ident)
                    last.then_inc(m_tx, 1)

                def up(T, u, e, w, bank, done):
                    for k in range(KD):
                        last = pe.matmul(ps[:, bank, :], xeT[u][:, k, :], w[:, bass.ds(e * 1024 + k * 512, 512)],
                                         start=(k == 0), stop=(k == KD - 1))
                    last.then_inc(done, 1)

                def turn_hidden(T, u):
                    pe.wait_ge(m_h, l * NT + T + 1)
                    if not (isinstance(T, int) and T == 0):
                        pe.wait_ge(m_hT, l * NT + T)
                    for c in range(4):
                        last = pe.transpose(ps[:, 4, c * SLOT:c * SLOT + SLOT],
                                            hid[u].rearrange("p (m c) -> p c m", c=4)[:, c], ident)
                    last.then_inc(m_th, 1)

                def down(T, u, e):
                    pe.wait_ge(m_hT, l * NT + T + 1)
                    if not (isinstance(T, int) and T == 0):
                        pe.wait_ge(m_y, l * NT + T)
                    for c in range(4):
                        last = pe.matmul(ps[:, 6 + u, 0:D], hidT[:, c, :], wd_s[:, bass.ds(e * 1024 + c * D, D)],
                                         start=(c == 0), stop=(c == 3))
                    last.then_inc(m_dn, 1)

                def expert_of(T):
                    return pe.value_load(tile_e[0:1, bass.ds(T, 1)], min_val=0, max_val=E - 1)

                def pair(i, first=False, end=False):
                    for u in range(2):
                        T = i * 2 + u
                        e = expert_of(T)
                        pe.wait_ge(m_xT, l * NT + T + 1)
                        if not first:
                            pe.wait_ge(m_h, l * NT + T - 1)
                        up(T, u, e, wg_s, 2 * u, m_g)
                        if not (first and u == 0):
                            turn_hidden(T - 1, 1 - u)
                        else:
                            turn_x(B - 1)
                        up(T, u, e, wu_s, 2 * u + 1, m_u)
                        if first and u == 0:
                            pe.wait_ge(d_lg, l * B + B - 1)
                            route_logits(B - 1)
                        if not (end and u == 1):
                            turn_tile(T + 1, 1 - u, i + 1 + u)
                        else:
                            norm_turn(l + 1, 0, 5)
                        if isinstance(i, int) and T == 2:
                            pe.wait_ge(d_lg, l * B + B)
                            alone(pe)
                        if isinstance(i, int) and T == 4:
                            pe.wait_ge(d_rt, l * 2 + 2)
                            alone(pe)
                        if not (first and u == 0):
                            down(T - 1, 1 - u, expert_of(T - 1))

                pe.wait_ge(d_te, l * 2 + 1)
                turn_tile(0, 0, 1)
                pair(0, first=True)
                pair(1)
                pe.wait_ge(m_y, l * NT + 2)
                count_rows(1)
                pair(2)
                with pe.Fori(3, WHOLE // 2) as i:
                    pair(i)
                pe.wait_ge(d_te, l * 2 + 2)
                alone(pe)
                with pe.Fori(WHOLE // 2, NT // 2 - 1) as i:
                    pair(i)
                pair(NT // 2 - 1, end=True)
                turn_hidden(NT - 1, 1)
                pe.wait_ge(a_t1, (l + 1) * (B // 2) + 1)
                norm_turn(l + 1, 1, 5)
                down(NT - 1, 1, expert_of(NT - 1))
                pe.wait_ge(m_y, (l + 1) * NT)
                pe.sem_inc(moe_done, 1)

            for n in range(GB // 2):
                if n:
                    pe.wait_ge(a_t1, n)
                norm_turn(0, n, 6)
            with pe.Fori(0, L) as l:
                small_wr = wr_s[:, bass.ds(l, 1), :, :].rearrange("p a k e -> p (a k) e")
                layer(l)

        @block.scalar
        def _(act):
            act.wait_ge(ld_const, 16)
            act.activation(ident_b[:, :], cst[0:S, C_ID:C_ID + S], ACT.Copy).then_inc(c_bf, 1)
            act.activation(causal_b[:, :], cst[0:S, C_CAUSAL:C_CAUSAL + S], ACT.Copy).then_inc(c_bf, 1)
            act.activation(low_b[:, :], cst[0:S, C_LOW:C_LOW + S], ACT.Copy).then_inc(c_bf, 1)
            act.activation(ones_b[:, :], cst[0:S, C_ONE:C_ONE + S], ACT.Copy).then_inc(c_bf, 1)

            def copy_turned(b):
                act.wait_ge(xT_done, b + 1)
                act.activation(decT[:, 0, :], ps[:, 0, 0:CTX], ACT.Copy).then_inc(decT_a, 1)
                act.activation(encT[:, :, bass.ds(b * S, S)], ps[:, 2, 0:KD * S].rearrange("p (k i) -> p k i", k=KD),
                               ACT.Copy).then_inc(encT_ready, 1)

            def exponents(b):
                act.wait_ge(max_ready, b + 1)
                act.activation(attn[:, 0:CTX], ps[0:S, 3, 0:CTX], ACT.Exp, bias=small[0:S, 33:34],
                               accum_out=small[0:S, 34:35]).then_inc(exp_done, 1)

            def copy_attn(b):
                act.wait_ge(aT_done, b + 1)
                act.activation(attnT, ps[0:CR, 4, 0:CB * S].rearrange("p (c i) -> p c i", c=CB), ACT.Copy).then_inc(aT_ready, 1)

            copy_turned(0)
            exponents(0)

            def xstep(b):
                copy_turned(b + 1)
                copy_attn(b)
                exponents(b + 1)

            with act.Fori(0, B - 1) as b:
                xstep(b)
            copy_attn(B - 1)

            act.wait_ge(batt_v, 2)
            act.activation(battD[:, 0, :], ps[0:B, 6, 0:S], ACT.Exp, bias=small[0:B, 41:42],
                           accum_out=small[0:B, 42:43]).then_inc(batt_a, 1)

            def features(b, u):
                if isinstance(b, int) and b < 2:
                    act.wait_ge(hq_ready, B)
                else:
                    act.wait_ge(feat_done, b - 1)
                act.activation(feat[u][:, 0:2, :], encT[:, :, bass.ds(b * S, S)], ACT.Copy)
                act.activation(feat[u][:, 2:4, :], hqT[:, :, bass.ds(b * S, S)], ACT.Copy).then_inc(feat_a, 1)

            for u in range(2):
                features(u, u)
            with act.Fori(1, B // 2) as i:
                for u in range(2):
                    features(i * 2 + u, u)
            act.wait_ge(ld_ln, 64)

            def square_in(l, b):
                act.wait_ge(d_x, l * B + b + 1)
                if b:
                    act.wait_ge(a_sq1, l * B + b)
                act.activation(xsq[:, 0, :], x_sb[:, b, 0:D], ACT.Square, scale=1.0 / 16,
                               accum_out=ms1[:, b % 4:b % 4 + 1]).then_inc(a_sq1, 1)

            def norm_in(l, pair):
                act.wait_ge(g_r1, l * (B // 2) + pair + 1)
                for u in range(2):
                    b = 2 * pair + u
                    act.activation(xn1[:, u, :], x_sb[:, b, 0:D], ACT.Copy, scale=r1[:, b % 4:b % 4 + 1]).then_inc(a_xn1, 1)

            def copy_in(l, pair, bank):
                act.wait_ge(p_t1, l * (B // 2) + pair + 1)
                alone(act)
                c = pair % 2 * 2 * S
                for k in range(KD):
                    scale = ln1T[:, l, k:k + 1] if isinstance(l, int) else ln1T[:, bass.ds(l, 1), k]
                    last = act.activation(xnT[:, k, c:c + 2 * S], ps[:, bank, k * 2 * S:(k + 1) * 2 * S], ACT.Copy, scale=scale)
                last.then_inc(a_t1, 1)

            def layer(l):
                def copy_values(g):
                    for pair in range(GB // 2):
                        first, second = VALUES[4 * g + 2 * pair:4 * g + 2 * pair + 2]
                        act.wait_ge(p_v, l * (B // 2) + 2 * g + pair + 1)
                        act.activation(v_s[:, first:second + 1:second - first, :],
                                       ps[0:S, 4 + pair, :].rearrange("p (u n) -> p u n", u=2), ACT.Copy).then_inc(a_v, 1)

                def spread_keys(g):
                    for n in range(2):
                        act.wait_ge(d_rope, l * 40 + g * 10 + n + 1)
                        for j in range(2):
                            last = act.activation(kz[:, n, j, :], rope[n][:, :], ACT.Copy, scale=cst[:, C_J + j:C_J + j + 1])
                        last.then_inc(a_key, 1)

                def exponents(b, p):
                    act.wait_ge(d_max, (l * B + b) * 2 + p + 1)
                    for n in range(8 * p, 8 * p + 8):
                        bank, h = n // 4, n % 4
                        last = act.activation(prob[:, b % 2, n, :], ps[0:S, bank, h * S:h * S + S], ACT.Exp,
                                              bias=nmax[:, b % 2, n:n + 1], scale=SCALE, accum_out=rsum[:, b % 2, n:n + 1])
                    last.then_inc(a_exp, 1)

                def copy_probs(b, unit):
                    act.wait_ge(p_pt, l * 64 + b * 4 + unit + 1)
                    act.activation(probT[:, unit, :], ps[0:S, 4 + unit % 2, 0:GN], ACT.Copy).then_inc(a_pt, 1)

                def copy_outputs(b):
                    act.wait_ge(p_ot0, l * B + b + 1)
                    act.activation(oT[:, 0, :], ps[:, 6, 0:GN], ACT.Copy).then_inc(a_ot, 1)

                def square_out(b):
                    act.wait_ge(d_wo, l * B + b + 1)
                    if b:
                        act.wait_ge(a_sq2, l * B + b)
                    act.activation(xsq[:, 1, :], x_sb[:, b, 0:D], ACT.Square, scale=1.0 / 16,
                                   accum_out=ms2[:, b:b + 1]).then_inc(a_sq2, 1)

                def copy_out(b):
                    act.wait_ge(p_t2, l * B + b + 1)
                    alone(act)
                    for k in range(KD):
                        last = act.activation(x2T[:, k, :], ps[:, 5, k * S:k * S + S], ACT.Copy,
                                              scale=ln2T[:, bass.ds(l, 1), k])
                    last.then_inc(a_t2, 1)

                def gate_exponents(h):
                    act.wait_ge(d_gate, l * 2 + h + 1)
                    n = PARTS[h][1] - PARTS[h][0]
                    act.activation(gate[:, 1, 0:n], gate[:, 0, 0:n], ACT.Exp).then_inc(a_rt, 1)

                spread_keys(0)
                copy_values(0)
                exponents(0, 0)
                exponents(0, 1)
                for g in range(NG):
                    for bb in range(GB):
                        b = g * 4 + bb
                        if g < NG - 1 and bb == 3:
                            copy_in(l, 2 * g + bb, 7)
                        copy_probs(b, 0)
                        if g < NG - 1 and bb == 2:
                            copy_in(l, 2 * g + bb, 7)
                        copy_probs(b, 1)
                        if bb == 3 and g < NG - 1:
                            spread_keys(g + 1)
                        if b < B - 1 and bb < 3:
                            exponents(b + 1, 0)
                        copy_outputs(b)
                        if g < NG - 1 and bb in (1, 2):
                            norm_in(l, 2 * g + 1 + bb)
                        if bb == 3 and b < B - 1:
                            copy_values(g + 1)
                            exponents(b + 1, 0)
                            copy_out(b - 1)
                        if b < B - 1:
                            exponents(b + 1, 1)
                        if b and (bb < 3 or b == B - 1):
                            copy_out(b - 1)
                        if g < NG - 1:
                            for nb in (2 * bb, 2 * bb + 1) if bb < 2 else ():
                                square_in(l, 4 * g + 4 + nb)
                        if b < B - 1:
                            square_out(b)
                        if b == RANK_STEP + 1:
                            gate_exponents(0)

                def copy_tile(T, u):
                    act.wait_ge(m_tx, l * NT + T + 1)
                    alone(act)
                    for k in range(KD):
                        last = act.activation(xeT[u][:, k, :], ps[:, 5, k * SLOT:k * SLOT + SLOT], ACT.Copy,
                                              scale=ln2T[:, bass.ds(l, 1), k])
                    last.then_inc(m_xT, 1)

                def tanh(T, u):
                    act.wait_ge(m_g, l * NT + T + 1)
                    act.wait_ge(m_r, l * NT + T + 1)
                    if not (isinstance(T, int) and T == 0):
                        act.wait_ge(m_h, l * NT + T)
                    act.activation(th, ps[:, 2 * u, :], ACT.Tanh, scale=er[:, u, 0:1]).then_inc(m_tanh, 1)

                def copy_hidden(T):
                    act.wait_ge(m_th, l * NT + T + 1)
                    if not (isinstance(T, int) and T == 0):
                        act.wait_ge(m_dn, l * NT + T)
                    act.activation(hidT, ps[:, 4, :].rearrange("p (c t) -> p c t", c=4), ACT.Copy).then_inc(m_hT, 1)

                def pair(i, first=False, end=False):
                    for u in range(2):
                        T = i * 2 + u
                        tanh(T, u)
                        if not (first and u == 0):
                            copy_hidden(T - 1)
                        else:
                            copy_out(B - 1)
                            square_out(B - 1)
                        if not (end and u == 1):
                            copy_tile(T + 1, 1 - u)

                copy_tile(0, 0)
                pair(0, first=True)
                pair(1)
                gate_exponents(1)
                with act.Fori(2, TAIL) as i:
                    pair(i)
                for i in range(TAIL, NT // 2):
                    pair(i, end=(i == NT // 2 - 1))
                    for b in AHEAD[i - TAIL]:
                        square_in(l + 1, b)
                    if i == NT // 2 - 2:
                        norm_in(l + 1, 0)
                copy_in(l + 1, 0, 5)
                norm_in(l + 1, 1)
                copy_hidden(NT - 1)
                copy_in(l + 1, 1, 5)

            for b in range(GB):
                square_in(0, b)
            for n in range(GB // 2):
                norm_in(0, n)
                copy_in(0, n, 6)
            with act.Fori(0, L) as l:
                layer(l)

        @block.vector
        def _(dve):
            dve.wait_ge(ld_x0, 16)
            dve.wait_ge(ld_xw, 16 * 3)

            def normed(step, src, dst, n, done):
                alone(dve)
                step(dve.bn_stats(small[0:S, 20:26], src))
                alone(dve)
                step(dve.bn_aggr(small[0:S, 26:28], small[0:S, 20:26]))
                dve.sem_inc(var_ready, 1)
                dve.wait_ge(rstd_ready, n)
                dve.tensor_scalar(dst, src, small[0:S, 26:27], small[0:S, 28:29],
                                  ALU.subtract, ALU.mult).then_inc(done, 1)

            def xrow(b):
                return x_sb[:, bass.ds(b, 1), 0:D].rearrange("p a d -> p (a d)")

            def encode(b, u, base):
                step = Steps(dve, dx, base)
                normed(step, xrow(b), enc[u], b + 1, enc_ready)
                dve.wait_ge(enc_ready, b + 1)
                step(dve.scalar_tensor_tensor(out=scratch, in0=enc[u], scalar=1.0, in1=w1row, op0=ALU.mult, op1=ALU.mult,
                                              accum_out=simrow[:, bass.ds(b, 1)]))
                assert step.n == 3

            def copy_turned(b):
                dve.wait_ge(xT_done, b + 1)
                dve.tensor_copy(decT[:, 1, :], ps[:, 1, 0:CTX]).then_inc(decT_v, 1)
                dve.wait_ge(encT_ready, b + 1)
                for k in range(KD):
                    last = dve.tensor_scalar(e3T[:, k, :], encT[:, k, bass.ds(b * S, S)], wsT[:, 2, k:k + 1],
                                             wsT[:, 1, k:k + 1], ALU.mult, ALU.add)
                last.then_inc(e3_ready, 1)

            def row_max(b, base):
                step = Steps(dve, dx, base)
                dve.wait_ge(sim_done, b + 1)
                step(dve.tensor_reduce(small[0:S, 32:33], ps[0:S, 3, 0:CTX], AX_X, ALU.max))
                dve.tensor_scalar(small[0:S, 33:34], small[0:S, 32:33], -1.0, None, ALU.mult).then_inc(max_ready, 1)
                step(dve.scalar_tensor_tensor(out=simmax[:, bass.ds(b, 1)], in0=small[0:S, 32:33], scalar=bsim[:, :],
                                              in1=simrow[:, bass.ds(b, 1)], op0=ALU.add, op1=ALU.add))
                assert step.n == 2

            def scale_attn(b, base):
                step = Steps(dve, dx, base)
                dve.wait_ge(exp_done, b + 1)
                step(dve.reciprocal(small[0:S, 35:36], small[0:S, 34:35]))
                dve.tensor_scalar(attn[:, 0:CTX], attn[:, 0:CTX], small[0:S, 35:36], None, ALU.mult).then_inc(attn_ready, 1)

            def copy_hq(b):
                dve.wait_ge(hq_done, b + 1)
                dve.tensor_copy(hqT[:, :, bass.ds(b * S, S)],
                                ps[:, 5, 0:KD * S].rearrange("p (k i) -> p k i", k=KD)).then_inc(hq_ready, 1)

            simmax = small[0:S, 0:B]
            encode(0, 0, 0)
            copy_turned(0)
            encode(1, 1, 3)
            row_max(0, 6)
            scale_attn(0, 8)

            def xstep(b, u, base, more):
                copy_turned(b + 1)
                n = 0
                if more:
                    encode(b + 2, u, base)
                    n = 3
                row_max(b + 1, base + n)
                copy_hq(b)
                scale_attn(b + 1, base + n + 2)

            dve.wait_ge(ld_x, 16)
            with dve.Fori(0, B // 2 - 1) as i:
                for u in range(2):
                    xstep(i * 2 + u, u, i * 12 + 9 + 6 * u, True)
            base = 9 + 12 * (B // 2 - 1)
            xstep(B - 2, 0, base, False)
            copy_hq(B - 1)
            step = Steps(dve, dx, base + 3)
            dve.sem_inc(batt_v, 1)
            dve.wait_ge(batt_p, 1)
            step(dve.tensor_reduce(small[0:B, 40:41], ps[0:B, 6, 0:S], AX_X, ALU.max))
            step(dve.tensor_scalar(small[0:B, 41:42], small[0:B, 40:41], -1.0, None, ALU.mult))
            dve.sem_inc(batt_v, 1)
            dve.wait_ge(batt_a, 1)
            step(dve.reciprocal(small[0:B, 43:44], small[0:B, 42:43]))
            step(dve.tensor_scalar(batt, battD[:, 0, :], small[0:B, 43:44], None, ALU.mult))
            step(dve.tensor_tensor(battD, bc(cst[0:B, C_ID:C_ID + B], 2, [B, B, S]), bc(batt, 1, [B, B, S]), ALU.mult))
            dve.sem_inc(batt_v, 1)
            dve.wait_ge(batt_p, 2)
            for k in range(KD):
                for n in range(4):
                    ins = dve.tensor_tensor(prodT[:, 4 * n:4 * n + 4, :],
                                            encT[:, k, n * GN:n * GN + GN].rearrange("p (b i) -> p b i", b=4),
                                            ps[:, n, 0:GN].rearrange("p (b i) -> p b i", b=4), ALU.mult)
                step(ins)
                step(dve.tensor_reduce(hcT[:, k, :], prodT, AX_X, ALU.add))
            base = base + 3 + step.n

            def features(b, u, base):
                step = Steps(dve, dx, base)
                if not (isinstance(b, int) and b < 2):
                    dve.wait_ge(feat_done, b - 1)
                e = encT[:, :, bass.ds(b * S, S)]
                dve.tensor_tensor(feat[u][:, 4:6, :], e, hqT[:, :, bass.ds(b * S, S)], ALU.mult)
                for k in range(KD):
                    last = dve.tensor_scalar(feat[u][:, 6 + k, :], encT[:, k, bass.ds(b * S, S)],
                                             hcT[:, k, bass.ds(b, 1)], None, ALU.mult)
                last.then_inc(feat_v, 1)

            def finish_x(b, u, base):
                step = Steps(dve, dx, base)
                r = res[:, bass.ds(b, 1), :].rearrange("p a d -> p (a d)")
                dve.wait_ge(feat_done, b + 1)
                step(dve.tensor_tensor(r, ps[0:S, 6 + u, 0:D], bqv, ALU.add))
                step(dve.tensor_tensor(r, r, xrow(b), ALU.add))
                normed(step, r, xrow(b), b + B + 1, x_ready)
                assert step.n == 4

            dve.wait_ge(ld_wq, 32)
            features(0, 0, 0)
            features(1, 1, 0)
            with dve.Fori(0, B // 2 - 1) as i:
                for u in range(2):
                    finish_x(i * 2 + u, u, i * 8 + 4 * u + base)
                    features(i * 2 + u + 2, u, 0)
            base += 8 * (B // 2 - 1)
            def combine(step, l, b):
                dve.wait_ge(gathered[b % 2], l * (16 * TOPK * B // 2) + (b // 2 + 1) * 16 * TOPK)
                step(dve.tensor_scalar(mix_b, y_in[:, b % 2, 0, :], wts[:, b, 0:1], None, ALU.mult))
                ins = dve.scalar_tensor_tensor(out=mix_b, in0=y_in[:, b % 2, 1, :], scalar=wts[:, b, 1:2], in1=mix_b,
                                               op0=ALU.mult, op1=ALU.add)
                ins.then_inc(d_yr, 1)
                dve.wait_ge(d_yr, l * B + b + 1)
                step(dve.tensor_tensor(x_sb[:, b, 0:D], x_sb[:, b, 0:D], mix_b, ALU.add))

            def rows_in(step, l, b):
                combine(step, l, b)
                dve.tensor_scalar(x_sb[:, b, 0:D], x_sb[:, b, 0:D], CLIP, -CLIP, ALU.min, ALU.max).then_inc(d_x, 1)

            def layer(l):
                step = Steps(dve, dv, 2 * GB + l * DVE_LAYER)

                def rotate(g, blocks=range(10)):
                    for n in blocks:
                        dve.wait_ge(p_qk, l * 40 + g * 10 + n + 1)
                        out_c = kz[:, n, 0, :] if n < 2 else qT[:, n - 2, :]
                        src = ps[:, n % 4, 0:GN].rearrange("p (b t) -> p b t", b=GB)
                        s = rope[n % 2][:, :].rearrange("p (b t) -> p b t", b=GB)
                        dve.tensor_tensor(out_c.rearrange("p (b t) -> p b t", b=GB), src,
                                          bc(cst[:, C_COS:C_COS + S], 1, [128, GB, S]), ALU.mult)
                        if n in (2, 3):
                            dve.wait_ge(a_key, l * 8 + g * 2 + n - 1)
                        if n > 3:
                            dve.wait_ge(g_rope, l * 32 + g * 8 + n - 3)
                        for a, z in ((0, 64), (64, 0)):
                            ins = dve.tensor_tensor(s[a:a + 64], src[z:z + 64],
                                                    bc(cst[a:a + 64, C_SIN:C_SIN + S], 1, [64, GB, S]), ALU.mult)
                        if n < 2:
                            step(ins)
                            ins = dve.tensor_tensor(rope[n % 2][:, :], out_c, rope[n % 2][:, :], ALU.add)
                        ins.then_inc(d_rope, 1)

                def maxima(b, p):
                    dve.wait_ge(p_sc, (l * B + b) * 2 + p + 1)
                    hs = slice(8 * p, 8 * p + 8)
                    step(dve.tensor_reduce(rmax[:, hs].rearrange("p (n h) -> p n h", n=2), heads(p), AX_X, ALU.max))
                    dve.tensor_scalar(nmax[:, b % 2, hs], rmax[:, hs], -SCALE, None, ALU.mult).then_inc(d_max, 1)

                def scale_probs(b, p):
                    dve.wait_ge(a_exp, (l * B + b) * 2 + p + 1)
                    hs = slice(8 * p, 8 * p + 8)
                    step(dve.reciprocal(rrec[:, hs], rsum[:, b % 2, hs]))
                    dve.tensor_tensor(prob[:, b % 2, hs, :], prob[:, b % 2, hs, :], bc(rrec[:, hs], 2, [S, 8, S]),
                                      ALU.mult).then_inc(d_norm, 1)

                def copy_probs(b):
                    for unit in range(2, 4):
                        dve.wait_ge(p_pt, l * 64 + b * 4 + unit + 1)
                        dve.tensor_copy(probT[:, unit, :], ps[0:S, 4 + unit % 2, 0:GN]).then_inc(d_pt, 1)

                def copy_outputs(b):
                    dve.wait_ge(p_ot1, l * B + b + 1)
                    dve.tensor_copy(oT[:, 1, :], ps[:, 7, 0:GN]).then_inc(d_ot, 1)

                def add_attention(b):
                    dve.wait_ge(p_wo, l * B + b + 1)
                    step(dve.tensor_tensor(x_sb[:, b, 0:D], ps[0:S, 6, 0:D], x_sb[:, b, 0:D], ALU.add))
                    dve.tensor_scalar(x_sb[:, b, 0:D], x_sb[:, b, 0:D], CLIP, -CLIP, ALU.min, ALU.max).then_inc(d_wo, 1)

                def logits(b):
                    dve.wait_ge(p_lg, l * B + b + 1)
                    dve.tensor_copy(lg[:, b % 2, :], ps[0:S, 7, 0:E]).then_inc(d_lg, 1)
                    dve.wait_ge(d_lg, l * B + b + 1)
                    alone(dve)
                    step(dve.max(top[:, b, :], lg[:, b % 2, :]))
                    alone(dve)
                    step(dve.max_index(idx[:, b, :], top[:, b, :], lg[:, b % 2, :]))

                def choose(h):
                    b0, b1 = PARTS[h]
                    n, N, hs = b1 - b0, (b1 - b0) * TOPK, slice(b0, b1)
                    hot = hot_all[:, 0:N * E].rearrange("p (a e) -> p a e", e=E)
                    idxf = idxf_all[:, 0:N]
                    step(dve.tensor_copy(idxf.rearrange("p (b k) -> p b k", k=TOPK), idx[:, hs, 0:TOPK]))
                    step(dve.tensor_tensor(hot, bc(idxf, 2, [S, N, E]), bc(cst[0:S, C_E:C_E + E], 1, [S, N, E]), ALU.is_equal))
                    step(dve.tensor_copy(oh_b[h][:, 1:N + 1, :], hot))
                    dve.sem_inc(d_oh, 1)

                def factors(h):
                    b0, b1 = PARTS[h]
                    n, hs = b1 - b0, slice(b0, b1)
                    dve.wait_ge(g_r2, l * 2 + h + 1)
                    dve.tensor_tensor(gate[:, 0, 0:n], top[:, hs, 1], top[:, hs, 0], ALU.subtract)
                    dve.tensor_copy(x_sb[:, hs, D], r2[:, 0:n])
                    step(dve.tensor_scalar(x_sb[:, hs, D + 1], r2[:, 0:n], 0.5, None, ALU.mult))
                    step(dve.tensor_tensor(x_sb[:, hs, D + 2], r2[:, 0:n], x_sb[:, hs, D + 1], ALU.mult))
                    dve.tensor_tensor(gate[:, 0, 0:n], gate[:, 0, 0:n], r2[:, 0:n], ALU.mult).then_inc(d_gate, 1)

                def running(out, values):
                    step(dve.tensor_tensor(tri[:, :, :], bc(values, 1, [S, E, E]),
                                           cst[0:S, C_TRI:C_END].rearrange("p (a e) -> p a e", e=E), ALU.mult))
                    step(dve.tensor_reduce(out, tri[:, :, :], AX_X, ALU.add))

                def spread(row, N):
                    return bc(row, 1, [S, N, E])

                def copy_ranks(h):
                    N = (PARTS[h][1] - PARTS[h][0]) * TOPK
                    dve.wait_ge(p_rt, l * 2 + h + 1)
                    step(dve.tensor_copy(rank_all[:, 0:(N + 1) * E], ps[0:S, 7, 128:128 + (N + 1) * E]))
                    dve.sem_inc(d_rt, 1)

                def tiles_of_first():
                    N = PARTS[0][1] * TOPK
                    total = rank_all[:, N * E:(N + 1) * E]
                    step(dve.tensor_tensor(cnt[:, :, :], bc(total, 2, [S, E, MA]), bc(cst[0:S, C_M:C_M + MA], 1, [S, E, MA]), ALU.is_ge))
                    step(dve.tensor_reduce(whole[:, :], cnt[:, :, :], AX_X, ALU.add))
                    running(ends[:, 0, :], whole[:, :])
                    fit = tef[:, 0:WHOLE, 0:E]
                    step(dve.tensor_tensor(fit, bc(ends[0:1, 0, :], 1, [1, WHOLE, E]),
                                           bc(cst[0:1, C_T:C_T + WHOLE], 2, [1, WHOLE, E]), ALU.is_le))
                    step(dve.tensor_reduce(tes[:, 0:WHOLE], fit, AX_X, ALU.add))
                    dve.tensor_copy(tile_e[:, 0:WHOLE], tes[:, 0:WHOLE]).then_inc(d_te, 1)
                    step(dve.tensor_scalar(whole[:, :], whole[:, :], float(SLOT), None, ALU.mult))
                    step(dve.tensor_tensor(over[:, :], total, whole[:, :], ALU.subtract))
                    step(dve.scalar_tensor_tensor(out=first[:, :], in0=ends[:, 0, :], scalar=float(SLOT), in1=whole[:, :],
                                                  op0=ALU.mult, op1=ALU.subtract))
                    step(dve.tensor_tensor(jump[:, :], cst[0:S, C_G:C_G + E], whole[:, :], ALU.subtract))
                    step(dve.tensor_tensor(jump[:, :], jump[:, :], first[:, :], ALU.subtract))

                def place_first(part):
                    N = PARTS[0][1] * TOPK
                    rank = rank_all[:, 0:N * E].rearrange("p (a e) -> p a e", e=E)
                    mask = mask_all[:, 0:N * E].rearrange("p (a e) -> p a e", e=E)
                    far = jump_all[:, 0:N * E].rearrange("p (a e) -> p a e", e=E)
                    if part == 1:
                        step(dve.tensor_tensor(rank, rank, spread(jump[:, :], N), ALU.add))
                        step(dve.tensor_tensor(rank, rank, far, ALU.add))
                        places(0, rank)
                        return
                    step(dve.tensor_tensor(mask, rank, spread(whole[:, :], N), ALU.is_lt))
                    step(dve.tensor_tensor(rank, rank, spread(first[:, :], N), ALU.add))
                    step(dve.tensor_scalar(far, rank, float(WHOLE * SLOT), float(E * SLOT), ALU.is_ge, ALU.mult))
                    step(dve.tensor_tensor(far, far, spread(jump[:, :], N), ALU.subtract))
                    step(dve.tensor_tensor(far, far, mask, ALU.mult))
                def tiles_of_second():
                    N = (PARTS[1][1] - PARTS[1][0]) * TOPK
                    rank = rank_all[:, 0:(N + 1) * E].rearrange("p (a e) -> p a e", e=E)
                    step(dve.tensor_tensor(rank, rank, spread(over[:, :], N + 1), ALU.add))
                    step(dve.tensor_tensor(cnt[:, :, 0:MB], bc(rank[:, N, :], 2, [S, E, MB]),
                                           bc(cst[0:S, C_M:C_M + MB], 1, [S, E, MB]), ALU.is_gt))
                    step(dve.tensor_reduce(whole[:, :], cnt[:, :, 0:MB], AX_X, ALU.add))
                    running(ends[:, 1, :], whole[:, :])
                    step(dve.tensor_scalar(ends[:, 1, :], ends[:, 1, :], ends[:, 0, E - 1:E], None, ALU.add))
                    step(dve.tensor_tensor(jump[:, :], ends[:, 1, :], whole[:, :], ALU.subtract))
                    step(dve.scalar_tensor_tensor(out=jump[:, :], in0=jump[:, :], scalar=float(SLOT), in1=cst[0:S, C_G:C_G + E],
                                                  op0=ALU.mult, op1=ALU.subtract))
                    step(dve.tensor_scalar(jump[:, :], jump[:, :], float((E - 1) * SLOT), None, ALU.add))

                def place_second():
                    N = (PARTS[1][1] - PARTS[1][0]) * TOPK
                    rank = rank_all[:, 0:N * E].rearrange("p (a e) -> p a e", e=E)
                    far = jump_all[:, 0:N * E].rearrange("p (a e) -> p a e", e=E)
                    step(dve.tensor_scalar(far, rank, float(SLOT), None, ALU.is_ge))
                    step(dve.tensor_tensor(far, far, spread(jump[:, :], N), ALU.mult))
                    step(dve.tensor_tensor(rank, rank, far, ALU.add))
                    step(dve.tensor_tensor(rank, rank, spread(cst[0:S, C_G:C_G + E], N), ALU.add))
                    places(1, rank)

                def experts_of_later():
                    T = NK - WHOLE
                    step(dve.tensor_tensor(tef[:, :, :], bc(ends[0:1, :, :].rearrange("p a e -> p (a e)"), 1, [1, T, 2 * E]),
                                           bc(cst[0:1, C_T + WHOLE:C_T + NK], 2, [1, T, 2 * E]), ALU.is_le))
                    step(dve.tensor_reduce(tes[:, :], tef[:, :, :], AX_X, ALU.add))
                    step(dve.tensor_scalar(tew[:, :], tes[:, :], float(E), float(E), ALU.is_ge, ALU.mult))
                    step(dve.tensor_tensor(tes[:, :], tes[:, :], tew[:, :], ALU.subtract))
                    dve.tensor_scalar(tile_e[:, WHOLE + E:NT], tes[:, :], float(E - 1), None, ALU.min).then_inc(d_te, 1)

                def places(h, rank):
                    b0, b1 = PARTS[h]
                    N = (b1 - b0) * TOPK
                    hot = hot_all[:, 0:N * E].rearrange("p (a e) -> p a e", e=E)
                    y, x = (t[:, b0:b1, :].rearrange("p b k -> p (b k)") for t in (pos, pos_x))
                    step(dve.tensor_tensor(rank, rank, hot, ALU.mult))
                    step(dve.tensor_reduce(posf[:, 0:N], rank, AX_X, ALU.add))
                    step(dve.tensor_copy(y, posf[:, 0:N]))
                    step(dve.tensor_scalar(posn[:, 0:N], y, SLOT - 1, None, ALU.bitwise_and))
                    step(dve.tensor_scalar(posn[:, 0:N], posn[:, 0:N], 2.0, float((NT - 1) * SLOT), ALU.mult, ALU.add))
                    dve.tensor_tensor(x, posn[:, 0:N], y, ALU.subtract).then_inc(d_pos, 1)

                def gates(h):
                    b0, b1 = PARTS[h]
                    n, hs = b1 - b0, slice(b0, b1)
                    dve.wait_ge(a_rt, l * 2 + h + 1)
                    step(dve.tensor_scalar(gate[:, 0, 0:n], gate[:, 1, 0:n], 1.0, None, ALU.add))
                    step(dve.reciprocal(wts[:, hs, 0], gate[:, 0, 0:n]))
                    step(dve.tensor_tensor(wts[:, hs, 1], wts[:, hs, 0], gate[:, 1, 0:n], ALU.mult))

                for u in range(2):
                    dve.wait_ge(st_ye[u], l * (8 * NT) + 16)
                rotate(0)
                for p in range(2):
                    maxima(0, p)
                for p in range(2):
                    scale_probs(0, p)
                for g in range(NG):
                    for bb in range(GB):
                        b = g * 4 + bb
                        if bb == 3 and g < NG - 1:
                            rotate(g + 1, range(0, 4))
                            copy_probs(b)
                            rotate(g + 1, range(4, 7))
                            copy_outputs(b)
                            rotate(g + 1, range(7, 10))
                        if b < B - 1:
                            maxima(b + 1, 0)
                        if b == RANK_STEP + 1:
                            copy_ranks(0)
                        if b < B - 1:
                            maxima(b + 1, 1)
                        if bb < 3 or b == B - 1:
                            copy_probs(b)
                        if g < NG - 1 and bb < 2:
                            rows_in(step, l, 4 * g + 4 + 2 * bb)
                        if b == RANK_STEP:
                            choose(0)
                        if b == RANK_STEP + 1:
                            tiles_of_first()
                        if b == RANK_STEP + 2:
                            place_first(1)
                        if bb < 3 or b == B - 1:
                            copy_outputs(b)
                        if b < B - 1:
                            scale_probs(b + 1, 0)
                        add_attention(b)
                        if g < NG - 1 and bb < 2:
                            rows_in(step, l, 4 * g + 4 + 2 * bb + 1)
                        if b < B - 1:
                            scale_probs(b + 1, 1)
                        if b:
                            logits(b - 1)
                        if b == RANK_STEP:
                            factors(0)
                        if b == RANK_STEP + 1:
                            place_first(0)
                        if b == RANK_STEP + 2:
                            gates(0)

                def copy_factors(T, u):
                    dve.wait_ge(m_tx, l * NT + T + 1)
                    dve.tensor_copy(er[:, u, :], xe[u][:, D + 1:D + 3]).then_inc(m_r, 1)

                def hidden(T, u, base):
                    step = Steps(dve, dm, base)
                    dve.wait_ge(m_tanh, l * NT + T + 1)
                    step(dve.scalar_tensor_tensor(out=th, in0=th, scalar=1.0, in1=ps[:, 2 * u, :], op0=ALU.add, op1=ALU.mult))
                    dve.wait_ge(m_u, l * NT + T + 1)
                    dve.scalar_tensor_tensor(out=hid[u], in0=th, scalar=er[:, u, 1:2], in1=ps[:, 2 * u + 1, :],
                                             op0=ALU.mult, op1=ALU.mult).then_inc(m_h, 1)

                def copy_result(T, u, n):
                    dve.wait_ge(m_dn, l * NT + T + 1)
                    dve.wait_ge(st_ye[u], l * (8 * NT) + n * 16)
                    dve.tensor_copy(ye[u], ps[:, 6 + u, 0:D]).then_inc(m_y, 1)

                mbase = l * NT

                def tile(i, u, first=False, end=False):
                    T = i * 2 + u
                    hidden(T, u, mbase + T)
                    if first and u == 0:
                        logits(B - 1)
                    if not (end and u == 1):
                        copy_factors(T + 1, 1 - u)
                    if not (first and u == 0):
                        copy_result(T - 1, 1 - u, i + u)

                def pair(i, end=False):
                    tile(i, 0)
                    tile(i, 1, end=end)

                copy_factors(0, 0)
                tile(0, 0, first=True)
                tile(0, 1)
                factors(1)
                tile(1, 0)
                choose(1)
                tile(1, 1)
                copy_ranks(1)
                tiles_of_second()
                tile(2, 0)
                place_second()
                tile(2, 1)
                experts_of_later()
                gates(1)
                alone(dve)
                with dve.Fori(3, TAIL) as i:
                    pair(i)
                for i in range(TAIL, NT // 2):
                    pair(i, end=(i == NT // 2 - 1))
                    for b in AHEAD[i - TAIL]:
                        rows_in(step, l + 1, b)
                copy_result(NT - 1, 1, NT // 2)
                assert step.n == DVE_LAYER, step.n

            dve.wait_ge(z_ready, 6)
            dve.wait_ge(x_ready, B - 2)
            step = Steps(dve, dv, 0)
            for b in range(GB):
                rows_in(step, 0, b)
                if b == 1:
                    finish_x(B - 2, 0, base)
                    finish_x(B - 1, 1, base + 4)
            dve.wait_ge(x_ready, B)
            dve.tensor_copy(tile_e[:, WHOLE:WHOLE + E], cst[0:1, C_E:C_E + E])
            with dve.Fori(0, L) as l:
                layer(l)

            step = Steps(dve, dv, 2 * GB + L * DVE_LAYER)
            dve.wait_ge(ld_res, 16)
            for b in range(B):
                if b < GB:
                    dve.wait_ge(d_x, L * B + b + 1)
                else:
                    combine(step, L, b)
                    step(dve.tensor_scalar(x_sb[:, b, 0:D], x_sb[:, b, 0:D], CLIP, -CLIP, ALU.min, ALU.max))
                dve.tensor_tensor(x_sb[:, b, 0:D], x_sb[:, b, 0:D], res[:, b, :], ALU.add).then_inc(d_out, 1)


VALUES = [b % 4 if b % 4 < 3 else 3 + b // 4 % 2 for b in range(B)]

RANK_STEP = PARTS[0][1] + 1
TAIL = FIRST // 2 + 1
AHEAD = [[0], [1], [2], [3], []]
assert TAIL + len(AHEAD) == NT // 2 and B - GB - 1 <= RANK_STEP

_INS = ["x", "ctx_1024", "L0_xattn_w_sim", "L0_xattn_b_sim", "L0_xattn_W_qv", "L0_xattn_b_qv", "L0_ffn_ln1_w",
        "L0_ffn_ln2_w", "L0_ffn_wq", "L0_ffn_wk", "L0_ffn_wv", "L0_ffn_wo", "L0_ffn_wr", "L0_ffn_wg", "L0_ffn_wu",
        "L0_ffn_wd"]


def kernel(**inputs):
    import numpy as _np
    import concourse.bacc as _bacc
    from concourse import mybir as _mybir
    from concourse.bass_utils import run_bass_kernel_spmd as _run

    nc = _bacc.Bacc("TRN2", target_bir_lowering=False, num_devices=1)
    arrays, args = {}, []
    given = {name: _np.ascontiguousarray(inputs[name]) for name in _INS}
    given["constants"] = constants()
    for name, a in given.items():
        arrays[f"in_{name}_dram"] = a
        args.append(nc.dram_tensor(f"in_{name}_dram", a.shape, _mybir.dt.from_np(a.dtype), kind="ExternalInput").ap())
    args.append(nc.dram_tensor("out_0_dram", (B, S, D), _mybir.dt.float32, kind="ExternalOutput").ap())
    xattn_ffn(nc, *args)
    r = _run(nc, [arrays], core_ids=[0])
    return r.results[0]["out_0_dram"]
```
